# Optimizing a Trainium2 kernel written in Bass

```python
import numpy as np
import jax
import jax.numpy as jnp

def _softmax(x, axis=-1):
    return jax.nn.softmax(x, axis=axis)

def _gelu(x):
    return jax.nn.gelu(x, approximate=True)

def _silu(x):
    return jax.nn.silu(x)

def _sigmoid(x):
    return jax.nn.sigmoid(x)

def _layernorm(x, axis=-1, eps=1e-05):
    m = jnp.mean(x, axis=axis, keepdims=True)
    v = jnp.var(x, axis=axis, keepdims=True)
    return (x - m) / jnp.sqrt(v + eps)

def _scatter_add(tgt, idx, src, axis=0):
    return tgt.at[idx].add(src)

def _segment_sum(src, seg, n):
    return jax.ops.segment_sum(src, seg, n)
kernel_name = 'mk_gnn_resnorm_d2_gnn_r64_1c672e'

def setup_inputs(seed: int=0):
    np.random.seed(seed)
    _w = jnp.asarray

    def _rec_inputs():
        import jax
        import jax.numpy as jnp
        _gk = jax.random.key(seed)
        x = -0.000202 + 1 * jax.random.normal(jax.random.fold_in(_gk, 1), (50000, 128), jnp.float32)
        src = jax.random.randint(jax.random.fold_in(_gk, 2), (12500,), 0, 50000, jnp.int32)
        dst = jnp.minimum((50000 * jax.random.uniform(jax.random.fold_in(_gk, 3), (12500,)) ** 2.0).astype(jnp.int32), 49999)
        _o = jnp.argsort(dst, stable=True)
        src = src[_o]
        dst = dst[_o]
        return (x, src, dst)
    x, src, dst = _rec_inputs()

    def _L0_gnn_setup():
        import jax, jax.numpy as jnp
        import numpy as np
        NHID = 256

        def gcn_conv(x, W, b, src, dst, n_nodes):
            h = x @ W
            deg = jax.ops.segment_sum(jnp.ones_like(dst, dtype=h.dtype), dst, num_segments=n_nodes)
            dinv = jnp.where(deg > 0, jax.lax.rsqrt(jnp.maximum(deg, 1.0)), 0.0)
            norm = dinv[src] * dinv[dst]
            msg = h[src] * norm[:, None]
            out = jax.ops.segment_sum(msg, dst, num_segments=n_nodes)
            return out + b
        key = jax.random.key(seed)
        k1, k2, k3, k4, k5 = jax.random.split(key, 5)
        N, E, F = (50000, 12500, 128)
        x = jax.random.normal(k1, (N, F), dtype=jnp.float32)
        edge_index = jax.random.randint(k2, (2, E), 0, N, dtype=jnp.int64)
        W1 = jax.random.normal(k3, (F, NHID), dtype=jnp.float32) / np.sqrt(F)
        b1 = jnp.zeros((NHID,), dtype=jnp.float32)
        W2 = jax.random.normal(k4, (NHID, F), dtype=jnp.float32) / np.sqrt(NHID)
        b2 = jnp.zeros((F,), dtype=jnp.float32)
        return {'x': x, 'edge_index': edge_index, 'W1': W1, 'b1': b1, 'W2': W2, 'b2': b2}
    _L0_gnn_all = _L0_gnn_setup()
    _L0_gnn_in = {k: v for k, v in _L0_gnn_all.items() if k in ('W1', 'b1', 'W2', 'b2')}
    del _L0_gnn_all

    def _L1_gnn_setup():
        import jax, jax.numpy as jnp
        import numpy as np
        NUM_LAYERS = 4
        HIDDEN = 128
        N_NODES = 50000
        N_EDGES = 12500

        def _gru_cell(inp, h, w_ih, w_hh, b_ih, b_hh):
            gi = inp @ w_ih.T + b_ih
            gh = h @ w_hh.T + b_hh
            i_r, i_z, i_n = jnp.split(gi, 3, axis=-1)
            h_r, h_z, h_n = jnp.split(gh, 3, axis=-1)
            r = jax.nn.sigmoid(i_r + h_r)
            z = jax.nn.sigmoid(i_z + h_z)
            n = jnp.tanh(i_n + r * h_n)
            return (1.0 - z) * n + z * h
        key = jax.random.key(seed)
        ks = jax.random.split(key, 8)
        s = 1.0 / np.sqrt(HIDDEN)
        node_embed = jax.random.normal(ks[0], (N_NODES, HIDDEN), dtype=jnp.float32)
        edge_index = jax.random.randint(ks[1], (2, N_EDGES), 0, N_NODES, dtype=jnp.int64)
        weight = jax.random.normal(ks[2], (NUM_LAYERS, HIDDEN, HIDDEN), dtype=jnp.float32) * s
        w_ih = jax.random.normal(ks[3], (3 * HIDDEN, HIDDEN), dtype=jnp.float32) * s
        w_hh = jax.random.normal(ks[4], (3 * HIDDEN, HIDDEN), dtype=jnp.float32) * s
        b_ih = jax.random.normal(ks[5], (3 * HIDDEN,), dtype=jnp.float32) * s
        b_hh = jax.random.normal(ks[6], (3 * HIDDEN,), dtype=jnp.float32) * s
        return {'node_embed': node_embed, 'edge_index': edge_index, 'weight': weight, 'w_ih': w_ih, 'w_hh': w_hh, 'b_ih': b_ih, 'b_hh': b_hh}
    _L1_gnn_all = _L1_gnn_setup()
    _L1_gnn_in = {k: v for k, v in _L1_gnn_all.items() if k in ('weight', 'w_ih', 'w_hh', 'b_ih', 'b_hh')}
    del _L1_gnn_all
    return {'x': x, 'src': src, 'dst': dst, 'L0_gnn_W1': _L0_gnn_in['W1'], 'L0_gnn_b1': _L0_gnn_in['b1'], 'L0_gnn_W2': _L0_gnn_in['W2'], 'L0_gnn_b2': _L0_gnn_in['b2'], 'L1_gnn_weight': _L1_gnn_in['weight'], 'L1_gnn_w_ih': _L1_gnn_in['w_ih'], 'L1_gnn_w_hh': _L1_gnn_in['w_hh'], 'L1_gnn_b_ih': _L1_gnn_in['b_ih'], 'L1_gnn_b_hh': _L1_gnn_in['b_hh']}

def reference(x, src, dst, L0_gnn_W1, L0_gnn_b1, L0_gnn_W2, L0_gnn_b2, L1_gnn_weight, L1_gnn_w_ih, L1_gnn_w_hh, L1_gnn_b_ih, L1_gnn_b_hh):
    import jax
    import jax.numpy as jnp

    def _L0_gnn_ref(x, edge_index, W1, b1, W2, b2):
        import jax, jax.numpy as jnp
        import numpy as np
        NHID = 256

        def gcn_conv(x, W, b, src, dst, n_nodes):
            h = x @ W
            deg = jax.ops.segment_sum(jnp.ones_like(dst, dtype=h.dtype), dst, num_segments=n_nodes)
            dinv = jnp.where(deg > 0, jax.lax.rsqrt(jnp.maximum(deg, 1.0)), 0.0)
            norm = dinv[src] * dinv[dst]
            msg = h[src] * norm[:, None]
            out = jax.ops.segment_sum(msg, dst, num_segments=n_nodes)
            return out + b
        n_nodes = x.shape[0]
        loops = jnp.arange(n_nodes, dtype=edge_index.dtype)
        src = jnp.concatenate([edge_index[0], loops])
        dst = jnp.concatenate([edge_index[1], loops])
        h = gcn_conv(x, W1, b1, src, dst, n_nodes)
        h = gcn_conv(h, W2, b2, src, dst, n_nodes)
        return jax.nn.sigmoid(h)

    def _L1_gnn_ref(node_embed, edge_index, weight, w_ih, w_hh, b_ih, b_hh):
        import jax, jax.numpy as jnp
        import numpy as np
        NUM_LAYERS = 4
        HIDDEN = 128
        N_NODES = 50000
        N_EDGES = 12500

        def _gru_cell(inp, h, w_ih, w_hh, b_ih, b_hh):
            gi = inp @ w_ih.T + b_ih
            gh = h @ w_hh.T + b_hh
            i_r, i_z, i_n = jnp.split(gi, 3, axis=-1)
            h_r, h_z, h_n = jnp.split(gh, 3, axis=-1)
            r = jax.nn.sigmoid(i_r + h_r)
            z = jax.nn.sigmoid(i_z + h_z)
            n = jnp.tanh(i_n + r * h_n)
            return (1.0 - z) * n + z * h
        src = edge_index[0]
        dst = edge_index[1]
        n_nodes = node_embed.shape[0]
        x = node_embed
        for l in range(NUM_LAYERS):
            m = x @ weight[l]
            agg = jax.ops.segment_sum(m[src], dst, num_segments=n_nodes)
            x = _gru_cell(agg, x, w_ih, w_hh, b_ih, b_hh)
        return x + node_embed
    edge_index = jnp.stack([src, dst])
    x = _layernorm(x + _L0_gnn_ref(x, edge_index, L0_gnn_W1, L0_gnn_b1, L0_gnn_W2, L0_gnn_b2), axis=-1)
    x = _layernorm(x + _L1_gnn_ref(x, edge_index, L1_gnn_weight, L1_gnn_w_ih, L1_gnn_w_hh, L1_gnn_b_ih, L1_gnn_b_hh), axis=-1)
    return x

_drawn_inputs = setup_inputs


def setup_inputs(seed=0):
    import zlib

    import numpy as np

    out = dict(_drawn_inputs(seed))
    spreads = {'L0_gnn_b1': (0.0, 0.344), 'L0_gnn_b2': (0.0, 0.398)}
    factors = {}
    for name, (base, spread) in spreads.items():
        noise = np.random.default_rng([zlib.crc32(name.encode()), seed]).standard_normal(out[name].shape)
        drawn = base * np.exp(spread * noise) if base else spread * noise
        out[name] = jnp.asarray(drawn.astype(out[name].dtype))
    for name, factor in factors.items():
        out[name] = (out[name] * factor).astype(out[name].dtype)
    return out
```

```python
import concourse.bass as bass
from concourse import mybir
from contextlib import ExitStack


def gcn_resnorm_ggnn_resnorm(
    nc: bass.Bass,
    x: bass.AP, src: bass.AP, dst: bass.AP,
    W1: bass.AP, b1: bass.AP, W2: bass.AP, b2: bass.AP,
    gw: bass.AP, w_ih: bass.AP, w_hh: bass.AP, b_ih: bass.AP, b_hh: bass.AP,
    out: bass.AP,
):
    f32 = mybir.dt.float32
    bf16 = mybir.dt.bfloat16
    i32 = mybir.dt.int32
    ALU = mybir.AluOpType
    ACT = mybir.ActivationFunctionType

    N, F = x.shape
    E = src.shape[0]
    HID = W1.shape[1]
    LEVELS = gw.shape[0]
    P = 128
    J = 4
    GS = J * P
    NG = -(-E // GS)
    NT = NG * J
    NS = NT * P
    FULL = E // P
    REST = E - FULL * P
    DP = 125
    DW = DP * J
    ND = N // DW
    EPS = 1e-5
    PAIRS = (NG - 1) // 2
    LEAD = ND - 2 * NG - (LEVELS - 1) * (PAIRS + 1)
    assert N == ND * DW and NG % 2 == 1 and LEAD >= 2

    x_g = x.rearrange("(g p j) f -> g p (j f)", p=DP, j=J)
    out_g = out.rearrange("(g p j) f -> g p (j f)", p=DP, j=J)

    ctx = ExitStack()
    with ctx:
        def sb(name, shape, dt=f32):
            return ctx.enter_context(nc.sbuf_tensor(name, shape, dt))

        def sem(name):
            return ctx.enter_context(nc.semaphore(name))

        def dram(name, shape, dt=f32):
            return nc.dram_tensor(name, shape, dt)

        tz = dram("tz", [2 * NS, F])
        tx = [dram(f"tx{l}", [2 * NS, F]) for l in range(LEVELS)]
        rec = dram("rec", [N, 2])
        first_d = dram("first_d", [NT, P])
        xd_d = dram("xd_d", [NS, F])
        hT_d = dram("hT_d", [NG, P, GS])

        def rows(t, side):
            return t[side * NS:(side + 1) * NS, :].rearrange("(g j p) f -> g p j f", j=J, p=P)

        ident = sb("ident", [P, P])
        tri = sb("tri", [P, P])
        one = sb("one", [1, 1])
        mhalf = sb("mhalf", [P, P])
        W12 = sb("W12", [P, P])
        c_bc = sb("c_bc", [P, P])
        b2_bc = sb("b2_bc", [P, P])
        cb2_bc = sb("cb2_bc", [P, P])
        whT = sb("whT", [P, 3 * P])
        wiT = sb("wiT", [P, 3 * P])
        wlT = sb("wlT", [P, LEVELS, 3 * P])
        b3 = sb("b3", [P, 2, 3])
        brz = sb("brz", [P, 2])
        W1s = sb("W1s", [P, HID])
        W2s = sb("W2s", [P, 2, P])
        W1T = sb("W1T", [P, 2, P])
        b1c = sb("b1c", [P, 2])
        b1f = sb("b1f", [P, 2, P])
        wih_s = sb("wih_s", [P, 3, P])
        whh_s = sb("whh_s", [P, 3, P])
        gw_s = sb("gw_s", [P, LEVELS, P])
        gwT = sb("gwT", [P, LEVELS, P])

        dstR = sb("dstR", [NT, P], i32)
        prevR = sb("prevR", [NT, P], i32)
        nextR = sb("nextR", [NT, P], i32)
        srcR = sb("srcR", [NT, P], i32)
        eR = sb("eR", [NT, P], i32)
        dstF = sb("dstF", [NT, P])
        prevF = sb("prevF", [NT, P])
        nextF = sb("nextF", [NT, P])
        srcF = sb("srcF", [NT, P])
        eF = sb("eF", [NT, P])
        startF = sb("startF", [NT, P])
        runF = sb("runF", [NT, P])
        carF = sb("carF", [1, NT + 1])
        firstF = sb("firstF", [NT, P])
        dinvF = sb("dinvF", [NT, P])
        scatF = sb("scatF", [NT, P])
        ecI = sb("ecI", [P, NT], i32)
        ecol = sb("ecol", [P, NT])
        t0I = sb("t0I", [P, NT], i32)
        t0col = sb("t0col", [P, NT])
        srcI = sb("srcI", [P, NT], i32)
        dstI = sb("dstI", [P, NT], i32)
        scatI = sb("scatI", [P, NT], i32)
        dstC = sb("dstC", [P, NT])
        dinvD = sb("dinvD", [P, NT])
        recrow = sb("recrow", [P, NT, 2])
        recS = sb("recS", [P, NT, 2])
        isd = sb("isd", [P, NT])
        mv = sb("mv", [P, NT])
        idxF = sb("idxF", [P, NT])
        idxI = sb("idxI", [P, NT], i32)
        recfill = sb("recfill", [DP, N // DP, 2])
        S = sb("S", [P, NS])
        FL = sb("FL", [P, NS], bf16)

        W = [GS, DW]
        rS = [sb(f"rS{i}", [P, W[i]]) for i in range(2)]
        zS = [sb(f"zS{i}", [P, W[i]]) for i in range(2)]
        tS = [sb(f"tS{i}", [P, W[i]]) for i in range(2)]
        nS = [sb(f"nS{i}", [P, W[i]]) for i in range(2)]
        dS = [sb(f"dS{i}", [P, W[i]]) for i in range(2)]
        hA = sb("hA", [P, GS])
        hB = sb("hB", [P, GS])
        h1 = sb("h1", [P, DW])
        x1T = sb("x1T", [P, DW])
        uT = sb("uT", [P, DW])
        xr1 = sb("xr1", [DP, J, P])
        xT1 = sb("xT1", [P, DW])
        z1 = sb("z1", [DP, J, P])
        xn1 = sb("xn1", [DP, J, P])
        o1 = sb("o1", [DP, J, P])
        xs = sb("xs", [P, J, P])
        xd = sb("xd", [P, J, P])
        xsT = sb("xsT", [P, GS])
        msg = sb("msg", [P, J, P])
        xdd = sb("xdd", [P, J, P])
        aggS = sb("aggS", [P, GS])
        zrow = sb("zrow", [P, J, P])
        zD = sb("zD", [P, J, P])
        z0 = sb("z0", [P, J, P])
        xn0 = sb("xn0", [P, J, P])
        stg = sb("stg", [P, J, P])
        idxa = sb("idxa", [P, J], i32)
        idxb = sb("idxb", [P, J], i32)
        zDr = sb("zDr", [P, J, P])
        xdr = sb("xdr", [P, J, P])

        def lnbuf(tag, p):
            return {"st": sb("st" + tag, [p, J, 6]), "ag": sb("ag" + tag, [p, J, 2]),
                    "rs": sb("rs" + tag, [p, J]), "nm": sb("nm" + tag, [p, J])}

        lnb = {"pre1": lnbuf("pre1", DP), "fin1": lnbuf("fin1", DP), "lane0": lnbuf("lane0", P)}

        def bank(name):
            return ctx.enter_context(nc.psum_tensor(name, [P, 512], f32))

        pR = [bank("pR0"), bank("pR1")]
        pN = [bank("pN0"), bank("pN1")]
        pZ = [bank("pZ0"), bank("pZ1")]
        pM = [bank("pM0"), bank("pM1")]

        s_const = sem("s_const")
        s_wload = sem("s_wload")
        s_pads = sem("s_pads")
        s_eload = sem("s_eload")
        s_prep_pe = sem("s_prep_pe")
        s_prep_cp = sem("s_prep_cp")
        s_wready = sem("s_wready")
        s_chain = sem("s_chain")
        s_col_pe = sem("s_col_pe")
        s_car_pe = sem("s_car_pe")
        s_deg = sem("s_deg")
        s_first = sem("s_first")
        s_firstst = sem("s_firstst")
        s_firstld = sem("s_firstld")
        s_S = sem("s_S")
        s_cols = sem("s_cols")
        s_recinit = sem("s_recinit")
        s_recg = sem("s_recg")
        s_idx = sem("s_idx")

        names = ["r_filled", "n_filled", "z_filled", "r_ready", "z_ready", "t_ready", "tanh_ready",
                 "diff_ready", "gated_ready", "h_ready", "m_filled"]
        L = [{n: sem(f"{n}{i}") for n in names} for i in range(2)]
        lns = {t: [sem(f"ln_{w}_{t}") for w in ("stats", "aggr", "rstd", "nmr", "out")] for t in lnb}
        s_x1load = sem("s_x1load")
        s_xT1 = sem("s_xT1")
        s_z1 = sem("s_z1")
        s_sig1 = sem("s_sig1")
        s_u1 = sem("s_u1")
        s_x1T = sem("s_x1T")
        s_uT = sem("s_uT")
        s_store1 = sem("s_store1")
        s_idxc = sem("s_idxc")
        s_gs = sem("s_gs")
        s_gd = sem("s_gd")
        s_scaled = sem("s_scaled")
        s_carry = sem("s_carry")
        s_carried = sem("s_carried")
        s_xsT = sem("s_xsT")
        s_self = sem("s_self")
        s_zs = sem("s_zs")
        s_zd = sem("s_zd")
        s_zpre = sem("s_zpre")
        s_zb = sem("s_zb")
        s_sig0 = sem("s_sig0")
        s_u0 = sem("s_u0")
        s_h0 = sem("s_h0")
        s_stg = sem("s_stg")
        st_zs = sem("st_zs")
        st_zd = sem("st_zd")
        st_xd = sem("st_xd")
        st_xn = sem("st_xn")
        st_stg = sem("st_stg")
        st_h = sem("st_h")
        s_ldz = sem("s_ldz")
        s_ldx = sem("s_ldx")
        s_ldh = sem("s_ldh")
        s_in = sem("s_in")
        s_fin = sem("s_fin")
        s_fout = sem("s_fout")
        s_scat = sem("s_scat")

        SU, GU, LU = 9, 3, 3
        M_G = SU * NG
        M_L = M_G + GU * NG
        GRU_L = 3 * NG
        LN_G = NG
        LN_L = 2 * NG

        from_one = [s_zpre, s_fin, s_u0, s_scaled, s_stg, s_store1, s_carried, s_carry,
                    st_xd, st_xn, st_stg, st_h, st_zs, st_zd]
        from_one += [L[i][n] for i in range(2) for n in names if n.endswith("_ready") or n == "m_filled"
                     if n not in ("tanh_ready", "diff_ready")]
        from_one += [lns[t][4] for t in lnb]

        turns = {"sp": sem("s_turn_sp"), "pool": sem("s_turn_pool"), "dve": sem("s_turn_dve")}

        def settle(eng, name):
            eng.sem_inc(turns[name], 1)

        block = ctx.enter_context(nc.Block())

        D_S = LEAD
        D_G = D_S + NG
        D_L = D_G + NG

        def schedule(eng, p):
            def dense(d, k, first=False, last=False):
                p.gru1(d, k)
                if k == 0 and not first:
                    p.fin(d - 1)
                if not last:
                    if k == 0:
                        p.load(d + 1)
                    if k == 1:
                        p.xt(d + 1)
                    if k == 2:
                        p.z(d + 1)
                if k == 3:
                    p.u(d)
                    if not last:
                        p.x1(d + 1)

            p.prep_weights()
            p.load1(0)
            p.xt(0)
            p.z(0)
            p.x1(0)
            for k in range(4):
                dense(0, k, first=True)
            p.prep_edges()
            with eng.Fori(1, LEAD) as d:
                for k in range(4):
                    dense(d, k)
            p.prep_edges2()
            with eng.Fori(0, NG) as i:
                d = i + D_S
                p.s_load(i)
                dense(d, 0)
                p.s0(i)
                dense(d, 1)
                p.s1(i)
                p.s_gru(i, 0)
                dense(d, 2)
                p.s_gru(i, 1)
                dense(d, 3)
                p.s_gru(i, 2)
            with eng.Fori(0, NG) as i:
                d = i + D_G
                p.g_load(i)
                dense(d, 0)
                p.g0(i)
                dense(d, 1)
                p.g1(i)
                dense(d, 2)
                p.g2(i)
                dense(d, 3)
            for l in range(LEVELS):
                if l < LEVELS - 1:
                    dl = D_L + l * (PAIRS + 1)
                    with eng.Fori(0, PAIRS) as i:
                        d = i + dl
                        dense(d, 0)
                        p.la(l, 2 * i)
                        dense(d, 1)
                        p.lb(l, 2 * i)
                        dense(d, 2)
                        p.lc(l, 2 * i)
                        p.la(l, 2 * i + 1)
                        dense(d, 3)
                        p.lb(l, 2 * i + 1)
                        p.lc(l, 2 * i + 1)
                    d = dl + PAIRS
                    last = d == ND - 1
                    dense(d, 0, last=last)
                    p.la(l, NG - 1)
                    dense(d, 1, last=last)
                    p.lb(l, NG - 1)
                    dense(d, 2, last=last)
                    p.lc(l, NG - 1)
                    dense(d, 3, last=last)
                    if last:
                        p.fin(d)
                else:
                    with eng.Fori(0, NG) as g:
                        p.la(l, g)
                        p.lb(l, g)
                        p.lc(l, g)

        def m1_use(what, d):
            if what == "fin":
                return 4 * d + 6 if not (isinstance(d, int) and d == ND - 1) else 4 * d + 3
            return 4 * d + {"xt": -1, "z": 0, "x1": 1}[what]

        class Pieces:
            def nothing(self, *a):
                pass
            prep_weights = prep_edges = prep_edges2 = load1 = load = xt = z = x1 = gru1 = fin = u = nothing
            s_load = s0 = s1 = s_gru = g_load = g0 = g1 = g2 = la = lb = lc = nothing

        def m1(what, d):
            if isinstance(d, int) and d == 0 and what != "fin":
                return {"xt": 0, "z": 1, "x1": 2}[what]
            return m1_use(what, d)

        @block.sync
        def _(sp):
            class Sync(Pieces):
                def prep_weights(self):
                    for s in from_one:
                        sp.sem_inc(s, 1)
                    sp.dma_start(W1s[:, :], W1[:, :]).then_inc(s_wload, 16)
                    sp.dma_start(W2s[:, :, :], W2.rearrange("(c p) f -> p c f", p=P)).then_inc(s_wload, 16)
                    sp.dma_start(wih_s[:, :, :], w_ih.rearrange("(c p) f -> p c f", p=P)).then_inc(s_wload, 16)
                    sp.dma_start(whh_s[:, :, :], w_hh.rearrange("(c p) f -> p c f", p=P)).then_inc(s_wload, 16)
                    sp.dma_start(gw_s[:, :, :], gw.rearrange("l p f -> p l f")).then_inc(s_wload, 16)
                    with nc.allow_non_contiguous_dma(reason="bias columns, once"):
                        sp.dma_start(b1c[:, :], b1.rearrange("(c p) -> p c", p=P)).then_inc(s_wload, 16)
                        sp.dma_start(b3[:, 0, :], b_ih.rearrange("(c p) -> p c", p=P)).then_inc(s_wload, 16)
                        sp.dma_start(b3[:, 1, :], b_hh.rearrange("(c p) -> p c", p=P)).then_inc(s_wload, 16)
                    sp.dma_start(b2_bc[:, :], b2.rearrange("(a f) -> a f", a=1).broadcast_to([P, P])).then_inc(s_wload, 16)

                def load1(self, d):
                    sp.dma_start(xr1[:, :, :].rearrange("p j f -> p (j f)"), x_g[d]).then_inc(s_x1load, 16)
                    sp.wait_ge(s_pads, 1)
                    for t, a in ((dstR, dst), (srcR, src)):
                        sp.dma_start(t[0:FULL, :], a[0:FULL * P].rearrange("(t p) -> t p", p=P)).then_inc(s_eload, 16)
                        sp.dma_start(t[FULL:FULL + 1, 0:REST], a[FULL * P:E].rearrange("(t p) -> t p", t=1)).then_inc(s_eload, 16)
                    sp.dma_start(nextR[0:FULL, :], dst[1:FULL * P + 1].rearrange("(t p) -> t p", p=P)).then_inc(s_eload, 16)
                    sp.dma_start(nextR[FULL:FULL + 1, 0:REST - 1], dst[FULL * P + 1:E].rearrange("(t p) -> t p", t=1)).then_inc(s_eload, 16)
                    sp.dma_start(prevR[0:1, 1:P], dst[0:P - 1].rearrange("(t p) -> t p", t=1)).then_inc(s_eload, 16)
                    sp.dma_start(prevR[1:FULL, :], dst[P - 1:FULL * P - 1].rearrange("(t p) -> t p", p=P)).then_inc(s_eload, 16)
                    sp.dma_start(prevR[FULL:FULL + 1, 0:REST + 1], dst[FULL * P - 1:E].rearrange("(t p) -> t p", t=1)).then_inc(s_eload, 16)
                    sp.dma_start(rec[:, :].rearrange("(p n) c -> p (n c)", p=DP),
                                 recfill[:, :, :].rearrange("p n c -> p (n c)")).then_inc(s_recinit, 16)

                def load(self, d):
                    sp.wait_ge(s_u1, d)
                    settle(sp, "sp")
                    sp.dma_start(xr1[:, :, :].rearrange("p j f -> p (j f)"), x_g[d]).then_inc(s_x1load, 16)

                def fin(self, d):
                    sp.wait_ge(lns["fin1"][4], 1 + d + 1)
                    settle(sp, "sp")
                    sp.dma_start(out_g[d], o1[:, :, :].rearrange("p j f -> p (j f)")).then_inc(s_store1, 16)

                def prep_edges(self):
                    sp.wait_ge(s_first, 1)
                    sp.dma_start(first_d[:, :], firstF[:, :]).then_inc(s_firstst, 16)
                    sp.wait_ge(s_firstst, 16)
                    sp.dma_start(S[:, :], first_d[:, :].rearrange("(a t) p -> a (t p)", a=1).broadcast_to([P, NS]),
                                 max_dma_last_dim=NS).then_inc(s_firstld, 16)

                def s0(self, i):
                    sp.wait_ge(s_gd, 64 * i + 64)
                    settle(sp, "sp")
                    sp.dma_start(xd_d[:, :].rearrange("(g j p) f -> g p j f", j=J, p=P)[i], xd[:, :, :]).then_inc(st_xd, 16)

                def s1(self, i):
                    sp.wait_ge(s_zs, i + 1)
                    settle(sp, "sp")
                    sp.dma_start(rows(tz, 0)[i], zrow[:, :, :]).then_inc(st_zs, 16)
                    sp.wait_ge(s_zd, i + 1)
                    settle(sp, "sp")
                    sp.dma_start(rows(tz, 1)[i], zD[:, :, :]).then_inc(st_zd, 16)
                    sp.wait_ge(lns["lane0"][4], 1 + i + 1)
                    settle(sp, "sp")
                    sp.dma_start(rows(tx[0], 0)[i], xn0[:, :, :]).then_inc(st_xn, 16)

                def s_gru(self, i, k):
                    sp.wait_ge(s_stg, 1 + 3 * i + k + 1)
                    settle(sp, "sp")
                    sp.dma_start(rows(tx[k + 1], 0)[i], stg[:, :, :]).then_inc(st_stg, 16)

                def g_load(self, i):
                    sp.wait_ge(st_zd, 1 + 16 * NG)
                    sp.wait_ge(st_xd, 1 + 16 * NG)
                    sp.wait_ge(s_zpre, 1 + i)
                    settle(sp, "sp")
                    sp.dma_start(zDr[:, :, :], rows(tz, 1)[i]).then_inc(s_ldz, 16)
                    sp.wait_ge(s_u0, 1 + i + NG)
                    settle(sp, "sp")
                    sp.dma_start(xdr[:, :, :], xd_d[:, :].rearrange("(g j p) f -> g p j f", j=J, p=P)[i]).then_inc(s_ldx, 16)

                def g2(self, i):
                    sp.wait_ge(lns["lane0"][4], 1 + LN_G + i + 1)
                    settle(sp, "sp")
                    sp.dma_start(rows(tx[0], 1)[i], xn0[:, :, :]).then_inc(st_xn, 16)
                    sp.wait_ge(s_h0, NG + i + 1)
                    settle(sp, "sp")
                    sp.dma_start(hT_d[i], hA[:, :]).then_inc(st_h, 16)

                def la(self, l, g):
                    q = l * NG + g
                    sp.wait_ge(st_h, 1 + 16 * NG * (l + 1))
                    sp.wait_ge(L[0]["h_ready"], 1 + GRU_L + q)
                    settle(sp, "sp")
                    sp.dma_start(hA[:, :], hT_d[g]).then_inc(s_ldh, 16)
                    if l == LEVELS - 1:
                        sp.wait_ge(s_fin, 1 + g)
                        settle(sp, "sp")
                        sp.dma_start(xdr[:, :, :], rows(tx[0], 1)[g]).then_inc(s_ldx, 16)

                def lc(self, l, g):
                    q = l * NG + g
                    if l < LEVELS - 1:
                        sp.wait_ge(L[0]["h_ready"], 1 + GRU_L + q + 1)
                        settle(sp, "sp")
                        sp.dma_start(hT_d[g], hB[:, :]).then_inc(st_h, 16)
                        sp.wait_ge(s_stg, 1 + 3 * NG + q + 1)
                        settle(sp, "sp")
                        sp.dma_start(rows(tx[l + 1], 1)[g], stg[:, :, :]).then_inc(st_stg, 16)

            schedule(sp, Sync())
            sp.wait_ge(s_store1, 1 + 16 * ND)
            sp.wait_ge(s_scat, 2 * 16 * NT)

        @block.gpsimd
        def _(pool):
            def gather(buf, table, ix, done):
                for j in range(J):
                    nc.gpsimd.indirect_dma_start(
                        out=buf[:, j, :], out_offset=None, in_=table,
                        in_offset=bass.IndirectOffsetOnAxis(ap=ix[:, j:j + 1], axis=0)).then_inc(done, 16)

            def rstd(tag, n):
                b, s = lnb[tag], lns[tag]
                pool.wait_ge(s[1], n + 1)
                settle(pool, "pool")
                nc.gpsimd.tensor_scalar(b["nm"][:, :], b["ag"][:, :, 0], -1.0, None, ALU.mult)
                nc.gpsimd.tensor_scalar(b["rs"][:, :], b["ag"][:, :, 1], EPS, None, ALU.add).then_inc(s[2], 1)
                pool.wait_ge(s[2], 2 * n + 1)
                settle(pool, "pool")
                nc.gpsimd.tensor_tensor(b["rs"][:, :], b["rs"][:, :], mhalf[0:b["rs"].shape[0], 0:J], ALU.pow).then_inc(s[2], 1)
                pool.wait_ge(s[2], 2 * n + 2)
                settle(pool, "pool")
                nc.gpsimd.tensor_tensor(b["nm"][:, :], b["nm"][:, :], b["rs"][:, :], ALU.mult).then_inc(s[3], 1)

            class Pool(Pieces):
                def z(self, d):
                    rstd("pre1", d)

                def fin(self, d):
                    rstd("fin1", d)

                def s1(self, i):
                    rstd("lane0", i)

                def g1(self, i):
                    rstd("lane0", LN_G + i)

                def prep_weights(self):
                    nc.gpsimd.memset(mhalf[:, :], -0.5)
                    nc.gpsimd.memset(ident[:, :], 0.0)
                    nc.gpsimd.memset(tri[:, :], 1.0)
                    nc.gpsimd.iota(eR[:, :], pattern=[[1, P]], base=0, channel_multiplier=P)
                    nc.gpsimd.iota(ecI[:, :], pattern=[[P, NT]], base=0, channel_multiplier=1)
                    nc.gpsimd.iota(t0I[:, :], pattern=[[P, NT]], base=0, channel_multiplier=0).then_inc(s_const, 1)
                    pool.wait_ge(s_const, 1)
                    nc.gpsimd.affine_select(out=ident[:, :], in_=ident[:, :], compare_op=ALU.not_equal, fill=1.0,
                                            base=0, pattern=[[-1, P]], channel_multiplier=1)
                    nc.gpsimd.affine_select(out=tri[:, :], in_=tri[:, :], compare_op=ALU.is_ge, fill=0.0,
                                            base=0, pattern=[[1, P]], channel_multiplier=-1).then_inc(s_const, 1)

                def prep_edges(self):
                    pool.wait_ge(s_deg, 1)
                    nc.gpsimd.tensor_tensor(dinvF[:, :], dinvF[:, :], mhalf[0:NT, :], ALU.pow).then_inc(s_deg, 1)
                    pool.wait_ge(s_cols, 1)
                    pool.wait_ge(s_recinit, 16)
                    for t in range(NT):
                        nc.gpsimd.indirect_dma_start(
                            out=rec[:, :], out_offset=bass.IndirectOffsetOnAxis(ap=scatI[:, t:t + 1], axis=0),
                            in_=recrow[:, t, :], in_offset=None, bounds_check=N - 1,
                            oob_is_err=False).then_inc(s_scat, 16)
                    pool.wait_ge(s_scat, 16 * NT)
                    for t in range(NT):
                        nc.gpsimd.indirect_dma_start(
                            out=recS[:, t, :], out_offset=None, in_=rec[:, :],
                            in_offset=bass.IndirectOffsetOnAxis(ap=srcI[:, t:t + 1], axis=0)).then_inc(s_recg, 16)

                def s_load(self, i):
                    pool.wait_ge(s_scaled, 1 + 2 * i)
                    settle(pool, "pool")
                    nc.gpsimd.tensor_copy(idxa[:, :], srcI[:, bass.ds(i * J, J)]).then_inc(s_idxc, 1)
                    nc.gpsimd.tensor_copy(idxb[:, :], dstI[:, bass.ds(i * J, J)]).then_inc(s_idxc, 1)
                    pool.wait_ge(s_idxc, 2 * i + 2)
                    pool.wait_ge(s_u0, 1 + i)
                    settle(pool, "pool")
                    gather(xs, x[:, :], idxa, s_gs)
                    pool.wait_ge(s_scaled, 1 + 2 * i)
                    pool.wait_ge(st_xd, 1 + 16 * i)
                    settle(pool, "pool")
                    gather(xd, x[:, :], idxb, s_gd)

                def g_load(self, i):
                    pool.wait_ge(s_gs, 64 * (NG + i))
                    settle(pool, "pool")
                    nc.gpsimd.tensor_copy(idxa[:, :], idxI[:, bass.ds(i * J, J)]).then_inc(s_idxc, 1)
                    pool.wait_ge(s_idxc, 2 * NG + i + 1)
                    pool.wait_ge(s_idx, 1)
                    pool.wait_ge(st_zs, 1 + 16 * NG)
                    pool.wait_ge(st_zd, 1 + 16 * NG)
                    pool.wait_ge(s_scaled, 1 + 2 * NG + i)
                    pool.wait_ge(s_u0, 1 + NG)
                    settle(pool, "pool")
                    gather(xs, tz[:, :], idxa, s_gs)

                def la(self, l, g):
                    q = l * NG + g
                    copies = 3 * NG + q + (g if l == LEVELS - 1 else 0)
                    pool.wait_ge(s_gs, 64 * (2 * NG + q))
                    settle(pool, "pool")
                    nc.gpsimd.tensor_copy(idxa[:, :], idxI[:, bass.ds(g * J, J)]).then_inc(s_idxc, 1)
                    pool.wait_ge(s_idxc, copies + 1)
                    pool.wait_ge(st_xn, 1 + 16 * 2 * NG)
                    pool.wait_ge(st_stg, 1 + 16 * NG * (3 + l))
                    pool.wait_ge(s_scaled, 1 + 3 * NG)
                    pool.wait_ge(L[0]["m_filled"], 1 + M_L + LU * q - 2)
                    settle(pool, "pool")
                    gather(xs, tx[l][:, :], idxa, s_gs)

                def lc(self, l, g):
                    if l == LEVELS - 1:
                        pool.wait_ge(s_scat, 16 * NT + 16 * J * g)
                        settle(pool, "pool")
                        nc.gpsimd.tensor_copy(idxb[:, :], scatI[:, bass.ds(g * J, J)]).then_inc(s_idxc, 1)
                        pool.wait_ge(s_idxc, 3 * NG + l * NG + 2 * g + 2)
                        settle(pool, "pool")
                        rstd("lane0", LN_L + g)
                        pool.wait_ge(lns["lane0"][4], 1 + LN_L + g + 1)
                        pool.wait_ge(s_store1, 1 + 16 * ND)
                        settle(pool, "pool")
                        for j in range(J):
                            nc.gpsimd.indirect_dma_start(
                                out=out[:, :], out_offset=bass.IndirectOffsetOnAxis(ap=idxb[:, j:j + 1], axis=0),
                                in_=xn0[:, j, :], in_offset=None, bounds_check=N - 1,
                                oob_is_err=False).then_inc(s_scat, 16)

            schedule(pool, Pool())

        @block.tensor
        def _(pe):
            def transposes(lane, source, p):
                bank = pM[lane]
                for j in range(J):
                    last = nc.tensor.transpose(bank[:, j * p:(j + 1) * p], source[:, j, :], ident[0:p, 0:p])
                last.then_inc(L[lane]["m_filled"], 1)

            def back(lane, source, p):
                bank = pM[lane]
                for j in range(J):
                    last = nc.tensor.transpose(bank[0:p, j * P:(j + 1) * P], source[:, j * p:(j + 1) * p], ident[:, :])
                last.then_inc(L[lane]["m_filled"], 1)

            def gates(lane, n, h, agg=None, l=None):
                s, w = L[lane], W[lane]
                pe.wait_ge(s["r_ready"], 1 + n)
                nc_mm = nc.tensor.matmul
                last = nc_mm(pR[lane][:, 0:w], whT[:, 0:P], h, start=True, stop=agg is None)
                if agg is not None:
                    last = nc_mm(pR[lane][:, 0:w], wlT[:, l, 0:P], agg, start=False, stop=True)
                last.then_inc(s["r_filled"], 1)
                pe.wait_ge(s["t_ready"], 1 + n)
                nc_mm(pN[lane][:, 0:w], whT[:, 2 * P:3 * P], h, start=True, stop=True).then_inc(s["n_filled"], 1)
                if agg is not None:
                    nc_mm(pM[lane][:, 0:w], wlT[:, l, 2 * P:3 * P], agg, start=True, stop=True).then_inc(s["m_filled"], 1)
                pe.wait_ge(s["z_ready"], 1 + n)
                last = nc_mm(pZ[lane][:, 0:w], whT[:, P:2 * P], h, start=True, stop=agg is None)
                if agg is not None:
                    last = nc_mm(pZ[lane][:, 0:w], wlT[:, l, P:2 * P], agg, start=False, stop=True)
                last.then_inc(s["z_filled"], 1)

            def sums(i, source):
                for j in range(J):
                    last = nc.tensor.matmul(pM[0][:, j * P:(j + 1) * P], source[:, j, :],
                                            S[:, bass.ds((i * J + j) * P, P)], start=True, stop=True)
                last.then_inc(L[0]["m_filled"], 1)

            class Tensor(Pieces):
                def prep_weights(self):
                    pe.wait_ge(s_const, 2)
                    pe.wait_ge(s_wload, 16 * 9)
                    for c in range(2):
                        last = nc.tensor.transpose(pR[0][:, c * P:(c + 1) * P], W1s[:, c * P:(c + 1) * P], ident[:, :])
                    for c in range(3):
                        last = nc.tensor.transpose(pN[0][:, c * P:(c + 1) * P], wih_s[:, c, :], ident[:, :])
                    for c in range(3):
                        last = nc.tensor.transpose(pZ[0][:, c * P:(c + 1) * P], whh_s[:, c, :], ident[:, :])
                    for c in range(LEVELS):
                        last = nc.tensor.transpose(pM[0][:, c * P:(c + 1) * P], gw_s[:, c, :], ident[:, :])
                    last.then_inc(s_prep_pe, 1)
                    pe.wait_ge(s_prep_cp, 1)
                    for c in range(2):
                        nc.tensor.matmul(pR[1][:, 0:P], W1T[:, c, :], W2s[:, c, :], start=c == 0, stop=c == 1)
                    for c in range(2):
                        nc.tensor.matmul(pN[1][:, 0:P], b1f[:, c, :], W2s[:, c, :], start=c == 0, stop=c == 1)
                    for l, b in enumerate((pZ[1], pM[1], pR[0], pN[0])):
                        last = nc.tensor.matmul(b[:, 0:3 * P], gwT[:, l, :], wiT[:, :], start=True, stop=True)
                    last.then_inc(s_prep_pe, 1)
                    pe.wait_ge(s_wready, 1)

                def prep_edges(self):
                    pe.wait_ge(s_car_pe, 1)
                    nc.tensor.matmul(pR[0][0:1, 0:NT], runF[:, P - 1:P], ident[0:NT, 0:NT], start=True, stop=True).then_inc(s_car_pe, 1)
                    pe.wait_ge(s_car_pe, 3)
                    nc.tensor.matmul(pN[0][0:NT, 0:1], carF[0:1, 0:NT], one[0:1, 0:1], start=True, stop=True).then_inc(s_car_pe, 1)
                    pe.wait_ge(s_col_pe, 1)
                    pe.wait_ge(s_deg, 2)
                    for c, t in enumerate((dstF, srcF, dinvF, scatF)):
                        last = nc.tensor.transpose(pZ[0][:, c * NT:(c + 1) * NT], t[:, :], ident[0:NT, 0:NT])
                    last.then_inc(s_col_pe, 1)

                def gru1(self, d, k):
                    if k == 0:
                        pe.wait_ge(s_x1T, d + 1)
                    else:
                        pe.wait_ge(L[1]["h_ready"], 1 + 4 * d + k)
                    gates(1, 4 * d + k, x1T[:, :] if k == 0 else h1[:, :])

                def xt(self, d):
                    pe.wait_ge(s_x1load, 16 * d + 16)
                    if isinstance(d, int) and d == 1:
                        pe.wait_ge(s_x1T, 1)
                    elif not isinstance(d, int) or d > 1:
                        pe.wait_ge(lns["fin1"][4], 1 + d - 1)
                    transposes(1, xr1, DP)

                def z(self, d):
                    pe.wait_ge(s_xT1, d + 1)
                    for j in range(J):
                        last = nc.tensor.matmul(pM[1][0:DP, j * P:(j + 1) * P], xT1[:, j * DP:(j + 1) * DP], W12[:, :],
                                                start=True, stop=True)
                    last.then_inc(L[1]["m_filled"], 1)

                def x1(self, d):
                    pe.wait_ge(lns["pre1"][4], 1 + d + 1)
                    pe.wait_ge(s_z1, d + 1)
                    transposes(1, xn1, DP)

                def fin(self, d):
                    pe.wait_ge(s_uT, d + 1)
                    if isinstance(d, int) and d == ND - 1:
                        pe.wait_ge(lns["fin1"][4], 1 + d)
                    else:
                        pe.wait_ge(s_x1T, d + 2)
                    back(1, uT, DP)

                def s0(self, i):
                    pe.wait_ge(s_gs, 64 * i + 64)
                    pe.wait_ge(s_stg, 1 + 3 * i)
                    transposes(0, xs, P)
                    pe.wait_ge(s_scaled, 1 + 2 * i + 1)
                    pe.wait_ge(s_S, NT)
                    pe.wait_ge(s_xsT, i + 1)
                    sums(i, msg)
                    pe.wait_ge(s_carry, 1 + J * (i + 1))
                    for j in range(J):
                        last = nc.tensor.matmul(pM[0][:, j * P:(j + 1) * P], xsT[:, j * P:(j + 1) * P], W12[:, :],
                                                start=True, stop=True)
                    last.then_inc(L[0]["m_filled"], 1)

                def s1(self, i):
                    pe.wait_ge(s_scaled, 1 + 2 * i + 2)
                    pe.wait_ge(s_zs, i + 1)
                    transposes(0, xdd, P)
                    pe.wait_ge(s_self, i + 1)
                    for j in range(J):
                        last = nc.tensor.matmul(pM[0][:, j * P:(j + 1) * P], aggS[:, j * P:(j + 1) * P], W12[:, :],
                                                start=True, stop=True)
                    last.then_inc(L[0]["m_filled"], 1)
                    pe.wait_ge(lns["lane0"][4], 1 + i + 1)
                    pe.wait_ge(s_zd, i + 1)
                    transposes(0, xn0, P)

                def s_gru(self, i, k):
                    n = 3 * i + k
                    if k == 0:
                        pe.wait_ge(s_h0, i + 1)
                    else:
                        pe.wait_ge(L[0]["h_ready"], 1 + n)
                    gates(0, n, hA[:, :] if k == 0 else hB[:, :])
                    pe.wait_ge(L[0]["h_ready"], 1 + n + 1)
                    if k:
                        pe.wait_ge(s_stg, 1 + n)
                    back(0, hB, P)

                def g0(self, i):
                    pe.wait_ge(s_scaled, 1 + 2 * NG + i + 1)
                    pe.wait_ge(s_stg, 1 + 3 * NG)
                    pe.wait_ge(s_h0, NG + i)
                    sums(i, msg)

                def g1(self, i):
                    pe.wait_ge(s_carry, 1 + J * (NG + i + 1))
                    back(0, aggS, P)

                def g2(self, i):
                    pe.wait_ge(lns["lane0"][4], 1 + LN_G + i + 1)
                    pe.wait_ge(s_zpre, 1 + i + 1)
                    transposes(0, xn0, P)

                def la(self, l, g):
                    q = l * NG + g
                    pe.wait_ge(s_gs, 64 * (2 * NG + q) + 64)
                    if l == LEVELS - 1:
                        pe.wait_ge(s_stg, 1 + 3 * NG + l * NG)
                        pe.wait_ge(s_fin, 1 + g)
                    else:
                        pe.wait_ge(s_h0, 2 * NG)
                        pe.wait_ge(s_stg, 1 + 3 * NG + q)
                    sums(g, xs)

                def lb(self, l, g):
                    q = l * NG + g
                    pe.wait_ge(s_ldh, 16 * q + 16)
                    pe.wait_ge(s_carry, 1 + J * (2 * NG + q + 1))
                    gates(0, GRU_L + q, hA[:, :], aggS[:, :], l)

                def lc(self, l, g):
                    q = l * NG + g
                    pe.wait_ge(L[0]["h_ready"], 1 + GRU_L + q + 1)
                    pe.wait_ge(s_in, q + 1)
                    back(0, hB, P)

            schedule(pe, Tensor())

        @block.scalar
        def _(act):
            def gate_acts(lane, n, added):
                s, w = L[lane], W[lane]
                act.wait_ge(s["r_filled"], n + 1)
                act.wait_ge(s["t_ready"], 1 + n)
                nc.scalar.activation(rS[lane][:, :], pR[lane][:, 0:w], ACT.Sigmoid, bias=brz[:, 0:1]).then_inc(s["r_ready"], 1)
                act.wait_ge(s["z_filled"], n + 1)
                act.wait_ge(s["gated_ready"], 1 + n)
                nc.scalar.activation(zS[lane][:, :], pZ[lane][:, 0:w], ACT.Sigmoid, bias=brz[:, 1:2]).then_inc(s["z_ready"], 1)
                if added is None:
                    act.wait_ge(s["t_ready"], 1 + n + 1)
                else:
                    act.wait_ge(s_in, added)
                act.wait_ge(s["h_ready"], 1 + n)
                nc.scalar.activation(nS[lane][:, :], tS[lane][:, :], ACT.Tanh, bias=b3[:, 0, 2:3]).then_inc(s["tanh_ready"], 1)

            def normalise(tag, n, source, dest, p, drained=None):
                b, s = lnb[tag], lns[tag]
                act.wait_ge(s[3], n + 1)
                for j in range(J):
                    last = nc.scalar.activation(dest[:, j, :], source(j), ACT.Identity,
                                                scale=b["rs"][:, j:j + 1], bias=b["nm"][:, j:j + 1])
                last.then_inc(s[4], 1)

            def copy_m(lane, use, dest, done):
                act.wait_ge(L[lane]["m_filled"], 1 + use + 1)
                nc.scalar.activation(dest, pM[lane][:, 0:W[lane]], ACT.Identity).then_inc(done, 1)

            class Scalar(Pieces):
                def gru1(self, d, k):
                    gate_acts(1, 4 * d + k, None)

                def xt(self, d):
                    act.wait_ge(L[1]["m_filled"], 1 + m1("xt", d) + 1)
                    nc.scalar.activation(xT1[:, :], pM[1][:, 0:DW], ACT.Identity).then_inc(s_xT1, 1)
                    act.wait_ge(s_xT1, d + 1)

                def z(self, d):
                    act.wait_ge(s_z1, d + 1)
                    nc.scalar.activation(z1[:, :, :], z1[:, :, :], ACT.Sigmoid).then_inc(s_sig1, 1)
                    act.wait_ge(s_x1T, d)
                    normalise("pre1", d, lambda j: z1[:, j, :], xn1, DP)

                def fin(self, d):
                    act.wait_ge(s_store1, 1 + 16 * d)
                    normalise("fin1", d, lambda j: pM[1][0:DP, j * P:(j + 1) * P], o1, DP)
                    act.wait_ge(lns["fin1"][4], 1 + d + 1)

                def s0(self, i):
                    copy_m(0, SU * i, xsT[:, :], s_xsT)
                    act.wait_ge(s_xsT, i + 1)
                    act.wait_ge(s_zb, i + 1)
                    nc.scalar.activation(z0[:, :, :], z0[:, :, :], ACT.Sigmoid).then_inc(s_sig0, 1)

                def s1(self, i):
                    act.wait_ge(st_xn, 1 + 16 * i)
                    normalise("lane0", i, lambda j: z0[:, j, :], xn0, P)
                    act.wait_ge(L[0]["h_ready"], 1 + 3 * i)
                    copy_m(0, SU * i + 5, hA[:, :], s_h0)
                    act.wait_ge(s_h0, i + 1)

                def s_gru(self, i, k):
                    gate_acts(0, 3 * i + k, None)
                    act.wait_ge(st_stg, 1 + 16 * (3 * i + k))
                    copy_m(0, SU * i + 6 + k, stg[:, :, :].rearrange("p j f -> p (j f)"), s_stg)
                    act.wait_ge(s_stg, 1 + 3 * i + k + 1)

                def g1(self, i):
                    act.wait_ge(s_zb, NG + i + 1)
                    nc.scalar.activation(z0[:, :, :], z0[:, :, :], ACT.Sigmoid).then_inc(s_sig0, 1)

                def g2(self, i):
                    act.wait_ge(st_xn, 1 + 16 * (NG + i))
                    normalise("lane0", LN_G + i, lambda j: z0[:, j, :], xn0, P)
                    act.wait_ge(st_h, 1 + 16 * i)
                    copy_m(0, M_G + GU * i + 2, hA[:, :], s_h0)
                    act.wait_ge(s_h0, NG + i + 1)

                def lb(self, l, g):
                    q = l * NG + g
                    gate_acts(0, GRU_L + q, q + 1)

                def lc(self, l, g):
                    q = l * NG + g
                    if l < LEVELS - 1:
                        act.wait_ge(st_stg, 1 + 16 * (3 * NG + q))
                        copy_m(0, M_L + LU * q + 2, stg[:, :, :].rearrange("p j f -> p (j f)"), s_stg)
                        act.wait_ge(s_stg, 1 + 3 * NG + q + 1)
                    else:
                        act.wait_ge(st_xn, 1 + 16 * 2 * NG)
                        act.wait_ge(s_scat, 16 * NT + 16 * J * g)
                        normalise("lane0", LN_L + g, lambda j: z0[:, j, :], xn0, P)

            schedule(act, Scalar())

        @block.vector
        def _(dve):
            V = nc.vector

            def gru(lane, n, h, hout, h_wait=None, added=None, use=None):
                s, w = L[lane], W[lane]
                dve.wait_ge(s["r_ready"], 1 + n + 1)
                dve.wait_ge(s["n_filled"], n + 1)
                V.scalar_tensor_tensor(out=tS[lane][:, :], in0=pN[lane][:, 0:w], scalar=b3[:, 1, 2:3], in1=rS[lane][:, :],
                                       op0=ALU.add, op1=ALU.mult).then_inc(s["t_ready"], 1)
                if added is not None:
                    dve.wait_ge(s["t_ready"], 1 + n + 1)
                    dve.wait_ge(s["m_filled"], 1 + use + 1)
                    V.tensor_tensor(tS[lane][:, :], tS[lane][:, :], pM[lane][:, 0:w], ALU.add).then_inc(s_in, 1)
                    dve.wait_ge(s_in, added)
                dve.wait_ge(s["tanh_ready"], n + 1)
                dve.wait_ge(s["h_ready"], 1 + n)
                V.tensor_tensor(dS[lane][:, :], h, nS[lane][:, :], ALU.subtract).then_inc(s["diff_ready"], 1)
                dve.wait_ge(s["diff_ready"], n + 1)
                dve.wait_ge(s["z_ready"], 1 + n + 1)
                V.tensor_tensor(dS[lane][:, :], dS[lane][:, :], zS[lane][:, :], ALU.mult).then_inc(s["gated_ready"], 1)
                dve.wait_ge(s["gated_ready"], 1 + n + 1)
                V.tensor_tensor(hout, dS[lane][:, :], nS[lane][:, :], ALU.add).then_inc(s["h_ready"], 1)

            def ln_stats(tag, n, source):
                b, s = lnb[tag], lns[tag]
                for j in range(J):
                    last = V.bn_stats(b["st"][:, j, :], source(j))
                last.then_inc(s[0], 1)
                dve.wait_ge(s[0], n + 1)
                dve.wait_ge(s[4], 1 + n)
                settle(dve, "dve")
                for j in range(J):
                    last = V.bn_aggr(b["ag"][:, j, :], b["st"][:, j, :])
                last.then_inc(s[1], 1)

            def carries(i, use, n):
                dve.wait_ge(L[0]["m_filled"], 1 + use + 1)
                for j in range(J):
                    dve.wait_ge(s_carry, 1 + J * n + j)
                    if j == 0:
                        dve.wait_ge(s_carried, 1 + n)
                    a = aggS[:, j * P:(j + 1) * P]
                    before = carry[:, 0:1] if j == 0 else aggS[:, j * P - 1:j * P]
                    V.scalar_tensor_tensor(out=a, in0=FL[:, bass.ds((i * J + j) * P, P)], scalar=before,
                                           in1=pM[0][:, j * P:(j + 1) * P], op0=ALU.mult, op1=ALU.add).then_inc(s_carry, 1)
                dve.wait_ge(s_carry, 1 + J * n + J)
                V.tensor_copy(carry[:, 0:1], aggS[:, GS - 1:GS]).then_inc(s_carried, 1)

            carry = ctx.enter_context(nc.sbuf_tensor("carry", [P, 1], f32))
            steps = [0]

            def chain(ins):
                steps[0] += 1
                ins.then_inc(s_chain, 1)
                dve.wait_ge(s_chain, steps[0])

            class Vector(Pieces):
                def prep_weights(self):
                    V.memset(dstR[:, :], N)
                    V.memset(prevR[:, :], N)
                    V.memset(nextR[:, :], N)
                    V.memset(srcR[:, :], 0)
                    V.memset(one[:, :], 1.0)
                    V.memset(carF[:, :], 0.0)
                    V.memset(carry[:, :], 0.0)
                    V.memset(recfill[:, :, 0], -1.0)
                    chain(V.memset(recfill[:, :, 1], 1.0))
                    V.memset(prevR[0:1, 0:1], -1).then_inc(s_pads, 1)
                    dve.wait_ge(s_wload, 16 * 9)
                    chain(V.tensor_tensor(brz[:, 0:2], b3[:, 0, 0:2], b3[:, 1, 0:2], ALU.add))
                    V.tensor_copy(b1f[:, 0, :], b1c[:, 0:1].broadcast_to([P, P]))
                    V.tensor_copy(b1f[:, 1, :], b1c[:, 1:2].broadcast_to([P, P]))
                    dve.wait_ge(s_prep_pe, 1)
                    V.tensor_copy(W1T[:, :, :].rearrange("p c f -> p (c f)"), pR[0][:, 0:2 * P])
                    V.tensor_copy(wiT[:, :], pN[0][:, 0:3 * P])
                    V.tensor_copy(whT[:, :], pZ[0][:, 0:3 * P])
                    V.tensor_copy(gwT[:, :, :].rearrange("p c f -> p (c f)"), pM[0][:, 0:LEVELS * P]).then_inc(s_prep_cp, 1)
                    dve.wait_ge(s_prep_pe, 2)
                    V.tensor_copy(W12[:, :], pR[1][:, 0:P])
                    for l, b in enumerate((pZ[1], pM[1], pR[0], pN[0])):
                        V.tensor_copy(wlT[:, l, :], b[:, 0:3 * P])
                    chain(V.tensor_copy(c_bc[:, :], pN[1][:, 0:P]))
                    V.tensor_tensor(cb2_bc[:, :], c_bc[:, :], b2_bc[:, :], ALU.add).then_inc(s_wready, 1)
                    dve.wait_ge(s_wready, 1)

                def prep_edges(self):
                    dve.wait_ge(s_eload, 16 * 9)
                    dve.wait_ge(s_const, 2)
                    for a, b in ((dstF, dstR), (prevF, prevR), (nextF, nextR), (srcF, srcR), (eF, eR)):
                        V.tensor_copy(a[:, :], b[:, :])
                    V.tensor_copy(ecol[:, :], ecI[:, :])
                    chain(V.tensor_copy(t0col[:, :], t0I[:, :]))
                    chain(V.tensor_tensor(startF[:, :], dstF[:, :], prevF[:, :], ALU.not_equal))
                    chain(V.tensor_tensor(startF[:, :], startF[:, :], eF[:, :], ALU.mult))
                    V.tensor_tensor_scan(runF[:, :], startF[:, :], startF[:, :], 0.0, ALU.max, ALU.max).then_inc(s_car_pe, 1)
                    dve.wait_ge(s_car_pe, 2)
                    chain(V.tensor_copy(mv[0:1, 0:NT], pR[0][0:1, 0:NT]))
                    V.tensor_tensor_scan(carF[0:1, 1:NT + 1], mv[0:1, 0:NT], mv[0:1, 0:NT], 0.0, ALU.max, ALU.max).then_inc(s_car_pe, 1)
                    dve.wait_ge(s_car_pe, 4)
                    chain(V.tensor_copy(isd[0:NT, 0:1], pN[0][0:NT, 0:1]))
                    V.tensor_scalar(firstF[:, :], runF[:, :], isd[0:NT, 0:1], None, ALU.max).then_inc(s_first, 1)
                    dve.wait_ge(s_first, 1)
                    chain(V.tensor_tensor(dinvF[:, :], eF[:, :], firstF[:, :], ALU.subtract))
                    V.tensor_scalar(dinvF[:, :], dinvF[:, :], 2.0, None, ALU.add).then_inc(s_deg, 1)
                    chain(V.tensor_tensor(scatF[:, :], dstF[:, :], nextF[:, :], ALU.is_equal))
                    V.scalar_tensor_tensor(out=scatF[:, :], in0=scatF[:, :], scalar=float(2 * N), in1=dstF[:, :],
                                           op0=ALU.mult, op1=ALU.add).then_inc(s_col_pe, 1)
                    dve.wait_ge(s_col_pe, 2)
                    V.tensor_copy(dstC[:, :], pZ[0][:, 0:NT])
                    V.tensor_copy(srcI[:, :], pZ[0][:, NT:2 * NT])
                    V.tensor_copy(dinvD[:, :], pZ[0][:, 2 * NT:3 * NT])
                    V.tensor_copy(recrow[:, :, 1], pZ[0][:, 2 * NT:3 * NT])
                    V.tensor_copy(scatI[:, :], pZ[0][:, 3 * NT:4 * NT])
                    chain(V.tensor_copy(recrow[:, :, 0], ecol[:, :]))
                    V.tensor_scalar(dstI[:, :], dstC[:, :], float(N - 1), None, ALU.min).then_inc(s_cols, 1)

                def prep_edges2(self):
                    dve.wait_ge(s_firstld, 16)
                    with dve.Fori(0, NT) as t:
                        cols = bass.ds(t * P, P)
                        V.tensor_scalar(FL[:, cols], S[:, cols], t0col[:, bass.ds(t, 1)], None, ALU.is_lt)
                        V.scalar_tensor_tensor(out=S[:, cols], in0=S[:, cols], scalar=ecol[:, bass.ds(t, 1)],
                                               in1=tri[:, :], op0=ALU.is_le, op1=ALU.mult).then_inc(s_S, 1)
                    dve.wait_ge(s_S, NT)
                    dve.wait_ge(s_recg, 16 * NT)
                    V.tensor_scalar(isd[:, :], recS[:, :, 0], 0.0, None, ALU.is_ge)
                    chain(V.tensor_tensor(mv[:, :], recS[:, :, 0], ecol[:, :], ALU.subtract))
                    chain(V.scalar_tensor_tensor(out=mv[:, :], in0=mv[:, :], scalar=float(NS), in1=isd[:, :],
                                                 op0=ALU.add, op1=ALU.mult))
                    V.tensor_tensor(idxI[:, :], mv[:, :], ecol[:, :], ALU.add).then_inc(s_idx, 1)
                    dve.wait_ge(s_idx, 1)

                def gru1(self, d, k):
                    if k == 0:
                        dve.wait_ge(s_uT, d)
                    gru(1, 4 * d + k, x1T[:, :] if k == 0 else h1[:, :], h1[:, :])

                def z(self, d):
                    dve.wait_ge(L[1]["m_filled"], 1 + m1("z", d) + 1)
                    dve.wait_ge(lns["pre1"][4], 1 + d)
                    V.tensor_tensor(z1[:, :, :], pM[1][0:DP, :].rearrange("p (j f) -> p j f", j=J),
                                    cb2_bc[0:DP, :].unsqueeze(1).broadcast_to([DP, J, P]), ALU.add).then_inc(s_z1, 1)
                    dve.wait_ge(s_z1, d + 1)
                    dve.wait_ge(s_sig1, d + 1)
                    V.tensor_tensor(z1[:, :, :], z1[:, :, :], xr1[:, :, :], ALU.add).then_inc(s_u1, 1)
                    dve.wait_ge(s_u1, d + 1)
                    ln_stats("pre1", d, lambda j: z1[:, j, :])

                def x1(self, d):
                    dve.wait_ge(L[1]["m_filled"], 1 + m1("x1", d) + 1)
                    dve.wait_ge(s_uT, d)
                    V.tensor_copy(x1T[:, :], pM[1][:, 0:DW]).then_inc(s_x1T, 1)
                    dve.wait_ge(s_x1T, d + 1)

                def u(self, d):
                    dve.wait_ge(lns["fin1"][4], 1 + d)
                    dve.wait_ge(L[1]["h_ready"], 1 + 4 * d + 4)
                    V.scalar_tensor_tensor(out=uT[:, :], in0=x1T[:, :], scalar=2.0, in1=h1[:, :],
                                           op0=ALU.mult, op1=ALU.add).then_inc(s_uT, 1)

                def fin(self, d):
                    dve.wait_ge(L[1]["m_filled"], 1 + m1("fin", d) + 1)
                    ln_stats("fin1", d, lambda j: pM[1][0:DP, j * P:(j + 1) * P])

                def s0(self, i):
                    dve.wait_ge(s_gs, 64 * i + 64)
                    dve.wait_ge(s_idx, 1)
                    dve.wait_ge(L[0]["m_filled"], 1 + SU * i)
                    for j in range(J):
                        last = V.tensor_scalar(msg[:, j, :], xs[:, j, :], recS[:, bass.ds(i * J + j, 1), 1], None, ALU.mult)
                    last.then_inc(s_scaled, 1)
                    dve.wait_ge(s_gd, 64 * i + 64)
                    for j in range(J):
                        last = V.tensor_scalar(xdd[:, j, :], xd[:, j, :], dinvD[:, bass.ds(i * J + j, 1)], None, ALU.mult)
                    last.then_inc(s_scaled, 1)
                    carries(i, SU * i + 1, i)
                    dve.wait_ge(L[0]["m_filled"], 1 + SU * i + 3)
                    dve.wait_ge(st_zs, 1 + 16 * i)
                    V.tensor_tensor(zrow[:, :, :], pM[0][:, :].rearrange("p (j f) -> p j f", j=J),
                                    c_bc[:, :].unsqueeze(1).broadcast_to([P, J, P]), ALU.add).then_inc(s_zs, 1)
                    dve.wait_ge(s_zs, i + 1)
                    dve.wait_ge(lns["lane0"][4], 1 + i)
                    V.tensor_tensor(z0[:, :, :], zrow[:, :, :], b2_bc[:, :].unsqueeze(1).broadcast_to([P, J, P]),
                                    ALU.add).then_inc(s_zb, 1)

                def s1(self, i):
                    dve.wait_ge(s_sig0, i + 1)
                    V.tensor_tensor(z0[:, :, :], z0[:, :, :], xs[:, :, :], ALU.add).then_inc(s_u0, 1)
                    dve.wait_ge(s_u0, 1 + i + 1)
                    ln_stats("lane0", i, lambda j: z0[:, j, :])
                    dve.wait_ge(L[0]["m_filled"], 1 + SU * i + 4)
                    V.tensor_tensor(aggS[:, :], aggS[:, :], pM[0][:, :], ALU.add).then_inc(s_self, 1)
                    dve.wait_ge(s_self, i + 1)
                    dve.wait_ge(L[0]["m_filled"], 1 + SU * i + 5)
                    dve.wait_ge(st_zd, 1 + 16 * i)
                    for j in range(J):
                        last = V.scalar_tensor_tensor(out=zD[:, j, :], in0=pM[0][:, j * P:(j + 1) * P],
                                                      scalar=dinvD[:, bass.ds(i * J + j, 1)], in1=c_bc[:, :],
                                                      op0=ALU.mult, op1=ALU.add)
                    last.then_inc(s_zd, 1)
                    dve.wait_ge(s_zd, i + 1)

                def s_gru(self, i, k):
                    if k == 0:
                        dve.wait_ge(s_h0, i + 1)
                    gru(0, 3 * i + k, hA[:, :] if k == 0 else hB[:, :], hB[:, :])

                def g0(self, i):
                    dve.wait_ge(s_gs, 64 * (NG + i) + 64)
                    dve.wait_ge(L[0]["m_filled"], 1 + M_G + GU * i)
                    if True:
                        for j in range(J):
                            last = V.tensor_scalar(msg[:, j, :], xs[:, j, :], recS[:, bass.ds(i * J + j, 1), 1], None, ALU.mult)
                        last.then_inc(s_scaled, 1)
                    carries(i, M_G + GU * i, NG + i)

                def g1(self, i):
                    dve.wait_ge(L[0]["m_filled"], 1 + M_G + GU * i + 2)
                    dve.wait_ge(s_ldz, 16 * i + 16)
                    dve.wait_ge(lns["lane0"][4], 1 + LN_G + i)
                    for j in range(J):
                        last = V.scalar_tensor_tensor(out=z0[:, j, :], in0=zDr[:, j, :], scalar=dinvD[:, bass.ds(i * J + j, 1)],
                                                      in1=pM[0][:, j * P:(j + 1) * P], op0=ALU.mult, op1=ALU.add)
                    last.then_inc(s_zpre, 1)
                    dve.wait_ge(s_zpre, 1 + i + 1)
                    for j in range(J):
                        last = V.scalar_tensor_tensor(out=z0[:, j, :], in0=z0[:, j, :], scalar=dinvD[:, bass.ds(i * J + j, 1)],
                                                      in1=b2_bc[:, :], op0=ALU.mult, op1=ALU.add)
                    last.then_inc(s_zb, 1)
                    dve.wait_ge(s_sig0, NG + i + 1)
                    dve.wait_ge(s_ldx, 16 * i + 16)
                    V.tensor_tensor(z0[:, :, :], z0[:, :, :], xdr[:, :, :], ALU.add).then_inc(s_u0, 1)
                    dve.wait_ge(s_u0, 1 + NG + i + 1)
                    ln_stats("lane0", LN_G + i, lambda j: z0[:, j, :])

                def la(self, l, g):
                    q = l * NG + g
                    carries(g, M_L + LU * q, 2 * NG + q)

                def lb(self, l, g):
                    q = l * NG + g
                    dve.wait_ge(L[0]["m_filled"], 1 + M_L + LU * q)
                    dve.wait_ge(st_h, 1 + (16 * (NG + q) if l < LEVELS - 1 else 16 * NG * LEVELS))
                    dve.wait_ge(s_ldh, 16 * q + 16)
                    gru(0, GRU_L + q, hA[:, :], hB[:, :], added=q + 1, use=M_L + LU * q + 1)

                def lc(self, l, g):
                    q = l * NG + g
                    if l == LEVELS - 1:
                        dve.wait_ge(L[0]["m_filled"], 1 + M_L + LU * q + 3)
                        dve.wait_ge(s_ldx, 16 * (NG + g) + 16)
                        dve.wait_ge(lns["lane0"][4], 1 + LN_L + g)
                        V.scalar_tensor_tensor(out=z0[:, :, :].rearrange("p j f -> p (j f)"),
                                               in0=xdr[:, :, :].rearrange("p j f -> p (j f)"), scalar=2.0,
                                               in1=pM[0][:, :], op0=ALU.mult, op1=ALU.add).then_inc(s_fin, 1)
                        dve.wait_ge(s_fin, 1 + g + 1)
                        ln_stats("lane0", LN_L + g, lambda j: z0[:, j, :])

            schedule(dve, Vector())


_INS = ['x', 'src', 'dst', 'L0_gnn_W1', 'L0_gnn_b1', 'L0_gnn_W2', 'L0_gnn_b2', 'L1_gnn_weight',
        'L1_gnn_w_ih', 'L1_gnn_w_hh', 'L1_gnn_b_ih', 'L1_gnn_b_hh']


def kernel(**inputs):
    import numpy as _np
    import concourse.bacc as _bacc
    from concourse import mybir as _mybir
    from concourse.bass_utils import run_bass_kernel_spmd as _run

    nc = _bacc.Bacc("TRN2", target_bir_lowering=False, num_devices=1)
    arrays, args = {}, []
    for name in _INS:
        a = _np.ascontiguousarray(inputs[name])
        arrays[f"in_{name}_dram"] = a
        args.append(nc.dram_tensor(f"in_{name}_dram", a.shape, _mybir.dt.from_np(a.dtype), kind="ExternalInput").ap())
    shape = inputs["x"].shape
    args.append(nc.dram_tensor("out_0_dram", shape, _mybir.dt.float32, kind="ExternalOutput").ap())
    gcn_resnorm_ggnn_resnorm(nc, *args)
    r = _run(nc, [arrays], core_ids=[0])
    return r.results[0]["out_0_dram"]
```

```python
import concourse.bass as bass
from concourse import mybir
from contextlib import ExitStack


def gcn_resnorm_ggnn_resnorm(
    nc: bass.Bass,
    x: bass.AP, src: bass.AP, dst: bass.AP,
    W1: bass.AP, b1: bass.AP, W2: bass.AP, b2: bass.AP,
    gw: bass.AP, w_ih: bass.AP, w_hh: bass.AP, b_ih: bass.AP, b_hh: bass.AP,
    out: bass.AP,
):
    f32 = mybir.dt.float32
    bf16 = mybir.dt.bfloat16
    i32 = mybir.dt.int32
    ALU = mybir.AluOpType
    ACT = mybir.ActivationFunctionType

    N, F = x.shape
    E = src.shape[0]
    HID = W1.shape[1]
    LEVELS = gw.shape[0]
    P = 128
    J = 4
    GS = J * P
    NG = -(-E // GS)
    NT = NG * J
    NS = NT * P
    FULL = E // P
    REST = E - FULL * P
    DP = 125
    DW = DP * J
    ND = N // DW
    EPS = 1e-5
    PAIRS = (NG - 1) // 2
    LEAD = ND - 2 * NG - (LEVELS - 1) * (PAIRS + 1)
    assert N == ND * DW and NG % 2 == 1 and LEAD >= 2

    x_g = x.rearrange("(g p j) f -> g p (j f)", p=DP, j=J)
    out_g = out.rearrange("(g p j) f -> g p (j f)", p=DP, j=J)

    ctx = ExitStack()
    with ctx:
        def sb(name, shape, dt=f32):
            return ctx.enter_context(nc.sbuf_tensor(name, shape, dt))

        def sem(name):
            return ctx.enter_context(nc.semaphore(name))

        def dram(name, shape, dt=f32):
            return nc.dram_tensor(name, shape, dt)

        tz = dram("tz", [2 * NS, F])
        tx = [dram(f"tx{l}", [2 * NS, F]) for l in range(LEVELS)]
        rec = dram("rec", [N, 2])
        first_d = dram("first_d", [NT, P])
        xd_d = dram("xd_d", [NS, F])
        hT_d = dram("hT_d", [NG, P, GS])

        def rows(t, side):
            return t[side * NS:(side + 1) * NS, :].rearrange("(g j p) f -> g p j f", j=J, p=P)

        ident = sb("ident", [P, P])
        tri = sb("tri", [P, P])
        one = sb("one", [1, 1])
        mhalf = sb("mhalf", [P, P])
        W12 = sb("W12", [P, P])
        c_bc = sb("c_bc", [P, P])
        b2_bc = sb("b2_bc", [P, P])
        cb2_bc = sb("cb2_bc", [P, P])
        whT = sb("whT", [P, 3 * P])
        wiT = sb("wiT", [P, 3 * P])
        wlT = sb("wlT", [P, LEVELS, 3 * P])
        b3 = sb("b3", [P, 2, 3])
        brz = sb("brz", [P, 2])
        W1s = sb("W1s", [P, HID])
        W2s = sb("W2s", [P, 2, P])
        W1T = sb("W1T", [P, 2, P])
        b1c = sb("b1c", [P, 2])
        b1f = sb("b1f", [P, 2, P])
        wih_s = sb("wih_s", [P, 3, P])
        whh_s = sb("whh_s", [P, 3, P])
        gw_s = sb("gw_s", [P, LEVELS, P])
        gwT = sb("gwT", [P, LEVELS, P])

        dstR = sb("dstR", [NT, P], i32)
        prevR = sb("prevR", [NT, P], i32)
        nextR = sb("nextR", [NT, P], i32)
        srcR = sb("srcR", [NT, P], i32)
        eR = sb("eR", [NT, P], i32)
        dstF = sb("dstF", [NT, P])
        prevF = sb("prevF", [NT, P])
        nextF = sb("nextF", [NT, P])
        srcF = sb("srcF", [NT, P])
        eF = sb("eF", [NT, P])
        startF = sb("startF", [NT, P])
        runF = sb("runF", [NT, P])
        carF = sb("carF", [1, NT + 1])
        firstF = sb("firstF", [NT, P])
        dinvF = sb("dinvF", [NT, P])
        scatF = sb("scatF", [NT, P])
        ecI = sb("ecI", [P, NT], i32)
        ecol = sb("ecol", [P, NT])
        t0I = sb("t0I", [P, NT], i32)
        t0col = sb("t0col", [P, NT])
        srcI = sb("srcI", [P, NT], i32)
        dstI = sb("dstI", [P, NT], i32)
        scatI = sb("scatI", [P, NT], i32)
        dstC = sb("dstC", [P, NT])
        dinvD = sb("dinvD", [P, NT])
        recrow = sb("recrow", [P, NT, 2])
        recS = sb("recS", [P, NT, 2])
        isd = sb("isd", [P, NT])
        mv = sb("mv", [P, NT])
        idxF = sb("idxF", [P, NT])
        idxI = sb("idxI", [P, NT], i32)
        recfill = sb("recfill", [DP, N // DP, 2])
        S = sb("S", [P, NS])
        FL = sb("FL", [P, NS], bf16)

        W = [GS, DW]
        rS = [sb(f"rS{i}", [P, W[i]]) for i in range(2)]
        zS = [sb(f"zS{i}", [P, W[i]]) for i in range(2)]
        tS = [sb(f"tS{i}", [P, W[i]]) for i in range(2)]
        nS = [sb(f"nS{i}", [P, W[i]]) for i in range(2)]
        dS = [sb(f"dS{i}", [P, W[i]]) for i in range(2)]
        hA = sb("hA", [P, GS])
        hB = sb("hB", [P, GS])
        h1 = sb("h1", [P, DW])
        x1T = sb("x1T", [P, DW])
        uT = sb("uT", [P, DW])
        xr1 = sb("xr1", [DP, J, P])
        xT1 = sb("xT1", [P, DW])
        z1 = sb("z1", [DP, J, P])
        xn1 = sb("xn1", [DP, J, P])
        o1 = sb("o1", [DP, J, P])
        xs = sb("xs", [P, J, P])
        xd = sb("xd", [P, J, P])
        xsT = sb("xsT", [P, GS])
        msg = sb("msg", [P, J, P])
        xdd = sb("xdd", [P, J, P])
        aggS = sb("aggS", [P, GS])
        zrow = sb("zrow", [P, J, P])
        zD = sb("zD", [P, J, P])
        z0 = sb("z0", [P, J, P])
        xn0 = sb("xn0", [P, J, P])
        stg = sb("stg", [P, J, P])
        idxa = sb("idxa", [P, J], i32)
        idxb = sb("idxb", [P, J], i32)
        idxr = sb("idxr", [P, NT // ((LEAD - 1) // 2)], i32)
        rowr = sb("rowr", [P, NT // ((LEAD - 1) // 2), 2])
        zDr = sb("zDr", [P, J, P])
        xdr = sb("xdr", [P, J, P])

        def lnbuf(tag, p):
            return {"st": sb("st" + tag, [p, J, 6]), "ag": sb("ag" + tag, [p, J, 2]),
                    "rs": sb("rs" + tag, [p, J]), "nm": sb("nm" + tag, [p, J])}

        lnb = {"pre1": lnbuf("pre1", DP), "fin1": lnbuf("fin1", DP), "lane0": lnbuf("lane0", P)}

        def bank(name):
            return ctx.enter_context(nc.psum_tensor(name, [P, 512], f32))

        pR = [bank("pR0"), bank("pR1")]
        pN = [bank("pN0"), bank("pN1")]
        pZ = [bank("pZ0"), bank("pZ1")]
        pM = [bank("pM0"), bank("pM1")]

        s_const = sem("s_const")
        s_wload = sem("s_wload")
        s_pads = sem("s_pads")
        s_eload = sem("s_eload")
        s_prep_pe = sem("s_prep_pe")
        s_prep_cp = sem("s_prep_cp")
        s_wready = sem("s_wready")
        s_chain = sem("s_chain")
        s_col_pe = sem("s_col_pe")
        s_car_pe = sem("s_car_pe")
        s_deg = sem("s_deg")
        s_first = sem("s_first")
        s_firstst = sem("s_firstst")
        s_firstld = sem("s_firstld")
        s_S = sem("s_S")
        s_cols = sem("s_cols")
        s_recinit = sem("s_recinit")
        s_recg = sem("s_recg")
        s_rcopy = sem("s_rcopy")
        s_recS = sem("s_recS")
        s_idx = sem("s_idx")

        names = ["r_filled", "n_filled", "z_filled", "r_ready", "z_ready", "t_ready", "tanh_ready",
                 "diff_ready", "gated_ready", "h_ready", "m_filled"]
        L = [{n: sem(f"{n}{i}") for n in names} for i in range(2)]
        lns = {t: [sem(f"ln_{w}_{t}") for w in ("stats", "aggr", "rstd", "nmr", "out")] for t in lnb}
        s_x1load = sem("s_x1load")
        s_xT1 = sem("s_xT1")
        s_z1 = sem("s_z1")
        s_sig1 = sem("s_sig1")
        s_u1 = sem("s_u1")
        s_x1T = sem("s_x1T")
        s_uT = sem("s_uT")
        s_store1 = sem("s_store1")
        s_idxc = sem("s_idxc")
        s_gs = sem("s_gs")
        s_gd = sem("s_gd")
        s_scaled = sem("s_scaled")
        s_carry = sem("s_carry")
        s_carried = sem("s_carried")
        s_xsT = sem("s_xsT")
        s_self = sem("s_self")
        s_zs = sem("s_zs")
        s_zd = sem("s_zd")
        s_zpre = sem("s_zpre")
        s_zb = sem("s_zb")
        s_sig0 = sem("s_sig0")
        s_u0 = sem("s_u0")
        s_h0 = sem("s_h0")
        s_stg = sem("s_stg")
        st_zs = sem("st_zs")
        st_zd = sem("st_zd")
        st_xd = sem("st_xd")
        st_xn = sem("st_xn")
        st_stg = sem("st_stg")
        st_h = sem("st_h")
        s_ldz = sem("s_ldz")
        s_ldx = sem("s_ldx")
        s_ldh = sem("s_ldh")
        s_in = sem("s_in")
        s_fin = sem("s_fin")
        s_fout = sem("s_fout")
        s_scat = sem("s_scat")

        SU, GU, LU = 9, 3, 3
        M_G = SU * NG
        M_L = M_G + GU * NG
        GRU_L = 3 * NG
        LN_G = NG
        LN_L = 2 * NG

        from_one = [s_zpre, s_fin, s_u0, s_scaled, s_stg, s_store1, s_carried, s_carry,
                    st_xd, st_xn, st_stg, st_h, st_zs, st_zd]
        from_one += [L[i][n] for i in range(2) for n in names if n.endswith("_ready") or n == "m_filled"
                     if n not in ("tanh_ready", "diff_ready")]
        from_one += [lns[t][4] for t in lnb]

        turns = {"sp": sem("s_turn_sp"), "pool": sem("s_turn_pool"), "dve": sem("s_turn_dve")}

        def settle(eng, name):
            eng.sem_inc(turns[name], 1)

        block = ctx.enter_context(nc.Block())

        D_S = LEAD
        D_G = D_S + NG
        D_L = D_G + NG
        RL = (LEAD - 1) // 2
        RC = NT // RL
        RK = RC // 4
        assert LEAD == 1 + 2 * RL and NT == RL * 4 * RK

        def schedule(eng, p):
            def dense(d, k, between=None, first=False, last=False):
                p.a1(d, k)
                if between is not None:
                    between()
                p.b1(d, k)
                if k == 0 and not first:
                    p.fin(d - 1)
                if not last:
                    if k == 0:
                        p.load(d + 1)
                    if k == 1:
                        p.xt(d + 1)
                    if k == 2:
                        p.z(d + 1)
                if k == 3:
                    p.u(d)
                    if not last:
                        p.x1(d + 1)

            p.prep_weights()
            p.load1(0)
            p.xt(0)
            p.z(0)
            p.x1(0)
            for k in range(4):
                dense(0, k, first=True)
            p.prep_edges()
            with eng.Fori(0, RL) as c:
                for k in range(4):
                    p.rec_scatter(c, k)
                    dense(c + 1, k)
            p.rec_all()
            with eng.Fori(0, RL) as c:
                for k in range(4):
                    p.rec_gather(c, k)
                    dense(c + (1 + RL), k)
                p.build_s(c)
            p.prep_edges2()

            p.sg(0)
            for st in (p.st0, p.st1, p.st2, p.st3):
                st(0)
            p.sg(1)

            def s_step(i, stage=True, gather=True):
                d = i + D_S
                dense(d, 0)
                p.a0s(i, 0)
                if stage:
                    p.st0(i + 1)
                dense(d, 1, lambda: p.b0s(i, 0))
                p.t0s(i, 0)
                p.a0s(i, 1)
                if stage:
                    p.st1(i + 1)
                dense(d, 2, lambda: p.b0s(i, 1))
                p.t0s(i, 1)
                p.a0s(i, 2)
                if stage:
                    p.st2(i + 1)
                if gather:
                    p.sg(i + 2)
                dense(d, 3, lambda: p.b0s(i, 2))
                p.t0s(i, 2)
                if stage:
                    p.st3(i + 1)

            with eng.Fori(0, NG - 2) as i:
                s_step(i)
            s_step(NG - 2, gather=False)
            p.gg(0)
            s_step(NG - 1, stage=False, gather=False)

            def g_step(i, gather=True):
                d = i + D_G
                dense(d, 0)
                p.g0(i)
                if gather:
                    p.gg(i + 1)
                dense(d, 1)
                p.g1(i)
                dense(d, 2)
                p.g2(i)
                dense(d, 3)
                p.g3(i)

            with eng.Fori(0, NG - 1) as i:
                g_step(i)
            g_step(NG - 1, gather=False)

            for l in range(LEVELS):
                p.lg(l, 0)
                p.ldh(l, 0)
                p.ldx(l, 0)
                p.sums0(l, 0)
                if l < LEVELS - 1:
                    dl = D_L + l * (PAIRS + 1)
                    with eng.Fori(0, PAIRS) as i:
                        d = i + dl
                        for h in range(2):
                            g = 2 * i + h
                            p.lg(l, g + 1)
                            dense(d, 2 * h)
                            p.a0(l, g)
                            dense(d, 2 * h + 1, lambda: p.b0(l, g))
                            p.ldh(l, g + 1)
                            p.t0(l, g)
                            p.sums0(l, g + 1)
                    d = dl + PAIRS
                    last = d == ND - 1
                    dense(d, 0, last=last)
                    p.a0(l, NG - 1)
                    dense(d, 1, lambda: p.b0(l, NG - 1), last=last)
                    p.t0(l, NG - 1)
                    dense(d, 2, last=last)
                    dense(d, 3, last=last)
                    if last:
                        p.fin(d)
                else:
                    with eng.Fori(0, NG - 1) as g:
                        p.a0(l, g)
                        p.lg(l, g + 1)
                        p.b0(l, g)
                        p.ldh(l, g + 1)
                        p.t0(l, g)
                        p.ldx(l, g + 1)
                        p.sums0(l, g + 1)
                    p.a0(l, NG - 1)
                    p.b0(l, NG - 1)
                    p.t0(l, NG - 1)

        class Pieces:
            def nothing(self, *a):
                pass
            prep_weights = prep_edges = prep_edges2 = build_s = rec_scatter = rec_all = rec_gather = nothing
            load1 = load = xt = z = x1 = a1 = b1 = fin = u = nothing
            sg = st0 = st1 = st2 = st3 = a0s = b0s = t0s = gg = g0 = g1 = g2 = g3 = nothing
            lg = ldh = ldx = sums0 = a0 = b0 = t0 = nothing

        def m1(what, d):
            if isinstance(d, int) and d == 0 and what != "fin":
                return {"xt": 0, "z": 1, "x1": 2}[what]
            if isinstance(d, int) and d == ND - 1 and what == "fin":
                return 4 * d + 3
            return 4 * d + {"xt": -1, "z": 0, "x1": 1, "fin": 6}[what]

        def m0s(what, e):
            if isinstance(e, int) and e == 0:
                return ("xs", "sums", "z", "xdd", "zd", "xn").index(what)
            return SU * e - 3 + {"xs": 0, "sums": 1, "z": 3, "xdd": 5, "zd": 7, "xn": 8}[what]

        def m0t(i, k):
            if isinstance(i, int) and i == NG - 1:
                return SU * i + 6 + k
            return SU * i + 8 + 2 * k

        @block.sync
        def _(sp):
            class Sync(Pieces):
                def prep_weights(self):
                    for s in from_one:
                        sp.sem_inc(s, 1)
                    sp.dma_start(W1s[:, :], W1[:, :]).then_inc(s_wload, 16)
                    sp.dma_start(W2s[:, :, :], W2.rearrange("(c p) f -> p c f", p=P)).then_inc(s_wload, 16)
                    sp.dma_start(wih_s[:, :, :], w_ih.rearrange("(c p) f -> p c f", p=P)).then_inc(s_wload, 16)
                    sp.dma_start(whh_s[:, :, :], w_hh.rearrange("(c p) f -> p c f", p=P)).then_inc(s_wload, 16)
                    sp.dma_start(gw_s[:, :, :], gw.rearrange("l p f -> p l f")).then_inc(s_wload, 16)
                    with nc.allow_non_contiguous_dma(reason="bias columns, once"):
                        sp.dma_start(b1c[:, :], b1.rearrange("(c p) -> p c", p=P)).then_inc(s_wload, 16)
                        sp.dma_start(b3[:, 0, :], b_ih.rearrange("(c p) -> p c", p=P)).then_inc(s_wload, 16)
                        sp.dma_start(b3[:, 1, :], b_hh.rearrange("(c p) -> p c", p=P)).then_inc(s_wload, 16)
                    sp.dma_start(b2_bc[:, :], b2.rearrange("(a f) -> a f", a=1).broadcast_to([P, P])).then_inc(s_wload, 16)

                def load1(self, d):
                    sp.dma_start(xr1[:, :, :].rearrange("p j f -> p (j f)"), x_g[d]).then_inc(s_x1load, 16)
                    sp.wait_ge(s_pads, 1)
                    for t, a in ((dstR, dst), (srcR, src)):
                        sp.dma_start(t[0:FULL, :], a[0:FULL * P].rearrange("(t p) -> t p", p=P)).then_inc(s_eload, 16)
                        sp.dma_start(t[FULL:FULL + 1, 0:REST], a[FULL * P:E].rearrange("(t p) -> t p", t=1)).then_inc(s_eload, 16)
                    sp.dma_start(nextR[0:FULL, :], dst[1:FULL * P + 1].rearrange("(t p) -> t p", p=P)).then_inc(s_eload, 16)
                    sp.dma_start(nextR[FULL:FULL + 1, 0:REST - 1], dst[FULL * P + 1:E].rearrange("(t p) -> t p", t=1)).then_inc(s_eload, 16)
                    sp.dma_start(prevR[0:1, 1:P], dst[0:P - 1].rearrange("(t p) -> t p", t=1)).then_inc(s_eload, 16)
                    sp.dma_start(prevR[1:FULL, :], dst[P - 1:FULL * P - 1].rearrange("(t p) -> t p", p=P)).then_inc(s_eload, 16)
                    sp.dma_start(prevR[FULL:FULL + 1, 0:REST + 1], dst[FULL * P - 1:E].rearrange("(t p) -> t p", t=1)).then_inc(s_eload, 16)
                    sp.dma_start(rec[:, :].rearrange("(p n) c -> p (n c)", p=DP),
                                 recfill[:, :, :].rearrange("p n c -> p (n c)")).then_inc(s_recinit, 16)

                def load(self, d):
                    sp.wait_ge(s_u1, d)
                    settle(sp, "sp")
                    sp.dma_start(xr1[:, :, :].rearrange("p j f -> p (j f)"), x_g[d]).then_inc(s_x1load, 16)

                def fin(self, d):
                    sp.wait_ge(lns["fin1"][4], 1 + d + 1)
                    settle(sp, "sp")
                    sp.dma_start(out_g[d], o1[:, :, :].rearrange("p j f -> p (j f)")).then_inc(s_store1, 16)

                def prep_edges(self):
                    sp.wait_ge(s_first, 1)
                    sp.dma_start(first_d[:, :], firstF[:, :]).then_inc(s_firstst, 16)
                    sp.wait_ge(s_firstst, 16)
                    sp.dma_start(S[:, :], first_d[:, :].rearrange("(a t) p -> a (t p)", a=1).broadcast_to([P, NS]),
                                 max_dma_last_dim=NS).then_inc(s_firstld, 16)

                def st0(self, e):
                    sp.wait_ge(s_gd, 64 * e + 64)
                    settle(sp, "sp")
                    sp.dma_start(xd_d[:, :].rearrange("(g j p) f -> g p j f", j=J, p=P)[e], xd[:, :, :]).then_inc(st_xd, 16)

                def st1(self, e):
                    sp.wait_ge(s_zs, e + 1)
                    settle(sp, "sp")
                    sp.dma_start(rows(tz, 0)[e], zrow[:, :, :]).then_inc(st_zs, 16)

                def st3(self, e):
                    sp.wait_ge(s_zd, e + 1)
                    settle(sp, "sp")
                    sp.dma_start(rows(tz, 1)[e], zD[:, :, :]).then_inc(st_zd, 16)
                    sp.wait_ge(lns["lane0"][4], 1 + e + 1)
                    settle(sp, "sp")
                    sp.dma_start(rows(tx[0], 0)[e], xn0[:, :, :]).then_inc(st_xn, 16)

                def t0s(self, i, k):
                    sp.wait_ge(s_stg, 1 + 3 * i + k + 1)
                    settle(sp, "sp")
                    sp.dma_start(rows(tx[k + 1], 0)[i], stg[:, :, :]).then_inc(st_stg, 16)

                def gg(self, i):
                    sp.wait_ge(st_zd, 1 + 16 * NG)
                    sp.wait_ge(st_xd, 1 + 16 * NG)
                    sp.wait_ge(s_zpre, 1 + i)
                    settle(sp, "sp")
                    sp.dma_start(zDr[:, :, :], rows(tz, 1)[i]).then_inc(s_ldz, 16)
                    if not isinstance(i, int):
                        sp.wait_ge(s_u0, 1 + i + NG)
                        settle(sp, "sp")
                    elif i:
                        sp.wait_ge(s_u0, 1 + i + NG)
                    sp.dma_start(xdr[:, :, :], xd_d[:, :].rearrange("(g j p) f -> g p j f", j=J, p=P)[i]).then_inc(s_ldx, 16)

                def g3(self, i):
                    sp.wait_ge(lns["lane0"][4], 1 + LN_G + i + 1)
                    settle(sp, "sp")
                    sp.dma_start(rows(tx[0], 1)[i], xn0[:, :, :]).then_inc(st_xn, 16)
                    sp.wait_ge(s_h0, NG + i + 1)
                    settle(sp, "sp")
                    sp.dma_start(hT_d[i], hA[:, :]).then_inc(st_h, 16)

                def ldh(self, l, g):
                    q = l * NG + g
                    sp.wait_ge(st_h, 1 + 16 * NG * (l + 1))
                    sp.wait_ge(L[0]["h_ready"], 1 + GRU_L + q)
                    settle(sp, "sp")
                    sp.dma_start(hA[:, :], hT_d[g]).then_inc(s_ldh, 16)

                def ldx(self, l, g):
                    if l == LEVELS - 1:
                        sp.wait_ge(s_fin, 1 + g)
                        settle(sp, "sp")
                        sp.dma_start(xdr[:, :, :], rows(tx[0], 1)[g]).then_inc(s_ldx, 16)

                def t0(self, l, g):
                    q = l * NG + g
                    if l < LEVELS - 1:
                        sp.wait_ge(L[0]["h_ready"], 1 + GRU_L + q + 1)
                        settle(sp, "sp")
                        sp.dma_start(hT_d[g], hB[:, :]).then_inc(st_h, 16)
                        sp.wait_ge(s_stg, 1 + 3 * NG + q + 1)
                        settle(sp, "sp")
                        sp.dma_start(rows(tx[l + 1], 1)[g], stg[:, :, :]).then_inc(st_stg, 16)

            schedule(sp, Sync())
            sp.wait_ge(s_store1, 1 + 16 * ND)
            sp.wait_ge(s_scat, 2 * 16 * NT)

        @block.gpsimd
        def _(pool):
            def gather(buf, table, ix, done):
                for j in range(J):
                    nc.gpsimd.indirect_dma_start(
                        out=buf[:, j, :], out_offset=None, in_=table,
                        in_offset=bass.IndirectOffsetOnAxis(ap=ix[:, j:j + 1], axis=0)).then_inc(done, 16)

            def rstd(tag, n):
                b, s = lnb[tag], lns[tag]
                pool.wait_ge(s[1], n + 1)
                settle(pool, "pool")
                nc.gpsimd.tensor_scalar(b["nm"][:, :], b["ag"][:, :, 0], -1.0, None, ALU.mult)
                nc.gpsimd.tensor_scalar(b["rs"][:, :], b["ag"][:, :, 1], EPS, None, ALU.add).then_inc(s[2], 1)
                pool.wait_ge(s[2], 2 * n + 1)
                settle(pool, "pool")
                nc.gpsimd.tensor_tensor(b["rs"][:, :], b["rs"][:, :], mhalf[0:b["rs"].shape[0], 0:J], ALU.pow).then_inc(s[2], 1)
                pool.wait_ge(s[2], 2 * n + 2)
                settle(pool, "pool")
                nc.gpsimd.tensor_tensor(b["nm"][:, :], b["nm"][:, :], b["rs"][:, :], ALU.mult).then_inc(s[3], 1)

            class Pool(Pieces):
                def z(self, d):
                    rstd("pre1", d)

                def fin(self, d):
                    rstd("fin1", d)

                def st2(self, e):
                    rstd("lane0", e)

                def g2(self, i):
                    rstd("lane0", LN_G + i)

                def prep_weights(self):
                    nc.gpsimd.memset(mhalf[:, :], -0.5)
                    nc.gpsimd.memset(ident[:, :], 0.0)
                    nc.gpsimd.memset(tri[:, :], 1.0)
                    nc.gpsimd.iota(eR[:, :], pattern=[[1, P]], base=0, channel_multiplier=P)
                    nc.gpsimd.iota(ecI[:, :], pattern=[[P, NT]], base=0, channel_multiplier=1)
                    nc.gpsimd.iota(t0I[:, :], pattern=[[P, NT]], base=0, channel_multiplier=0).then_inc(s_const, 1)
                    pool.wait_ge(s_const, 1)
                    nc.gpsimd.affine_select(out=ident[:, :], in_=ident[:, :], compare_op=ALU.not_equal, fill=1.0,
                                            base=0, pattern=[[-1, P]], channel_multiplier=1)
                    nc.gpsimd.affine_select(out=tri[:, :], in_=tri[:, :], compare_op=ALU.is_ge, fill=0.0,
                                            base=0, pattern=[[1, P]], channel_multiplier=-1).then_inc(s_const, 1)

                def prep_edges(self):
                    pool.wait_ge(s_deg, 1)
                    nc.gpsimd.tensor_tensor(dinvF[:, :], dinvF[:, :], mhalf[0:NT, :], ALU.pow).then_inc(s_deg, 1)
                    pool.wait_ge(s_cols, 1)
                    pool.wait_ge(s_recinit, 16)

                def rec_scatter(self, c, k):
                    if k == 0:
                        nc.gpsimd.tensor_copy(idxr[:, :], scatI[:, bass.ds(c * RC, RC)])
                        nc.gpsimd.tensor_copy(rowr[:, :, :], recrow[:, bass.ds(c * RC, RC), :]).then_inc(s_rcopy, 1)
                        pool.wait_ge(s_rcopy, c + 1)
                        settle(pool, "pool")
                    for t in range(k * RK, (k + 1) * RK):
                        nc.gpsimd.indirect_dma_start(
                            out=rec[:, :], out_offset=bass.IndirectOffsetOnAxis(ap=idxr[:, t:t + 1], axis=0),
                            in_=rowr[:, t, :], in_offset=None, bounds_check=N - 1,
                            oob_is_err=False).then_inc(s_scat, 16)
                    if k == 3:
                        pool.wait_ge(s_scat, 16 * RC * (c + 1))
                        settle(pool, "pool")

                def rec_all(self):
                    pool.wait_ge(s_scat, 16 * NT)

                def rec_gather(self, c, k):
                    if k == 0:
                        nc.gpsimd.tensor_copy(idxr[:, :], srcI[:, bass.ds(c * RC, RC)]).then_inc(s_rcopy, 1)
                        pool.wait_ge(s_rcopy, RL + c + 1)
                        settle(pool, "pool")
                    for t in range(k * RK, (k + 1) * RK):
                        nc.gpsimd.indirect_dma_start(
                            out=rowr[:, t, :], out_offset=None, in_=rec[:, :],
                            in_offset=bass.IndirectOffsetOnAxis(ap=idxr[:, t:t + 1], axis=0)).then_inc(s_recg, 16)
                    if k == 3:
                        pool.wait_ge(s_recg, 16 * RC * (c + 1))
                        settle(pool, "pool")
                        nc.gpsimd.tensor_copy(recS[:, bass.ds(c * RC, RC), :], rowr[:, :, :]).then_inc(s_recS, 1)

                def sg(self, e):
                    pool.wait_ge(s_scaled, 1 + 2 * e)
                    pool.wait_ge(s_u0, 1 + e)
                    pool.wait_ge(st_xd, 1 + 16 * e)
                    settle(pool, "pool")
                    nc.gpsimd.tensor_copy(idxa[:, :], srcI[:, bass.ds(e * J, J)]).then_inc(s_idxc, 1)
                    nc.gpsimd.tensor_copy(idxb[:, :], dstI[:, bass.ds(e * J, J)]).then_inc(s_idxc, 1)
                    pool.wait_ge(s_idxc, 2 * e + 2)
                    settle(pool, "pool")
                    gather(xs, x[:, :], idxa, s_gs)
                    gather(xd, x[:, :], idxb, s_gd)

                def gg(self, i):
                    pool.wait_ge(s_idx, 1)
                    pool.wait_ge(s_scaled, 1 + 2 * NG + i)
                    pool.wait_ge(s_u0, 1 + NG)
                    nc.gpsimd.tensor_copy(idxa[:, :], idxI[:, bass.ds(i * J, J)]).then_inc(s_idxc, 1)
                    pool.wait_ge(st_zs, 1 + 16 * NG)
                    pool.wait_ge(st_zd, 1 + 16 * NG)
                    pool.wait_ge(s_idxc, 2 * NG + i + 1)
                    settle(pool, "pool")
                    gather(xs, tz[:, :], idxa, s_gs)

                def lg(self, l, g):
                    q = l * NG + g
                    pool.wait_ge(s_gs, 64 * (2 * NG + q))
                    pool.wait_ge(s_scaled, 1 + 3 * NG)
                    pool.wait_ge(L[0]["m_filled"], 1 + M_L + LU * q - 2)
                    nc.gpsimd.tensor_copy(idxa[:, :], idxI[:, bass.ds(g * J, J)]).then_inc(s_idxc, 1)
                    pool.wait_ge(st_xn, 1 + 16 * 2 * NG)
                    pool.wait_ge(st_stg, 1 + 16 * NG * (3 + l))
                    pool.wait_ge(s_idxc, 3 * NG + q + (g - 1 if l == LEVELS - 1 and not (isinstance(g, int) and g == 0) else 0) + 1)
                    settle(pool, "pool")
                    gather(xs, tx[l][:, :], idxa, s_gs)

                def t0(self, l, g):
                    if l == LEVELS - 1:
                        rstd("lane0", LN_L + g)
                        pool.wait_ge(s_scat, 16 * NT + 16 * J * g)
                        nc.gpsimd.tensor_copy(idxb[:, :], scatI[:, bass.ds(g * J, J)]).then_inc(s_idxc, 1)
                        pool.wait_ge(s_idxc, 3 * NG + l * NG + 2 * g + 2 + (0 if isinstance(g, int) and g == NG - 1 else 1))
                        pool.wait_ge(s_store1, 1 + 16 * ND)
                        pool.wait_ge(lns["lane0"][4], 1 + LN_L + g + 1)
                        settle(pool, "pool")
                        for j in range(J):
                            nc.gpsimd.indirect_dma_start(
                                out=out[:, :], out_offset=bass.IndirectOffsetOnAxis(ap=idxb[:, j:j + 1], axis=0),
                                in_=xn0[:, j, :], in_offset=None, bounds_check=N - 1,
                                oob_is_err=False).then_inc(s_scat, 16)

            schedule(pool, Pool())

        @block.tensor
        def _(pe):
            def transposes(lane, source, p):
                bank = pM[lane]
                for j in range(J):
                    last = nc.tensor.transpose(bank[:, j * p:(j + 1) * p], source[:, j, :], ident[0:p, 0:p])
                last.then_inc(L[lane]["m_filled"], 1)

            def back(lane, source, p):
                bank = pM[lane]
                for j in range(J):
                    last = nc.tensor.transpose(bank[0:p, j * P:(j + 1) * P], source[:, j * p:(j + 1) * p], ident[:, :])
                last.then_inc(L[lane]["m_filled"], 1)

            def gates(lane, n, h, agg=None, l=None):
                s, w = L[lane], W[lane]
                pe.wait_ge(s["r_ready"], 1 + n)
                nc_mm = nc.tensor.matmul
                last = nc_mm(pR[lane][:, 0:w], whT[:, 0:P], h, start=True, stop=agg is None)
                if agg is not None:
                    last = nc_mm(pR[lane][:, 0:w], wlT[:, l, 0:P], agg, start=False, stop=True)
                last.then_inc(s["r_filled"], 1)
                pe.wait_ge(s["t_ready"], 1 + n)
                nc_mm(pN[lane][:, 0:w], whT[:, 2 * P:3 * P], h, start=True, stop=True).then_inc(s["n_filled"], 1)
                if agg is not None:
                    nc_mm(pM[lane][:, 0:w], wlT[:, l, 2 * P:3 * P], agg, start=True, stop=True).then_inc(s["m_filled"], 1)
                pe.wait_ge(s["z_ready"], 1 + n)
                last = nc_mm(pZ[lane][:, 0:w], whT[:, P:2 * P], h, start=True, stop=agg is None)
                if agg is not None:
                    last = nc_mm(pZ[lane][:, 0:w], wlT[:, l, P:2 * P], agg, start=False, stop=True)
                last.then_inc(s["z_filled"], 1)

            def sums(i, source):
                for j in range(J):
                    last = nc.tensor.matmul(pM[0][:, j * P:(j + 1) * P], source[:, j, :],
                                            S[:, bass.ds((i * J + j) * P, P)], start=True, stop=True)
                last.then_inc(L[0]["m_filled"], 1)

            class Tensor(Pieces):
                def prep_weights(self):
                    pe.wait_ge(s_const, 2)
                    pe.wait_ge(s_wload, 16 * 9)
                    for c in range(2):
                        last = nc.tensor.transpose(pR[0][:, c * P:(c + 1) * P], W1s[:, c * P:(c + 1) * P], ident[:, :])
                    for c in range(3):
                        last = nc.tensor.transpose(pN[0][:, c * P:(c + 1) * P], wih_s[:, c, :], ident[:, :])
                    for c in range(3):
                        last = nc.tensor.transpose(pZ[0][:, c * P:(c + 1) * P], whh_s[:, c, :], ident[:, :])
                    for c in range(LEVELS):
                        last = nc.tensor.transpose(pM[0][:, c * P:(c + 1) * P], gw_s[:, c, :], ident[:, :])
                    last.then_inc(s_prep_pe, 1)
                    pe.wait_ge(s_prep_cp, 1)
                    for c in range(2):
                        nc.tensor.matmul(pR[1][:, 0:P], W1T[:, c, :], W2s[:, c, :], start=c == 0, stop=c == 1)
                    for c in range(2):
                        nc.tensor.matmul(pN[1][:, 0:P], b1f[:, c, :], W2s[:, c, :], start=c == 0, stop=c == 1)
                    for l, b in enumerate((pZ[1], pM[1], pR[0], pN[0])):
                        last = nc.tensor.matmul(b[:, 0:3 * P], gwT[:, l, :], wiT[:, :], start=True, stop=True)
                    last.then_inc(s_prep_pe, 1)
                    pe.wait_ge(s_wready, 1)

                def prep_edges(self):
                    pe.wait_ge(s_car_pe, 1)
                    nc.tensor.matmul(pR[0][0:1, 0:NT], runF[:, P - 1:P], ident[0:NT, 0:NT], start=True, stop=True).then_inc(s_car_pe, 1)
                    pe.wait_ge(s_car_pe, 3)
                    nc.tensor.matmul(pN[0][0:NT, 0:1], carF[0:1, 0:NT], one[0:1, 0:1], start=True, stop=True).then_inc(s_car_pe, 1)
                    pe.wait_ge(s_col_pe, 1)
                    pe.wait_ge(s_deg, 2)
                    for c, t in enumerate((dstF, srcF, dinvF, scatF)):
                        last = nc.tensor.transpose(pZ[0][:, c * NT:(c + 1) * NT], t[:, :], ident[0:NT, 0:NT])
                    last.then_inc(s_col_pe, 1)

                def a1(self, d, k):
                    if k == 0:
                        pe.wait_ge(s_x1T, d + 1)
                    else:
                        pe.wait_ge(L[1]["h_ready"], 1 + 4 * d + k)
                    gates(1, 4 * d + k, x1T[:, :] if k == 0 else h1[:, :])

                def xt(self, d):
                    pe.wait_ge(s_x1load, 16 * d + 16)
                    if isinstance(d, int) and d == 1:
                        pe.wait_ge(s_x1T, 1)
                    elif not isinstance(d, int) or d > 1:
                        pe.wait_ge(lns["fin1"][4], 1 + d - 1)
                    transposes(1, xr1, DP)

                def z(self, d):
                    pe.wait_ge(s_xT1, d + 1)
                    for j in range(J):
                        last = nc.tensor.matmul(pM[1][0:DP, j * P:(j + 1) * P], xT1[:, j * DP:(j + 1) * DP], W12[:, :],
                                                start=True, stop=True)
                    last.then_inc(L[1]["m_filled"], 1)

                def x1(self, d):
                    pe.wait_ge(lns["pre1"][4], 1 + d + 1)
                    pe.wait_ge(s_z1, d + 1)
                    transposes(1, xn1, DP)

                def fin(self, d):
                    pe.wait_ge(s_uT, d + 1)
                    if isinstance(d, int) and d == ND - 1:
                        pe.wait_ge(lns["fin1"][4], 1 + d)
                    else:
                        pe.wait_ge(s_x1T, d + 2)
                    back(1, uT, DP)

                def st0(self, e):
                    pe.wait_ge(s_gs, 64 * e + 64)
                    pe.wait_ge(s_h0, e)
                    transposes(0, xs, P)
                    pe.wait_ge(s_scaled, 1 + 2 * e + 1)
                    pe.wait_ge(s_S, NT)
                    pe.wait_ge(s_xsT, e + 1)
                    sums(e, msg)

                def rows_by(self, left):
                    for j in range(J):
                        last = nc.tensor.matmul(pM[0][:, j * P:(j + 1) * P], left[:, j * P:(j + 1) * P], W12[:, :],
                                                start=True, stop=True)
                    last.then_inc(L[0]["m_filled"], 1)

                def st1(self, e):
                    pe.wait_ge(s_xsT, e + 1)
                    pe.wait_ge(s_carry, 1 + J * (e + 1))
                    if not (isinstance(e, int) and e == 0):
                        pe.wait_ge(s_stg, 1 + 3 * e - 2)
                    self.rows_by(xsT)

                def st2(self, e):
                    pe.wait_ge(s_scaled, 1 + 2 * e + 2)
                    pe.wait_ge(s_zs, e + 1)
                    if not (isinstance(e, int) and e == 0):
                        pe.wait_ge(s_stg, 1 + 3 * e - 1)
                    transposes(0, xdd, P)

                def st3(self, e):
                    pe.wait_ge(s_self, e + 1)
                    if not (isinstance(e, int) and e == 0):
                        pe.wait_ge(s_stg, 1 + 3 * e)
                    self.rows_by(aggS)
                    pe.wait_ge(lns["lane0"][4], 1 + e + 1)
                    pe.wait_ge(s_zd, e + 1)
                    transposes(0, xn0, P)

                def a0s(self, i, k):
                    if k == 0:
                        pe.wait_ge(s_h0, i + 1)
                    else:
                        pe.wait_ge(L[0]["h_ready"], 1 + 3 * i + k)
                    gates(0, 3 * i + k, hA[:, :] if k == 0 else hB[:, :])

                def t0s(self, i, k):
                    pe.wait_ge(L[0]["h_ready"], 1 + 3 * i + k + 1)
                    if isinstance(i, int) and i == NG - 1:
                        pe.wait_ge(s_h0, NG)
                        pe.wait_ge(s_stg, 1 + 3 * i + k)
                    elif k == 0:
                        pe.wait_ge(s_carry, 1 + J * (i + 2))
                    elif k == 1:
                        pe.wait_ge(s_zs, i + 2)
                    else:
                        pe.wait_ge(s_self, i + 2)
                    back(0, hB, P)

                def g0(self, i):
                    pe.wait_ge(s_scaled, 1 + 2 * NG + i + 1)
                    pe.wait_ge(s_stg, 1 + 3 * NG)
                    pe.wait_ge(s_h0, NG + i)
                    sums(i, msg)

                def g1(self, i):
                    pe.wait_ge(s_carry, 1 + J * (NG + i + 1))
                    back(0, aggS, P)

                def g3(self, i):
                    pe.wait_ge(lns["lane0"][4], 1 + LN_G + i + 1)
                    pe.wait_ge(s_zpre, 1 + i + 1)
                    transposes(0, xn0, P)

                def sums0(self, l, g):
                    q = l * NG + g
                    pe.wait_ge(s_gs, 64 * (2 * NG + q) + 64)
                    if l == LEVELS - 1:
                        pe.wait_ge(s_stg, 1 + 3 * NG + l * NG)
                        pe.wait_ge(s_fin, 1 + g)
                    else:
                        pe.wait_ge(s_h0, 2 * NG)
                        pe.wait_ge(s_stg, 1 + 3 * NG + q)
                    sums(g, xs)

                def a0(self, l, g):
                    q = l * NG + g
                    pe.wait_ge(s_ldh, 16 * q + 16)
                    pe.wait_ge(s_carry, 1 + J * (2 * NG + q + 1))
                    gates(0, GRU_L + q, hA[:, :], aggS[:, :], l)

                def t0(self, l, g):
                    q = l * NG + g
                    pe.wait_ge(L[0]["h_ready"], 1 + GRU_L + q + 1)
                    pe.wait_ge(s_in, q + 1)
                    back(0, hB, P)

            schedule(pe, Tensor())

        @block.scalar
        def _(act):
            def gate_acts(lane, n, added):
                s, w = L[lane], W[lane]
                act.wait_ge(s["r_filled"], n + 1)
                act.wait_ge(s["t_ready"], 1 + n)
                nc.scalar.activation(rS[lane][:, :], pR[lane][:, 0:w], ACT.Sigmoid, bias=brz[:, 0:1]).then_inc(s["r_ready"], 1)
                if added is None:
                    act.wait_ge(s["t_ready"], 1 + n + 1)
                else:
                    act.wait_ge(s_in, added)
                act.wait_ge(s["h_ready"], 1 + n)
                nc.scalar.activation(nS[lane][:, :], tS[lane][:, :], ACT.Tanh, bias=b3[:, 0, 2:3]).then_inc(s["tanh_ready"], 1)
                act.wait_ge(s["z_filled"], n + 1)
                act.wait_ge(s["gated_ready"], 1 + n)
                nc.scalar.activation(zS[lane][:, :], pZ[lane][:, 0:w], ACT.Sigmoid, bias=brz[:, 1:2]).then_inc(s["z_ready"], 1)

            def normalise(tag, n, source, dest, p, drained=None):
                b, s = lnb[tag], lns[tag]
                act.wait_ge(s[3], n + 1)
                for j in range(J):
                    last = nc.scalar.activation(dest[:, j, :], source(j), ACT.Identity,
                                                scale=b["rs"][:, j:j + 1], bias=b["nm"][:, j:j + 1])
                last.then_inc(s[4], 1)

            def copy_m(lane, use, dest, done):
                act.wait_ge(L[lane]["m_filled"], 1 + use + 1)
                nc.scalar.activation(dest, pM[lane][:, 0:W[lane]], ACT.Identity).then_inc(done, 1)

            class Scalar(Pieces):
                def a1(self, d, k):
                    gate_acts(1, 4 * d + k, None)

                def xt(self, d):
                    copy_m(1, m1("xt", d), xT1[:, :], s_xT1)

                def z(self, d):
                    act.wait_ge(s_z1, d + 1)
                    nc.scalar.activation(z1[:, :, :], z1[:, :, :], ACT.Sigmoid).then_inc(s_sig1, 1)

                def x1(self, d):
                    act.wait_ge(s_x1T, d)
                    normalise("pre1", d, lambda j: z1[:, j, :], xn1, DP)
                    act.wait_ge(s_uT, d)
                    copy_m(1, m1("x1", d), x1T[:, :], s_x1T)

                def fin(self, d):
                    act.wait_ge(s_store1, 1 + 16 * d)
                    normalise("fin1", d, lambda j: pM[1][0:DP, j * P:(j + 1) * P], o1, DP)

                def st0(self, e):
                    copy_m(0, m0s("xs", e), xsT[:, :], s_xsT)

                def st1(self, e):
                    act.wait_ge(s_zb, e + 1)
                    nc.scalar.activation(z0[:, :, :], z0[:, :, :], ACT.Sigmoid).then_inc(s_sig0, 1)

                def st3(self, e):
                    act.wait_ge(st_xn, 1 + 16 * e)
                    normalise("lane0", e, lambda j: z0[:, j, :], xn0, P)
                    if not (isinstance(e, int) and e == 0):
                        act.wait_ge(L[0]["h_ready"], 1 + 3 * e - 2)
                    copy_m(0, m0s("xn", e), hA[:, :], s_h0)

                def a0s(self, i, k):
                    gate_acts(0, 3 * i + k, None)

                def t0s(self, i, k):
                    act.wait_ge(st_stg, 1 + 16 * (3 * i + k))
                    copy_m(0, m0t(i, k), stg[:, :, :].rearrange("p j f -> p (j f)"), s_stg)

                def g1(self, i):
                    act.wait_ge(s_zb, NG + i + 1)
                    nc.scalar.activation(z0[:, :, :], z0[:, :, :], ACT.Sigmoid).then_inc(s_sig0, 1)

                def g3(self, i):
                    act.wait_ge(st_xn, 1 + 16 * (NG + i))
                    normalise("lane0", LN_G + i, lambda j: z0[:, j, :], xn0, P)
                    act.wait_ge(L[0]["h_ready"], 1 + 3 * NG)
                    act.wait_ge(st_h, 1 + 16 * i)
                    copy_m(0, M_G + GU * i + 2, hA[:, :], s_h0)

                def a0(self, l, g):
                    q = l * NG + g
                    gate_acts(0, GRU_L + q, q + 1)

                def t0(self, l, g):
                    q = l * NG + g
                    if l < LEVELS - 1:
                        act.wait_ge(st_stg, 1 + 16 * (3 * NG + q))
                        copy_m(0, M_L + LU * q + 2, stg[:, :, :].rearrange("p j f -> p (j f)"), s_stg)
                    else:
                        act.wait_ge(st_xn, 1 + 16 * 2 * NG)
                        act.wait_ge(s_scat, 16 * NT + 16 * J * g)
                        normalise("lane0", LN_L + g, lambda j: z0[:, j, :], xn0, P)

            schedule(act, Scalar())

        @block.vector
        def _(dve):
            V = nc.vector

            def gate_n(lane, n, use=None):
                s, w = L[lane], W[lane]
                dve.wait_ge(s["r_ready"], 1 + n + 1)
                dve.wait_ge(s["n_filled"], n + 1)
                V.scalar_tensor_tensor(out=tS[lane][:, :], in0=pN[lane][:, 0:w], scalar=b3[:, 1, 2:3], in1=rS[lane][:, :],
                                       op0=ALU.add, op1=ALU.mult).then_inc(s["t_ready"], 1)
                if use is not None:
                    dve.wait_ge(s["t_ready"], 1 + n + 1)
                    dve.wait_ge(s["m_filled"], 1 + use + 1)
                    V.tensor_tensor(tS[lane][:, :], tS[lane][:, :], pM[lane][:, 0:w], ALU.add).then_inc(s_in, 1)

            def state(lane, n, h, hout):
                s = L[lane]
                dve.wait_ge(s["tanh_ready"], n + 1)
                dve.wait_ge(s["h_ready"], 1 + n)
                V.tensor_tensor(dS[lane][:, :], h, nS[lane][:, :], ALU.subtract).then_inc(s["diff_ready"], 1)
                dve.wait_ge(s["diff_ready"], n + 1)
                dve.wait_ge(s["z_ready"], 1 + n + 1)
                V.tensor_tensor(dS[lane][:, :], dS[lane][:, :], zS[lane][:, :], ALU.mult).then_inc(s["gated_ready"], 1)
                dve.wait_ge(s["gated_ready"], 1 + n + 1)
                V.tensor_tensor(hout, dS[lane][:, :], nS[lane][:, :], ALU.add).then_inc(s["h_ready"], 1)

            def ln_stats(tag, n, source):
                b, s = lnb[tag], lns[tag]
                for j in range(J):
                    last = V.bn_stats(b["st"][:, j, :], source(j))
                last.then_inc(s[0], 1)
                dve.wait_ge(s[0], n + 1)
                dve.wait_ge(s[4], 1 + n)
                settle(dve, "dve")
                for j in range(J):
                    last = V.bn_aggr(b["ag"][:, j, :], b["st"][:, j, :])
                last.then_inc(s[1], 1)

            def carries(i, use, n):
                dve.wait_ge(L[0]["m_filled"], 1 + use + 1)
                for j in range(J):
                    dve.wait_ge(s_carry, 1 + J * n + j)
                    if j == 0:
                        dve.wait_ge(s_carried, 1 + n)
                    a = aggS[:, j * P:(j + 1) * P]
                    before = carry[:, 0:1] if j == 0 else aggS[:, j * P - 1:j * P]
                    V.scalar_tensor_tensor(out=a, in0=FL[:, bass.ds((i * J + j) * P, P)], scalar=before,
                                           in1=pM[0][:, j * P:(j + 1) * P], op0=ALU.mult, op1=ALU.add).then_inc(s_carry, 1)
                dve.wait_ge(s_carry, 1 + J * n + J)
                V.tensor_copy(carry[:, 0:1], aggS[:, GS - 1:GS]).then_inc(s_carried, 1)

            carry = ctx.enter_context(nc.sbuf_tensor("carry", [P, 1], f32))
            steps = [0]

            def chain(ins):
                steps[0] += 1
                ins.then_inc(s_chain, 1)
                dve.wait_ge(s_chain, steps[0])

            class Vector(Pieces):
                def prep_weights(self):
                    V.memset(dstR[:, :], N)
                    V.memset(prevR[:, :], N)
                    V.memset(nextR[:, :], N)
                    V.memset(srcR[:, :], 0)
                    V.memset(one[:, :], 1.0)
                    V.memset(carF[:, :], 0.0)
                    V.memset(carry[:, :], 0.0)
                    V.memset(recfill[:, :, 0], -1.0)
                    chain(V.memset(recfill[:, :, 1], 1.0))
                    V.memset(prevR[0:1, 0:1], -1).then_inc(s_pads, 1)
                    dve.wait_ge(s_wload, 16 * 9)
                    chain(V.tensor_tensor(brz[:, 0:2], b3[:, 0, 0:2], b3[:, 1, 0:2], ALU.add))
                    V.tensor_copy(b1f[:, 0, :], b1c[:, 0:1].broadcast_to([P, P]))
                    V.tensor_copy(b1f[:, 1, :], b1c[:, 1:2].broadcast_to([P, P]))
                    dve.wait_ge(s_prep_pe, 1)
                    V.tensor_copy(W1T[:, :, :].rearrange("p c f -> p (c f)"), pR[0][:, 0:2 * P])
                    V.tensor_copy(wiT[:, :], pN[0][:, 0:3 * P])
                    V.tensor_copy(whT[:, :], pZ[0][:, 0:3 * P])
                    V.tensor_copy(gwT[:, :, :].rearrange("p c f -> p (c f)"), pM[0][:, 0:LEVELS * P]).then_inc(s_prep_cp, 1)
                    dve.wait_ge(s_prep_pe, 2)
                    V.tensor_copy(W12[:, :], pR[1][:, 0:P])
                    for l, b in enumerate((pZ[1], pM[1], pR[0], pN[0])):
                        V.tensor_copy(wlT[:, l, :], b[:, 0:3 * P])
                    chain(V.tensor_copy(c_bc[:, :], pN[1][:, 0:P]))
                    V.tensor_tensor(cb2_bc[:, :], c_bc[:, :], b2_bc[:, :], ALU.add).then_inc(s_wready, 1)
                    dve.wait_ge(s_wready, 1)

                def prep_edges(self):
                    dve.wait_ge(s_eload, 16 * 9)
                    dve.wait_ge(s_const, 2)
                    for a, b in ((dstF, dstR), (prevF, prevR), (nextF, nextR), (srcF, srcR), (eF, eR)):
                        V.tensor_copy(a[:, :], b[:, :])
                    V.tensor_copy(ecol[:, :], ecI[:, :])
                    chain(V.tensor_copy(t0col[:, :], t0I[:, :]))
                    chain(V.tensor_tensor(startF[:, :], dstF[:, :], prevF[:, :], ALU.not_equal))
                    chain(V.tensor_tensor(startF[:, :], startF[:, :], eF[:, :], ALU.mult))
                    V.tensor_tensor_scan(runF[:, :], startF[:, :], startF[:, :], 0.0, ALU.max, ALU.max).then_inc(s_car_pe, 1)
                    dve.wait_ge(s_car_pe, 2)
                    chain(V.tensor_copy(mv[0:1, 0:NT], pR[0][0:1, 0:NT]))
                    V.tensor_tensor_scan(carF[0:1, 1:NT + 1], mv[0:1, 0:NT], mv[0:1, 0:NT], 0.0, ALU.max, ALU.max).then_inc(s_car_pe, 1)
                    dve.wait_ge(s_car_pe, 4)
                    chain(V.tensor_copy(isd[0:NT, 0:1], pN[0][0:NT, 0:1]))
                    V.tensor_scalar(firstF[:, :], runF[:, :], isd[0:NT, 0:1], None, ALU.max).then_inc(s_first, 1)
                    dve.wait_ge(s_first, 1)
                    chain(V.tensor_tensor(dinvF[:, :], eF[:, :], firstF[:, :], ALU.subtract))
                    V.tensor_scalar(dinvF[:, :], dinvF[:, :], 2.0, None, ALU.add).then_inc(s_deg, 1)
                    chain(V.tensor_tensor(scatF[:, :], dstF[:, :], nextF[:, :], ALU.is_equal))
                    V.scalar_tensor_tensor(out=scatF[:, :], in0=scatF[:, :], scalar=float(2 * N), in1=dstF[:, :],
                                           op0=ALU.mult, op1=ALU.add).then_inc(s_col_pe, 1)
                    dve.wait_ge(s_col_pe, 2)
                    V.tensor_copy(dstC[:, :], pZ[0][:, 0:NT])
                    V.tensor_copy(srcI[:, :], pZ[0][:, NT:2 * NT])
                    V.tensor_copy(dinvD[:, :], pZ[0][:, 2 * NT:3 * NT])
                    V.tensor_copy(recrow[:, :, 1], pZ[0][:, 2 * NT:3 * NT])
                    V.tensor_copy(scatI[:, :], pZ[0][:, 3 * NT:4 * NT])
                    chain(V.tensor_copy(recrow[:, :, 0], ecol[:, :]))
                    V.tensor_scalar(dstI[:, :], dstC[:, :], float(N - 1), None, ALU.min).then_inc(s_cols, 1)

                def build_s(self, c):
                    dve.wait_ge(s_firstld, 16)
                    for t in range(RC):
                        cols = bass.ds((c * RC + t) * P, P)
                        V.tensor_scalar(FL[:, cols], S[:, cols], t0col[:, bass.ds(c * RC + t, 1)], None, ALU.is_lt)
                        V.scalar_tensor_tensor(out=S[:, cols], in0=S[:, cols], scalar=ecol[:, bass.ds(c * RC + t, 1)],
                                               in1=tri[:, :], op0=ALU.is_le, op1=ALU.mult).then_inc(s_S, 1)

                def prep_edges2(self):
                    dve.wait_ge(s_S, NT)
                    dve.wait_ge(s_recS, RL)
                    V.tensor_scalar(isd[:, :], recS[:, :, 0], 0.0, None, ALU.is_ge)
                    chain(V.tensor_tensor(mv[:, :], recS[:, :, 0], ecol[:, :], ALU.subtract))
                    chain(V.scalar_tensor_tensor(out=mv[:, :], in0=mv[:, :], scalar=float(NS), in1=isd[:, :],
                                                 op0=ALU.add, op1=ALU.mult))
                    V.tensor_tensor(idxI[:, :], mv[:, :], ecol[:, :], ALU.add).then_inc(s_idx, 1)
                    dve.wait_ge(s_idx, 1)

                def a1(self, d, k):
                    gate_n(1, 4 * d + k)

                def b1(self, d, k):
                    if k == 0:
                        dve.wait_ge(s_uT, d)
                    state(1, 4 * d + k, x1T[:, :] if k == 0 else h1[:, :], h1[:, :])

                def z(self, d):
                    dve.wait_ge(L[1]["m_filled"], 1 + m1("z", d) + 1)
                    dve.wait_ge(lns["pre1"][4], 1 + d)
                    V.tensor_tensor(z1[:, :, :], pM[1][0:DP, :].rearrange("p (j f) -> p j f", j=J),
                                    cb2_bc[0:DP, :].unsqueeze(1).broadcast_to([DP, J, P]), ALU.add).then_inc(s_z1, 1)
                    dve.wait_ge(s_sig1, d + 1)
                    V.tensor_tensor(z1[:, :, :], z1[:, :, :], xr1[:, :, :], ALU.add).then_inc(s_u1, 1)
                    dve.wait_ge(s_u1, d + 1)
                    ln_stats("pre1", d, lambda j: z1[:, j, :])

                def u(self, d):
                    dve.wait_ge(lns["fin1"][4], 1 + d)
                    dve.wait_ge(L[1]["h_ready"], 1 + 4 * d + 4)
                    V.scalar_tensor_tensor(out=uT[:, :], in0=x1T[:, :], scalar=2.0, in1=h1[:, :],
                                           op0=ALU.mult, op1=ALU.add).then_inc(s_uT, 1)

                def fin(self, d):
                    dve.wait_ge(L[1]["m_filled"], 1 + m1("fin", d) + 1)
                    ln_stats("fin1", d, lambda j: pM[1][0:DP, j * P:(j + 1) * P])

                def scale(self, to, rows, by, e):
                    for j in range(J):
                        last = V.tensor_scalar(to[:, j, :], rows[:, j, :], by(e * J + j), None, ALU.mult)
                    last.then_inc(s_scaled, 1)

                def st0(self, e):
                    dve.wait_ge(s_gs, 64 * e + 64)
                    dve.wait_ge(L[0]["m_filled"], 1 + m0s("xs", e))
                    self.scale(msg, xs, lambda t: recS[:, bass.ds(t, 1), 1], e)
                    dve.wait_ge(s_gd, 64 * e + 64)
                    self.scale(xdd, xd, lambda t: dinvD[:, bass.ds(t, 1)], e)
                    carries(e, m0s("sums", e), e)

                def st1(self, e):
                    dve.wait_ge(L[0]["m_filled"], 1 + m0s("z", e) + 1)
                    dve.wait_ge(st_zs, 1 + 16 * e)
                    V.tensor_tensor(zrow[:, :, :], pM[0][:, :].rearrange("p (j f) -> p j f", j=J),
                                    c_bc[:, :].unsqueeze(1).broadcast_to([P, J, P]), ALU.add).then_inc(s_zs, 1)
                    dve.wait_ge(s_zs, e + 1)
                    dve.wait_ge(lns["lane0"][4], 1 + e)
                    V.tensor_tensor(z0[:, :, :], zrow[:, :, :], b2_bc[:, :].unsqueeze(1).broadcast_to([P, J, P]),
                                    ALU.add).then_inc(s_zb, 1)

                def st2(self, e):
                    dve.wait_ge(s_sig0, e + 1)
                    V.tensor_tensor(z0[:, :, :], z0[:, :, :], xs[:, :, :], ALU.add).then_inc(s_u0, 1)
                    dve.wait_ge(s_u0, 1 + e + 1)
                    ln_stats("lane0", e, lambda j: z0[:, j, :])
                    dve.wait_ge(L[0]["m_filled"], 1 + m0s("xdd", e) + 1)
                    V.tensor_tensor(aggS[:, :], aggS[:, :], pM[0][:, :], ALU.add).then_inc(s_self, 1)

                def st3(self, e):
                    dve.wait_ge(L[0]["m_filled"], 1 + m0s("zd", e) + 1)
                    dve.wait_ge(st_zd, 1 + 16 * e)
                    for j in range(J):
                        last = V.scalar_tensor_tensor(out=zD[:, j, :], in0=pM[0][:, j * P:(j + 1) * P],
                                                      scalar=dinvD[:, bass.ds(e * J + j, 1)], in1=c_bc[:, :],
                                                      op0=ALU.mult, op1=ALU.add)
                    last.then_inc(s_zd, 1)

                def a0s(self, i, k):
                    gate_n(0, 3 * i + k)

                def b0s(self, i, k):
                    if k == 0:
                        dve.wait_ge(s_h0, i + 1)
                    state(0, 3 * i + k, hA[:, :] if k == 0 else hB[:, :], hB[:, :])

                def g0(self, i):
                    dve.wait_ge(s_gs, 64 * (NG + i) + 64)
                    dve.wait_ge(L[0]["m_filled"], 1 + M_G + GU * i)
                    self.scale(msg, xs, lambda t: recS[:, bass.ds(t, 1), 1], i)
                    carries(i, M_G + GU * i, NG + i)

                def g1(self, i):
                    dve.wait_ge(L[0]["m_filled"], 1 + M_G + GU * i + 2)
                    dve.wait_ge(s_ldz, 16 * i + 16)
                    dve.wait_ge(lns["lane0"][4], 1 + LN_G + i)
                    for j in range(J):
                        last = V.scalar_tensor_tensor(out=z0[:, j, :], in0=zDr[:, j, :], scalar=dinvD[:, bass.ds(i * J + j, 1)],
                                                      in1=pM[0][:, j * P:(j + 1) * P], op0=ALU.mult, op1=ALU.add)
                    last.then_inc(s_zpre, 1)
                    dve.wait_ge(s_zpre, 1 + i + 1)
                    for j in range(J):
                        last = V.scalar_tensor_tensor(out=z0[:, j, :], in0=z0[:, j, :], scalar=dinvD[:, bass.ds(i * J + j, 1)],
                                                      in1=b2_bc[:, :], op0=ALU.mult, op1=ALU.add)
                    last.then_inc(s_zb, 1)

                def g2(self, i):
                    dve.wait_ge(s_sig0, NG + i + 1)
                    dve.wait_ge(s_ldx, 16 * i + 16)
                    V.tensor_tensor(z0[:, :, :], z0[:, :, :], xdr[:, :, :], ALU.add).then_inc(s_u0, 1)
                    dve.wait_ge(s_u0, 1 + NG + i + 1)
                    ln_stats("lane0", LN_G + i, lambda j: z0[:, j, :])

                def sums0(self, l, g):
                    q = l * NG + g
                    carries(g, M_L + LU * q, 2 * NG + q)

                def a0(self, l, g):
                    q = l * NG + g
                    gate_n(0, GRU_L + q, M_L + LU * q + 1)

                def b0(self, l, g):
                    q = l * NG + g
                    dve.wait_ge(L[0]["m_filled"], 1 + M_L + LU * q)
                    dve.wait_ge(st_h, 1 + (16 * (NG + q) if l < LEVELS - 1 else 16 * NG * LEVELS))
                    dve.wait_ge(s_ldh, 16 * q + 16)
                    state(0, GRU_L + q, hA[:, :], hB[:, :])

                def t0(self, l, g):
                    q = l * NG + g
                    if l == LEVELS - 1:
                        dve.wait_ge(L[0]["m_filled"], 1 + M_L + LU * q + 3)
                        dve.wait_ge(s_ldx, 16 * (NG + g) + 16)
                        dve.wait_ge(lns["lane0"][4], 1 + LN_L + g)
                        V.scalar_tensor_tensor(out=z0[:, :, :].rearrange("p j f -> p (j f)"),
                                               in0=xdr[:, :, :].rearrange("p j f -> p (j f)"), scalar=2.0,
                                               in1=pM[0][:, :], op0=ALU.mult, op1=ALU.add).then_inc(s_fin, 1)
                        dve.wait_ge(s_fin, 1 + g + 1)
                        ln_stats("lane0", LN_L + g, lambda j: z0[:, j, :])

            schedule(dve, Vector())


_INS = ['x', 'src', 'dst', 'L0_gnn_W1', 'L0_gnn_b1', 'L0_gnn_W2', 'L0_gnn_b2', 'L1_gnn_weight',
        'L1_gnn_w_ih', 'L1_gnn_w_hh', 'L1_gnn_b_ih', 'L1_gnn_b_hh']


def kernel(**inputs):
    import numpy as _np
    import concourse.bacc as _bacc
    from concourse import mybir as _mybir
    from concourse.bass_utils import run_bass_kernel_spmd as _run

    nc = _bacc.Bacc("TRN2", target_bir_lowering=False, num_devices=1)
    arrays, args = {}, []
    for name in _INS:
        a = _np.ascontiguousarray(inputs[name])
        arrays[f"in_{name}_dram"] = a
        args.append(nc.dram_tensor(f"in_{name}_dram", a.shape, _mybir.dt.from_np(a.dtype), kind="ExternalInput").ap())
    shape = inputs["x"].shape
    args.append(nc.dram_tensor("out_0_dram", shape, _mybir.dt.float32, kind="ExternalOutput").ap())
    gcn_resnorm_ggnn_resnorm(nc, *args)
    r = _run(nc, [arrays], core_ids=[0])
    return r.results[0]["out_0_dram"]
```

```python
import concourse.bass as bass
from concourse import mybir
from contextlib import ExitStack


def gcn_resnorm_ggnn_resnorm(
    nc: bass.Bass,
    x: bass.AP, src: bass.AP, dst: bass.AP,
    W1: bass.AP, b1: bass.AP, W2: bass.AP, b2: bass.AP,
    gw: bass.AP, w_ih: bass.AP, w_hh: bass.AP, b_ih: bass.AP, b_hh: bass.AP,
    out: bass.AP,
):
    f32 = mybir.dt.float32
    bf16 = mybir.dt.bfloat16
    i32 = mybir.dt.int32
    ALU = mybir.AluOpType
    ACT = mybir.ActivationFunctionType

    N, F = x.shape
    E = src.shape[0]
    HID = W1.shape[1]
    LEVELS = gw.shape[0]
    P = 128
    J = 4
    GS = J * P
    NG = -(-E // GS)
    NT = NG * J
    NS = NT * P
    FULL = E // P
    REST = E - FULL * P
    DP = 125
    DW = DP * J
    ND = N // DW
    EPS = 1e-5
    PAIRS = (NG - 1) // 2
    LEAD = ND - 2 * NG - (LEVELS - 1) * (PAIRS + 1)
    assert N == ND * DW and NG % 2 == 1 and LEAD >= 2

    x_g = x.rearrange("(g p j) f -> g p (j f)", p=DP, j=J)
    out_g = out.rearrange("(g p j) f -> g p (j f)", p=DP, j=J)

    ctx = ExitStack()
    with ctx:
        def sb(name, shape, dt=f32):
            return ctx.enter_context(nc.sbuf_tensor(name, shape, dt))

        def sem(name):
            return ctx.enter_context(nc.semaphore(name))

        def dram(name, shape, dt=f32):
            return nc.dram_tensor(name, shape, dt)

        tz = dram("tz", [2 * NS, F])
        tx = [dram(f"tx{l}", [2 * NS, F]) for l in range(LEVELS)]
        rec = dram("rec", [N, 2])
        first_d = dram("first_d", [NT, P])
        xd_d = dram("xd_d", [NS, F])
        hT_d = dram("hT_d", [NG, P, GS])

        def rows(t, side):
            return t[side * NS:(side + 1) * NS, :].rearrange("(g j p) f -> g p j f", j=J, p=P)

        ident = sb("ident", [P, P])
        tri = sb("tri", [P, P])
        one = sb("one", [1, 1])
        mhalf = sb("mhalf", [P, P])
        W12 = sb("W12", [P, P])
        c_bc = sb("c_bc", [P, P])
        b2_bc = sb("b2_bc", [P, P])
        cb2_bc = sb("cb2_bc", [P, P])
        whT = sb("whT", [P, 3 * P])
        wiT = sb("wiT", [P, 3 * P])
        wlT = sb("wlT", [P, LEVELS, 3 * P])
        b3 = sb("b3", [P, 2, 3])
        brz = sb("brz", [P, 2])
        W1s = sb("W1s", [P, HID])
        W2s = sb("W2s", [P, 2, P])
        W1T = sb("W1T", [P, 2, P])
        b1c = sb("b1c", [P, 2])
        b1f = sb("b1f", [P, 2, P])
        wih_s = sb("wih_s", [P, 3, P])
        whh_s = sb("whh_s", [P, 3, P])
        gw_s = sb("gw_s", [P, LEVELS, P])
        gwT = sb("gwT", [P, LEVELS, P])

        dstR = sb("dstR", [NT, P], i32)
        prevR = sb("prevR", [NT, P], i32)
        nextR = sb("nextR", [NT, P], i32)
        srcR = sb("srcR", [NT, P], i32)
        eR = sb("eR", [NT, P], i32)
        dstF = sb("dstF", [NT, P])
        prevF = sb("prevF", [NT, P])
        nextF = sb("nextF", [NT, P])
        srcF = sb("srcF", [NT, P])
        eF = sb("eF", [NT, P])
        startF = sb("startF", [NT, P])
        runF = sb("runF", [NT, P])
        carF = sb("carF", [1, NT + 1])
        firstF = sb("firstF", [NT, P])
        dinvF = sb("dinvF", [NT, P])
        scatF = sb("scatF", [NT, P])
        ecI = sb("ecI", [P, NT], i32)
        ecol = sb("ecol", [P, NT])
        t0I = sb("t0I", [P, NT], i32)
        t0col = sb("t0col", [P, NT])
        srcI = sb("srcI", [P, NT], i32)
        dstI = sb("dstI", [P, NT], i32)
        scatI = sb("scatI", [P, NT], i32)
        dstC = sb("dstC", [P, NT])
        dinvD = sb("dinvD", [P, NT])
        recrow = sb("recrow", [P, NT, 2])
        recS = sb("recS", [P, NT, 2])
        isd = sb("isd", [P, NT])
        mv = sb("mv", [P, NT])
        idxI = sb("idxI", [P, NT], i32)
        recfill = sb("recfill", [DP, N // DP, 2])
        S = sb("S", [P, NS])
        FL = sb("FL", [P, NS], bf16)

        W = [GS, DW]
        rS = [sb(f"rS{i}", [P, W[i]]) for i in range(2)]
        zS = [sb(f"zS{i}", [P, W[i]]) for i in range(2)]
        tS = [sb(f"tS{i}", [P, W[i]]) for i in range(2)]
        nS = [sb(f"nS{i}", [P, W[i]]) for i in range(2)]
        dS = [sb(f"dS{i}", [P, W[i]]) for i in range(2)]
        hA = sb("hA", [P, GS])
        hB = sb("hB", [P, GS])
        h1 = sb("h1", [P, DW])
        x1T = sb("x1T", [P, DW])
        x2T = sb("x2T", [P, DW])
        uT = sb("uT", [P, DW])
        xr1 = sb("xr1", [DP, J, P])
        xT1 = sb("xT1", [P, DW])
        z1 = sb("z1", [DP, J, P])
        xn1 = sb("xn1", [DP, J, P])
        o1 = sb("o1", [DP, J, P])
        xs = sb("xs", [P, J, P])
        xd = sb("xd", [P, J, P])
        xsT = sb("xsT", [P, GS])
        msg = sb("msg", [P, J, P])
        xdd = sb("xdd", [P, J, P])
        aggS = sb("aggS", [P, GS])
        zrow = sb("zrow", [P, J, P])
        zD = sb("zD", [P, J, P])
        z0 = sb("z0", [P, J, P])
        xn0 = sb("xn0", [P, J, P])
        stg = sb("stg", [P, J, P])
        idxa = sb("idxa", [P, J], i32)
        idxb = sb("idxb", [P, J], i32)
        idxr = sb("idxr", [P, NT // ((LEAD - 1) // 2)], i32)
        rowr = sb("rowr", [P, NT // ((LEAD - 1) // 2), 2])
        zDr = sb("zDr", [P, J, P])
        xdr = sb("xdr", [P, J, P])

        def lnbuf(tag, p):
            return {"st": sb("st" + tag, [p, J, 6]), "ag": sb("ag" + tag, [p, J, 2]),
                    "rs": sb("rs" + tag, [p, J]), "nm": sb("nm" + tag, [p, J])}

        lnb = {"pre1": lnbuf("pre1", DP), "fin1": lnbuf("fin1", DP), "lane0": lnbuf("lane0", P)}

        def bank(name):
            return ctx.enter_context(nc.psum_tensor(name, [P, 512], f32))

        pR = [bank("pR0"), bank("pR1")]
        pN = [bank("pN0"), bank("pN1")]
        pZ = [bank("pZ0"), bank("pZ1")]
        pM = [bank("pM0"), bank("pM1")]

        s_const = sem("s_const")
        s_wload = sem("s_wload")
        s_pads = sem("s_pads")
        s_eload = sem("s_eload")
        s_prep_pe = sem("s_prep_pe")
        s_prep_cp = sem("s_prep_cp")
        s_wready = sem("s_wready")
        s_chain = sem("s_chain")
        s_col_pe = sem("s_col_pe")
        s_car_pe = sem("s_car_pe")
        s_deg = sem("s_deg")
        s_first = sem("s_first")
        s_firstst = sem("s_firstst")
        s_firstld = sem("s_firstld")
        s_S = sem("s_S")
        s_cols = sem("s_cols")
        s_recinit = sem("s_recinit")
        s_recg = sem("s_recg")
        s_rcopy = sem("s_rcopy")
        s_recS = sem("s_recS")
        s_idx = sem("s_idx")

        names = ["r_filled", "n_filled", "z_filled", "r_ready", "z_ready", "t_ready", "tanh_ready",
                 "diff_ready", "gated_ready", "h_ready"]
        L = [{n: sem(f"{n}{i}") for n in names} for i in range(2)]
        m_xs = sem("m_xs")
        m_sums = sem("m_sums")
        m_zs = sem("m_zs")
        m_xdd = sem("m_xdd")
        m_zd = sem("m_zd")
        m_agg = sem("m_agg")
        m_xn = sem("m_xn")
        m_t = sem("m_t")
        m_in = sem("m_in")
        m_xt = sem("m_xt")
        m_z = sem("m_z")
        m_x1 = sem("m_x1")
        m_fin = sem("m_fin")
        lns = {t: [sem(f"ln_{w}_{t}") for w in ("stats", "aggr", "rstd", "nmr", "out")] for t in lnb}
        s_x1load = sem("s_x1load")
        s_xT1 = sem("s_xT1")
        s_z1 = sem("s_z1")
        s_sig1 = sem("s_sig1")
        s_u1 = sem("s_u1")
        s_x1T = sem("s_x1T")
        s_x2 = sem("s_x2")
        s_uT = sem("s_uT")
        s_store1 = sem("s_store1")
        s_idxc = sem("s_idxc")
        s_gs = sem("s_gs")
        s_gd = sem("s_gd")
        s_scaled = sem("s_scaled")
        s_carry = sem("s_carry")
        s_carried = sem("s_carried")
        s_xsT = sem("s_xsT")
        s_self = sem("s_self")
        s_zs = sem("s_zs")
        s_zd = sem("s_zd")
        s_zpre = sem("s_zpre")
        s_zb = sem("s_zb")
        s_sig0 = sem("s_sig0")
        s_u0 = sem("s_u0")
        s_h0 = sem("s_h0")
        s_stg = sem("s_stg")
        st_zs = sem("st_zs")
        st_zd = sem("st_zd")
        st_xd = sem("st_xd")
        st_xn = sem("st_xn")
        st_stg = sem("st_stg")
        st_h = sem("st_h")
        s_ldz = sem("s_ldz")
        s_ldx = sem("s_ldx")
        s_ldh = sem("s_ldh")
        s_in = sem("s_in")
        s_fin = sem("s_fin")
        s_scat = sem("s_scat")

        GRU_L = 3 * NG
        LN_G = NG
        LN_L = 2 * NG

        from_one = [s_zpre, s_fin, s_u0, s_scaled, s_stg, s_store1, s_carried, s_carry, m_agg,
                    st_xd, st_xn, st_stg, st_h, st_zs, st_zd]
        from_one += [L[i][n] for i in range(2) for n in names if n.endswith("_ready")
                     if n not in ("tanh_ready", "diff_ready")]
        from_one += [lns[t][4] for t in lnb]

        turns = {"sp": sem("s_turn_sp"), "pool": sem("s_turn_pool"), "dve": sem("s_turn_dve")}

        def settle(eng, name):
            eng.sem_inc(turns[name], 1)

        block = ctx.enter_context(nc.Block())

        D_S = LEAD
        D_G = D_S + NG
        D_L = D_G + NG
        RL = (LEAD - 1) // 2
        RC = NT // RL
        RK = RC // 4
        assert LEAD == 1 + 2 * RL and NT == RL * 4 * RK

        class Step:
            def __init__(self, lane, n, kind, h, hout, d=None, i=None, k=None, l=None, g=None, q=None):
                self.lane, self.n, self.kind, self.h, self.hout = lane, n, kind, h, hout
                self.d, self.i, self.k, self.l, self.g, self.q = d, i, k, l, g, q
                self.agg = kind == "edge"

        def dense_step(d, k):
            return Step(1, 4 * d + k, "dense", x1T[:, :] if k == 0 else h1[:, :], h1[:, :], d=d, k=k)

        def src_step(i, k):
            return Step(0, 3 * i + k, "src", hA[:, :] if k == 0 else hB[:, :], hB[:, :], i=i, k=k)

        def edge_step(l, g):
            return Step(0, GRU_L + l * NG + g, "edge", hA[:, :], hB[:, :], l=l, g=g, q=l * NG + g)

        def schedule(eng, p):
            def run(pieces):
                for piece, *args in pieces:
                    piece(*args)

            def quarter(d, k, after_r=(), pe=(), dve=(), sig=(), mid=(), act=(), late=(), end=(),
                        stat=True, copy_last=False, first=False, last=False):
                s = dense_step(d, k)
                more = not last
                p.pe_r(s)
                run(after_r)
                p.pe_n(s)
                if k == 0 and not first:
                    p.fin_pe(d - 1)
                p.pe_z(s)
                if k == 0 and more:
                    p.load(d + 1)
                if k == 1 and more:
                    p.xt(d + 1)
                run(dve)
                run(pe)
                p.act_r(s)
                run(sig)
                p.dve_t(s)
                if k == 0 and not first:
                    p.fin_stat(d - 1)
                if k == 2 and more:
                    p.zadd(d + 1)
                run(mid)
                p.act_t(s)
                p.act_z(s)
                if k == 3 and more:
                    p.x1_norm(d + 1)
                    p.x1(d + 1)
                if k == 1 and more and not copy_last:
                    p.xt_act(d + 1)
                run(act)
                if k == 1 and more:
                    if copy_last:
                        p.xt_act(d + 1)
                    p.zmm(d + 1)
                if k == 3 and more:
                    p.x1_act(d + 1)
                run(late)
                if k == 2 and more:
                    p.zsig(d + 1)
                p.dve_diff(s)
                p.dve_gated(s)
                p.dve_h(s)
                if k == 3:
                    p.u(d)
                if k == 2 and more and stat:
                    p.zstat(d + 1)
                if k == 0 and not first:
                    p.fin_norm(d - 1)
                run(end)
                if k == 1:
                    p.x2(d)

            p.prep_weights()
            p.load1(0)
            for f in (p.xt, p.xt_act, p.zmm, p.zadd, p.zsig, p.zstat, p.x1_norm, p.x1, p.x1_act):
                f(0)
            for k in range(4):
                quarter(0, k, first=True)
            p.prep_edges()
            with eng.Fori(0, RL) as c:
                for k in range(4):
                    p.rec_scatter(c, k)
                    quarter(c + 1, k)
            p.rec_all()
            with eng.Fori(0, RL) as c:
                for k in range(4):
                    p.rec_gather(c, k)
                    quarter(c + (1 + RL), k)
                p.build_s(c)
            p.prep_edges2()

            def gates(s, *between):
                return [(p.pe_r, s)] + [(p.t_pe, s.i, s.k - 1)] * (s.k > 0) + [(p.pe_n, s), *between, (p.pe_z, s)]

            def new_state(s):
                return [(p.dve_diff, s), (p.dve_gated, s), (p.dve_h, s)]

            def s_step(i, stage=True, gather=True):
                d = i + D_S
                e = i + 1
                g = [src_step(i, k) for k in range(3)]

                def ahead(*pieces):
                    return [(f, e) for f in pieces] if stage else []

                quarter(d, 0, pe=[(p.xn_pe, i)] + gates(g[0], (p.zd_pe, i)),
                        act=[(p.xn_act, i), (p.act_r, g[0])],
                        end=ahead(p.scale_msg) + [(p.dve_t, g[0]), (p.act_t, g[0]), (p.zd_dve, i)] + ahead(p.scale_xdd))
                quarter(d, 1, sig=[(p.act_z, g[0])] + ahead(p.xs_act), mid=new_state(g[0]),
                        pe=ahead(p.xs_pe) + gates(g[1], *ahead(p.sums_s)),
                        act=[(p.act_r, g[1]), (p.t_act, i, 0)], copy_last=True,
                        end=[(p.dve_t, g[1]), (p.act_t, g[1])] + ahead(p.carry_s) + [(p.gg, 0), (p.gl, 0)] * (not stage))
                quarter(d, 2, sig=[(p.act_z, g[1])], mid=new_state(g[1]),
                        pe=gates(g[2], *ahead(p.zs_pe)),
                        act=[(p.act_r, g[2]), (p.t_act, i, 1)],
                        end=[(p.dve_t, g[2]), (p.act_t, g[2])] + ahead(p.zs_dve, p.zs_act) + [(p.zstat, d + 1)],
                        stat=False)
                quarter(d, 3, dve=ahead(p.us), sig=[(p.act_z, g[2])],
                        mid=ahead(p.self_dve) + new_state(g[2]) + [(p.sg, i + 2)] * gather,
                        pe=ahead(p.xdd_pe) + [(p.t_pe, i, 2)],
                        act=[(p.t_act, i, 2)],
                        end=ahead(p.xn_norm))

            p.sg(0)
            for f in (p.scale_msg, p.scale_xdd, p.xs_pe, p.xs_act, p.sums_s, p.carry_s, p.zs_pe, p.zs_dve, p.zs_act,
                      p.xdd_pe, p.us, p.self_dve, p.xn_norm):
                f(0)
            p.sg(1)
            with eng.Fori(0, NG - 2) as i:
                s_step(i)
            s_step(NG - 2, gather=False)
            s_step(NG - 1, stage=False, gather=False)

            def g_step(i, gather=True):
                d = i + D_G
                before = [] if is_int(i, 0) else [i - 1]
                quarter(d, 0, dve=[(p.g_scale, i)] + [(p.gg, i + 1)] * gather, pe=[(p.g3, b) for b in before] + [(p.g_sums, i)],
                        act=[(p.g3_act, b) for b in before],
                        end=[(p.g_carry, i)])
                quarter(d, 1, pe=[(p.agg_pe, i)], mid=[(p.g1, i)], end=[(p.g1b, i)])
                quarter(d, 2)
                quarter(d, 3, mid=[(p.g2, i)], end=[(p.g3_norm, i)] + [(p.gl, i + 1)] * gather)

            g_step(0)
            with eng.Fori(1, NG - 1) as i:
                g_step(i)
            g_step(NG - 1, gather=False)
            p.g3(NG - 1)
            p.g3_act(NG - 1)

            def half(l, g, d, k, more=True):
                s = edge_step(l, g)
                if more:
                    p.lg(l, g + 1)
                quarter(d, k, pe=[(p.pe_r, s), (p.pe_n, s), (p.pe_in, s)],
                        act=[(p.act_r, s)], end=[(p.dve_t, s), (p.act_t, s)], last=is_int(d, ND - 1))
                quarter(d, k + 1, after_r=[(p.pe_z, s)], mid=new_state(s) + [(p.ldh, l, g + 1)] * more,
                        pe=[(p.l_pe, l, g)], late=[(p.sums_l, l, g + 1)] * more,
                        sig=[(p.act_z, s)], act=[(p.l_act, l, g)],
                        end=[(p.carry_l, l, g + 1)] * more, last=is_int(d, ND - 1))

            p.lg(0, 0)
            p.ldh(0, 0)
            p.sums_l(0, 0)
            p.carry_l(0, 0)
            for l in range(LEVELS - 1):
                dl = D_L + l * (PAIRS + 1)

                def pair(i):
                    half(l, 2 * i, i + dl, 0)
                    half(l, 2 * i + 1, i + dl, 2)

                pair(0)
                with eng.Fori(1, PAIRS) as i:
                    pair(i)
                d = dl + PAIRS
                half(l, NG - 1, d, 0, more=False)
                quarter(d, 2, mid=[(p.lg, l + 1, 0), (p.ldh, l + 1, 0), (p.ldx, l + 1, 0)], last=is_int(d, ND - 1))
                quarter(d, 3, pe=[(p.sums_l, l + 1, 0)], end=[(p.carry_l, l + 1, 0)], last=is_int(d, ND - 1))
                if is_int(d, ND - 1):
                    for f in (p.fin_pe, p.fin_stat, p.fin_norm):
                        f(d)

            l = LEVELS - 1

            def group(g, more=True, gather=True):
                s = edge_step(l, g)
                for f in (p.pe_r, p.pe_n, p.pe_in, p.pe_z, p.act_r, p.dve_t, p.act_t, p.act_z):
                    f(s)
                if more:
                    p.sums_l(l, g + 1)
                run(new_state(s))
                p.l_pe(l, g)
                if more:
                    p.ldh(l, g + 1)
                    p.carry_l(l, g + 1)
                if gather:
                    p.lg(l, g + 2)
                p.fin0(l, g)
                if more:
                    p.ldx(l, g + 1)

            p.lg(l, 1)
            group(0)
            with eng.Fori(1, NG - 2) as g:
                group(g)
            group(NG - 2, gather=False)
            group(NG - 1, more=False, gather=False)

        class Pieces:
            def nothing(self, *a):
                pass
            prep_weights = prep_edges = prep_edges2 = build_s = rec_scatter = rec_all = rec_gather = nothing
            pe_r = pe_n = pe_in = pe_z = act_r = act_t = act_z = dve_t = dve_diff = dve_gated = dve_h = nothing
            load1 = load = xt = xt_act = zmm = zadd = zsig = zstat = x1_norm = x1 = x1_act = x2 = nothing
            u = fin_pe = fin_stat = fin_norm = nothing
            sg = scale_msg = scale_xdd = xs_pe = xs_act = sums_s = carry_s = zs_pe = zs_dve = zs_act = nothing
            xdd_pe = self_dve = us = zd_pe = zd_dve = xn_norm = xn_pe = xn_act = t_pe = t_act = nothing
            gg = gl = g_scale = g_sums = g_carry = agg_pe = g1 = g1b = g2 = g3 = g3_norm = g3_act = nothing
            lg = ldh = ldx = sums_l = carry_l = l_pe = l_act = fin0 = nothing

        def is_int(v, *values):
            return isinstance(v, int) and v in values

        @block.sync
        def _(sp):
            class Sync(Pieces):
                def prep_weights(self):
                    for s in from_one:
                        sp.sem_inc(s, 1)
                    sp.dma_start(W1s[:, :], W1[:, :]).then_inc(s_wload, 16)
                    sp.dma_start(W2s[:, :, :], W2.rearrange("(c p) f -> p c f", p=P)).then_inc(s_wload, 16)
                    sp.dma_start(wih_s[:, :, :], w_ih.rearrange("(c p) f -> p c f", p=P)).then_inc(s_wload, 16)
                    sp.dma_start(whh_s[:, :, :], w_hh.rearrange("(c p) f -> p c f", p=P)).then_inc(s_wload, 16)
                    sp.dma_start(gw_s[:, :, :], gw.rearrange("l p f -> p l f")).then_inc(s_wload, 16)
                    with nc.allow_non_contiguous_dma(reason="bias columns, once"):
                        sp.dma_start(b1c[:, :], b1.rearrange("(c p) -> p c", p=P)).then_inc(s_wload, 16)
                        sp.dma_start(b3[:, 0, :], b_ih.rearrange("(c p) -> p c", p=P)).then_inc(s_wload, 16)
                        sp.dma_start(b3[:, 1, :], b_hh.rearrange("(c p) -> p c", p=P)).then_inc(s_wload, 16)
                    sp.dma_start(b2_bc[:, :], b2.rearrange("(a f) -> a f", a=1).broadcast_to([P, P])).then_inc(s_wload, 16)

                def load1(self, d):
                    sp.dma_start(xr1[:, :, :].rearrange("p j f -> p (j f)"), x_g[d]).then_inc(s_x1load, 16)
                    sp.wait_ge(s_pads, 1)
                    for t, a in ((dstR, dst), (srcR, src)):
                        sp.dma_start(t[0:FULL, :], a[0:FULL * P].rearrange("(t p) -> t p", p=P)).then_inc(s_eload, 16)
                        sp.dma_start(t[FULL:FULL + 1, 0:REST], a[FULL * P:E].rearrange("(t p) -> t p", t=1)).then_inc(s_eload, 16)
                    sp.dma_start(nextR[0:FULL, :], dst[1:FULL * P + 1].rearrange("(t p) -> t p", p=P)).then_inc(s_eload, 16)
                    sp.dma_start(nextR[FULL:FULL + 1, 0:REST - 1], dst[FULL * P + 1:E].rearrange("(t p) -> t p", t=1)).then_inc(s_eload, 16)
                    sp.dma_start(prevR[0:1, 1:P], dst[0:P - 1].rearrange("(t p) -> t p", t=1)).then_inc(s_eload, 16)
                    sp.dma_start(prevR[1:FULL, :], dst[P - 1:FULL * P - 1].rearrange("(t p) -> t p", p=P)).then_inc(s_eload, 16)
                    sp.dma_start(prevR[FULL:FULL + 1, 0:REST + 1], dst[FULL * P - 1:E].rearrange("(t p) -> t p", t=1)).then_inc(s_eload, 16)
                    sp.dma_start(rec[:, :].rearrange("(p n) c -> p (n c)", p=DP),
                                 recfill[:, :, :].rearrange("p n c -> p (n c)")).then_inc(s_recinit, 16)

                def load(self, d):
                    sp.wait_ge(s_u1, d)
                    settle(sp, "sp")
                    sp.dma_start(xr1[:, :, :].rearrange("p j f -> p (j f)"), x_g[d]).then_inc(s_x1load, 16)

                def fin_norm(self, d):
                    sp.wait_ge(lns["fin1"][4], 1 + d + 1)
                    settle(sp, "sp")
                    sp.dma_start(out_g[d], o1[:, :, :].rearrange("p j f -> p (j f)")).then_inc(s_store1, 16)

                def prep_edges(self):
                    sp.wait_ge(s_first, 1)
                    sp.dma_start(first_d[:, :], firstF[:, :]).then_inc(s_firstst, 16)
                    sp.wait_ge(s_firstst, 16)
                    sp.dma_start(S[:, :], first_d[:, :].rearrange("(a t) p -> a (t p)", a=1).broadcast_to([P, NS]),
                                 max_dma_last_dim=NS).then_inc(s_firstld, 16)

                def scale_msg(self, e):
                    sp.wait_ge(s_gd, 64 * e + 64)
                    settle(sp, "sp")
                    sp.dma_start(xd_d[:, :].rearrange("(g j p) f -> g p j f", j=J, p=P)[e], xd[:, :, :]).then_inc(st_xd, 16)

                def zs_dve(self, e):
                    sp.wait_ge(s_zs, e + 1)
                    settle(sp, "sp")
                    sp.dma_start(rows(tz, 0)[e], zrow[:, :, :]).then_inc(st_zs, 16)

                def zd_dve(self, e):
                    sp.wait_ge(s_zd, e + 1)
                    settle(sp, "sp")
                    sp.dma_start(rows(tz, 1)[e], zD[:, :, :]).then_inc(st_zd, 16)

                def xn_norm(self, e):
                    sp.wait_ge(lns["lane0"][4], 1 + e + 1)
                    settle(sp, "sp")
                    sp.dma_start(rows(tx[0], 0)[e], xn0[:, :, :]).then_inc(st_xn, 16)

                def t_act(self, i, k):
                    sp.wait_ge(s_stg, 1 + 3 * i + k + 1)
                    settle(sp, "sp")
                    sp.dma_start(rows(tx[k + 1], 0)[i], stg[:, :, :]).then_inc(st_stg, 16)

                def gl(self, i):
                    sp.wait_ge(st_zd, 1 + 16 * NG)
                    sp.wait_ge(st_xd, 1 + 16 * NG)
                    sp.wait_ge(s_zpre, 1 + i)
                    settle(sp, "sp")
                    sp.dma_start(zDr[:, :, :], rows(tz, 1)[i]).then_inc(s_ldz, 16)
                    if not isinstance(i, int):
                        sp.wait_ge(s_u0, 1 + i + NG)
                        settle(sp, "sp")
                    elif i:
                        sp.wait_ge(s_u0, 1 + i + NG)
                    sp.dma_start(xdr[:, :, :], xd_d[:, :].rearrange("(g j p) f -> g p j f", j=J, p=P)[i]).then_inc(s_ldx, 16)

                def g3_norm(self, i):
                    sp.wait_ge(lns["lane0"][4], 1 + LN_G + i + 1)
                    settle(sp, "sp")
                    sp.dma_start(rows(tx[0], 1)[i], xn0[:, :, :]).then_inc(st_xn, 16)

                def g3_act(self, i):
                    sp.wait_ge(s_h0, NG + i + 1)
                    settle(sp, "sp")
                    sp.dma_start(hT_d[i], hA[:, :]).then_inc(st_h, 16)

                def ldh(self, l, g):
                    q = l * NG + g
                    sp.wait_ge(st_h, 1 + 16 * NG * (l + 1))
                    sp.wait_ge(L[0]["diff_ready"], GRU_L + q)
                    sp.wait_ge(L[0]["z_filled"], GRU_L + q)
                    settle(sp, "sp")
                    sp.dma_start(hA[:, :], hT_d[g]).then_inc(s_ldh, 16)

                def ldx(self, l, g):
                    if l == LEVELS - 1:
                        sp.wait_ge(s_fin, 1 + g)
                        settle(sp, "sp")
                        sp.dma_start(xdr[:, :, :], rows(tx[0], 1)[g]).then_inc(s_ldx, 16)

                def dve_h(self, s):
                    if s.kind == "edge" and s.l < LEVELS - 1:
                        sp.wait_ge(L[0]["h_ready"], 1 + s.n + 1)
                        settle(sp, "sp")
                        sp.dma_start(hT_d[s.g], hB[:, :]).then_inc(st_h, 16)

                def l_act(self, l, g):
                    q = l * NG + g
                    if l < LEVELS - 1:
                        sp.wait_ge(s_stg, 1 + 3 * NG + q + 1)
                        settle(sp, "sp")
                        sp.dma_start(rows(tx[l + 1], 1)[g], stg[:, :, :]).then_inc(st_stg, 16)

            schedule(sp, Sync())
            sp.wait_ge(s_store1, 1 + 16 * ND)
            sp.wait_ge(s_scat, 2 * 16 * NT)

        @block.gpsimd
        def _(pool):
            def gather(buf, table, ix, done):
                for j in range(J):
                    nc.gpsimd.indirect_dma_start(
                        out=buf[:, j, :], out_offset=None, in_=table,
                        in_offset=bass.IndirectOffsetOnAxis(ap=ix[:, j:j + 1], axis=0)).then_inc(done, 16)

            def rstd(tag, n):
                b, s = lnb[tag], lns[tag]
                pool.wait_ge(s[1], n + 1)
                settle(pool, "pool")
                nc.gpsimd.tensor_scalar(b["rs"][:, :], b["ag"][:, :, 1], EPS, None, ALU.add).then_inc(s[2], 1)
                nc.gpsimd.tensor_scalar(b["nm"][:, :], b["ag"][:, :, 0], -1.0, None, ALU.mult)
                pool.wait_ge(s[2], 2 * n + 1)
                settle(pool, "pool")
                nc.gpsimd.tensor_tensor(b["rs"][:, :], b["rs"][:, :], mhalf[0:b["rs"].shape[0], 0:J], ALU.pow).then_inc(s[2], 1)
                pool.wait_ge(s[2], 2 * n + 2)
                settle(pool, "pool")
                nc.gpsimd.tensor_tensor(b["nm"][:, :], b["nm"][:, :], b["rs"][:, :], ALU.mult).then_inc(s[3], 1)

            class Pool(Pieces):
                def zstat(self, d):
                    rstd("pre1", d)

                def fin_stat(self, d):
                    rstd("fin1", d)

                def us(self, e):
                    rstd("lane0", e)

                def g2(self, i):
                    rstd("lane0", LN_G + i)

                def prep_weights(self):
                    nc.gpsimd.memset(mhalf[:, :], -0.5)
                    nc.gpsimd.memset(ident[:, :], 0.0)
                    nc.gpsimd.memset(tri[:, :], 1.0)
                    nc.gpsimd.iota(eR[:, :], pattern=[[1, P]], base=0, channel_multiplier=P)
                    nc.gpsimd.iota(ecI[:, :], pattern=[[P, NT]], base=0, channel_multiplier=1)
                    nc.gpsimd.iota(t0I[:, :], pattern=[[P, NT]], base=0, channel_multiplier=0).then_inc(s_const, 1)
                    pool.wait_ge(s_const, 1)
                    nc.gpsimd.affine_select(out=ident[:, :], in_=ident[:, :], compare_op=ALU.not_equal, fill=1.0,
                                            base=0, pattern=[[-1, P]], channel_multiplier=1)
                    nc.gpsimd.affine_select(out=tri[:, :], in_=tri[:, :], compare_op=ALU.is_ge, fill=0.0,
                                            base=0, pattern=[[1, P]], channel_multiplier=-1).then_inc(s_const, 1)

                def prep_edges(self):
                    pool.wait_ge(s_deg, 1)
                    nc.gpsimd.tensor_tensor(dinvF[:, :], dinvF[:, :], mhalf[0:NT, :], ALU.pow).then_inc(s_deg, 1)
                    pool.wait_ge(s_cols, 1)
                    pool.wait_ge(s_recinit, 16)

                def rec_scatter(self, c, k):
                    if k == 0:
                        nc.gpsimd.tensor_copy(idxr[:, :], scatI[:, bass.ds(c * RC, RC)])
                        nc.gpsimd.tensor_copy(rowr[:, :, :], recrow[:, bass.ds(c * RC, RC), :]).then_inc(s_rcopy, 1)
                        pool.wait_ge(s_rcopy, c + 1)
                        settle(pool, "pool")
                    for t in range(k * RK, (k + 1) * RK):
                        nc.gpsimd.indirect_dma_start(
                            out=rec[:, :], out_offset=bass.IndirectOffsetOnAxis(ap=idxr[:, t:t + 1], axis=0),
                            in_=rowr[:, t, :], in_offset=None, bounds_check=N - 1,
                            oob_is_err=False).then_inc(s_scat, 16)
                    if k == 3:
                        pool.wait_ge(s_scat, 16 * RC * (c + 1))
                        settle(pool, "pool")

                def rec_all(self):
                    pool.wait_ge(s_scat, 16 * NT)

                def rec_gather(self, c, k):
                    if k == 0:
                        nc.gpsimd.tensor_copy(idxr[:, :], srcI[:, bass.ds(c * RC, RC)]).then_inc(s_rcopy, 1)
                        pool.wait_ge(s_rcopy, RL + c + 1)
                        settle(pool, "pool")
                    for t in range(k * RK, (k + 1) * RK):
                        nc.gpsimd.indirect_dma_start(
                            out=rowr[:, t, :], out_offset=None, in_=rec[:, :],
                            in_offset=bass.IndirectOffsetOnAxis(ap=idxr[:, t:t + 1], axis=0)).then_inc(s_recg, 16)
                    if k == 3:
                        pool.wait_ge(s_recg, 16 * RC * (c + 1))
                        settle(pool, "pool")
                        nc.gpsimd.tensor_copy(recS[:, bass.ds(c * RC, RC), :], rowr[:, :, :]).then_inc(s_recS, 1)

                def sg(self, e):
                    pool.wait_ge(s_scaled, 1 + 2 * e)
                    pool.wait_ge(s_u0, 1 + e)
                    pool.wait_ge(st_xd, 1 + 16 * e)
                    settle(pool, "pool")
                    nc.gpsimd.tensor_copy(idxa[:, :], srcI[:, bass.ds(e * J, J)]).then_inc(s_idxc, 1)
                    nc.gpsimd.tensor_copy(idxb[:, :], dstI[:, bass.ds(e * J, J)]).then_inc(s_idxc, 1)
                    pool.wait_ge(s_idxc, 2 * e + 2)
                    settle(pool, "pool")
                    gather(xs, x[:, :], idxa, s_gs)
                    gather(xd, x[:, :], idxb, s_gd)

                def gg(self, i):
                    pool.wait_ge(s_idx, 1)
                    pool.wait_ge(s_scaled, 1 + 2 * NG + i)
                    pool.wait_ge(s_u0, 1 + NG)
                    nc.gpsimd.tensor_copy(idxa[:, :], idxI[:, bass.ds(i * J, J)]).then_inc(s_idxc, 1)
                    pool.wait_ge(st_zs, 1 + 16 * NG)
                    pool.wait_ge(st_zd, 1 + 16 * NG)
                    pool.wait_ge(s_idxc, 2 * NG + i + 1)
                    settle(pool, "pool")
                    gather(xs, tz[:, :], idxa, s_gs)

                def lg(self, l, g):
                    q = l * NG + g
                    pool.wait_ge(s_gs, 64 * (2 * NG + q))
                    pool.wait_ge(s_scaled, 1 + 3 * NG)
                    pool.wait_ge(m_sums, 2 * NG + q)
                    nc.gpsimd.tensor_copy(idxa[:, :], idxI[:, bass.ds(g * J, J)]).then_inc(s_idxc, 1)
                    pool.wait_ge(st_xn, 1 + 16 * 2 * NG)
                    pool.wait_ge(st_stg, 1 + 16 * NG * (3 + l))
                    pool.wait_ge(s_idxc, 3 * NG + q + (g - 2 if l == LEVELS - 1 and not is_int(g, 0, 1) else 0) + 1)
                    settle(pool, "pool")
                    gather(xs, tx[l][:, :], idxa, s_gs)

                def fin0(self, l, g):
                    if l == LEVELS - 1:
                        rstd("lane0", LN_L + g)
                        pool.wait_ge(s_scat, 16 * NT + 16 * J * g)
                        nc.gpsimd.tensor_copy(idxb[:, :], scatI[:, bass.ds(g * J, J)]).then_inc(s_idxc, 1)
                        pool.wait_ge(s_idxc, 3 * NG + l * NG + 2 * g + 2 + (0 if is_int(g, NG - 1) else 1 if is_int(g, NG - 2) else 2))
                        pool.wait_ge(s_store1, 1 + 16 * ND)
                        pool.wait_ge(lns["lane0"][4], 1 + LN_L + g + 1)
                        settle(pool, "pool")
                        for j in range(J):
                            nc.gpsimd.indirect_dma_start(
                                out=out[:, :], out_offset=bass.IndirectOffsetOnAxis(ap=idxb[:, j:j + 1], axis=0),
                                in_=xn0[:, j, :], in_offset=None, bounds_check=N - 1,
                                oob_is_err=False).then_inc(s_scat, 16)

            schedule(pool, Pool())

        @block.tensor
        def _(pe):
            def transposes(lane, source, p, filled):
                bank = pM[lane]
                for j in range(J):
                    last = nc.tensor.transpose(bank[:, j * p:(j + 1) * p], source[:, j, :], ident[0:p, 0:p])
                last.then_inc(filled, 1)

            def back(bank, source, p, filled):
                for j in range(J):
                    last = nc.tensor.transpose(bank[0:p, j * P:(j + 1) * P], source[:, j * p:(j + 1) * p], ident[:, :])
                last.then_inc(filled, 1)

            def sums(i, source):
                for j in range(J):
                    last = nc.tensor.matmul(pM[0][:, j * P:(j + 1) * P], source[:, j, :],
                                            S[:, bass.ds((i * J + j) * P, P)], start=True, stop=True)
                last.then_inc(m_sums, 1)

            class Tensor(Pieces):
                def prep_weights(self):
                    pe.wait_ge(s_const, 2)
                    pe.wait_ge(s_wload, 16 * 9)
                    for c in range(2):
                        last = nc.tensor.transpose(pR[0][:, c * P:(c + 1) * P], W1s[:, c * P:(c + 1) * P], ident[:, :])
                    for c in range(3):
                        last = nc.tensor.transpose(pN[0][:, c * P:(c + 1) * P], wih_s[:, c, :], ident[:, :])
                    for c in range(3):
                        last = nc.tensor.transpose(pZ[0][:, c * P:(c + 1) * P], whh_s[:, c, :], ident[:, :])
                    for c in range(LEVELS):
                        last = nc.tensor.transpose(pM[0][:, c * P:(c + 1) * P], gw_s[:, c, :], ident[:, :])
                    last.then_inc(s_prep_pe, 1)
                    pe.wait_ge(s_prep_cp, 1)
                    for c in range(2):
                        nc.tensor.matmul(pR[1][:, 0:P], W1T[:, c, :], W2s[:, c, :], start=c == 0, stop=c == 1)
                    for c in range(2):
                        nc.tensor.matmul(pN[1][:, 0:P], b1f[:, c, :], W2s[:, c, :], start=c == 0, stop=c == 1)
                    for l, b in enumerate((pZ[1], pM[1], pR[0], pN[0])):
                        last = nc.tensor.matmul(b[:, 0:3 * P], gwT[:, l, :], wiT[:, :], start=True, stop=True)
                    last.then_inc(s_prep_pe, 1)
                    pe.wait_ge(s_wready, 1)

                def prep_edges(self):
                    pe.wait_ge(s_car_pe, 1)
                    nc.tensor.matmul(pR[0][0:1, 0:NT], runF[:, P - 1:P], ident[0:NT, 0:NT], start=True, stop=True).then_inc(s_car_pe, 1)
                    pe.wait_ge(s_car_pe, 3)
                    nc.tensor.matmul(pN[0][0:NT, 0:1], carF[0:1, 0:NT], one[0:1, 0:1], start=True, stop=True).then_inc(s_car_pe, 1)
                    pe.wait_ge(s_col_pe, 1)
                    pe.wait_ge(s_deg, 2)
                    for c, t in enumerate((dstF, srcF, dinvF, scatF)):
                        last = nc.tensor.transpose(pZ[0][:, c * NT:(c + 1) * NT], t[:, :], ident[0:NT, 0:NT])
                    last.then_inc(s_col_pe, 1)

                def gate(self, s, bank, c, filled):
                    to = bank[s.lane][:, 0:W[s.lane]]
                    last = nc.tensor.matmul(to, whT[:, c * P:(c + 1) * P], s.h, start=True, stop=not s.agg)
                    if s.agg:
                        last = nc.tensor.matmul(to, wlT[:, s.l, c * P:(c + 1) * P], aggS[:, :], start=False, stop=True)
                    last.then_inc(L[s.lane][filled], 1)

                def pe_r(self, s):
                    if s.kind == "dense" and s.k == 0:
                        pe.wait_ge(s_x1T, s.d + 1)
                    elif s.kind == "src" and s.k == 0:
                        pe.wait_ge(s_h0, s.i + 1)
                    elif s.kind == "edge":
                        pe.wait_ge(s_ldh, 16 * s.q + 16)
                        pe.wait_ge(s_carry, 1 + J * (2 * NG + s.q + 1))
                    else:
                        pe.wait_ge(L[s.lane]["h_ready"], 1 + s.n)
                    pe.wait_ge(L[s.lane]["r_ready"], 1 + s.n)
                    self.gate(s, pR, 0, "r_filled")

                def pe_n(self, s):
                    pe.wait_ge(L[s.lane]["t_ready"], 1 + s.n)
                    nc.tensor.matmul(pN[s.lane][:, 0:W[s.lane]], whT[:, 2 * P:3 * P], s.h,
                                     start=True, stop=True).then_inc(L[s.lane]["n_filled"], 1)

                def pe_in(self, s):
                    pe.wait_ge(s_carry, 1 + J * (2 * NG + s.q + 1))
                    nc.tensor.matmul(pM[0][:, :], wlT[:, s.l, 2 * P:3 * P], aggS[:, :],
                                     start=True, stop=True).then_inc(m_in, 1)

                def pe_z(self, s):
                    pe.wait_ge(L[s.lane]["z_ready"], 1 + s.n)
                    self.gate(s, pZ, 1, "z_filled")

                def xt(self, d):
                    pe.wait_ge(s_x1load, 16 * d + 16)
                    if is_int(d, 0, 1):
                        pe.wait_ge(s_x1T, d)
                    else:
                        pe.wait_ge(lns["fin1"][4], 1 + d - 1)
                    transposes(1, xr1, DP, m_xt)

                def zmm(self, d):
                    pe.wait_ge(s_xT1, d + 1)
                    for j in range(J):
                        last = nc.tensor.matmul(pM[1][0:DP, j * P:(j + 1) * P], xT1[:, j * DP:(j + 1) * DP], W12[:, :],
                                                start=True, stop=True)
                    last.then_inc(m_z, 1)

                def x1(self, d):
                    pe.wait_ge(lns["pre1"][4], 1 + d + 1)
                    pe.wait_ge(s_z1, d + 1)
                    transposes(1, xn1, DP, m_x1)

                def fin_pe(self, d):
                    pe.wait_ge(s_uT, d + 1)
                    pe.wait_ge(s_x1T, ND if is_int(d, ND - 1) else d + 2)
                    if is_int(d, ND - 1):
                        pe.wait_ge(lns["fin1"][4], 1 + d)
                    back(pM[1], uT, DP, m_fin)

                def xs_pe(self, e):
                    pe.wait_ge(s_gs, 64 * e + 64)
                    pe.wait_ge(s_zd, e)
                    transposes(0, xs, P, m_xs)

                def sums_s(self, e):
                    pe.wait_ge(s_scaled, 1 + 2 * e + 1)
                    pe.wait_ge(s_S, NT)
                    pe.wait_ge(s_xsT, e + 1)
                    if not is_int(e, 0):
                        pe.wait_ge(s_stg, 1 + 3 * e - 2)
                    sums(e, msg)

                def rows_by(self, left, filled):
                    for j in range(J):
                        last = nc.tensor.matmul(pM[0][:, j * P:(j + 1) * P], left[:, j * P:(j + 1) * P], W12[:, :],
                                                start=True, stop=True)
                    last.then_inc(filled, 1)

                def zs_pe(self, e):
                    pe.wait_ge(s_xsT, e + 1)
                    pe.wait_ge(s_carry, 1 + J * (e + 1))
                    if not is_int(e, 0):
                        pe.wait_ge(s_stg, 1 + 3 * e - 1)
                    self.rows_by(xsT, m_zs)

                def xdd_pe(self, e):
                    pe.wait_ge(s_scaled, 1 + 2 * e + 2)
                    pe.wait_ge(s_zs, e + 1)
                    transposes(0, xdd, P, m_xdd)

                def zd_pe(self, e):
                    pe.wait_ge(s_self, e + 1)
                    pe.wait_ge(s_h0, e + 1)
                    self.rows_by(aggS, m_zd)

                def xn_pe(self, e):
                    pe.wait_ge(lns["lane0"][4], 1 + e + 1)
                    pe.wait_ge(s_self, e + 1)
                    pe.wait_ge(s_stg, 1 + 3 * e)
                    transposes(0, xn0, P, m_xn)

                def t_pe(self, i, k):
                    pe.wait_ge(L[0]["h_ready"], 1 + 3 * i + k + 1)
                    if is_int(i, NG - 1):
                        pe.wait_ge(s_zd, i + 1)
                        pe.wait_ge(s_stg, 1 + 3 * i + k)
                    elif k == 0:
                        pe.wait_ge(s_xsT, i + 2)
                    elif k == 1:
                        pe.wait_ge(s_carry, 1 + J * (i + 2))
                    else:
                        pe.wait_ge(s_self, i + 2)
                    back(pM[0], hB, P, m_t)

                def g_sums(self, i):
                    pe.wait_ge(s_scaled, 1 + 2 * NG + i + 1)
                    pe.wait_ge(s_stg, 1 + 3 * NG)
                    pe.wait_ge(s_h0, NG + i)
                    sums(i, msg)

                def agg_pe(self, i):
                    pe.wait_ge(s_carry, 1 + J * (NG + i + 1))
                    back(pM[0], aggS, P, m_agg)

                def g3(self, i):
                    pe.wait_ge(lns["lane0"][4], 1 + LN_G + i + 1)
                    pe.wait_ge(s_zpre, 1 + i + 1)
                    transposes(0, xn0, P, m_xn)

                def sums_l(self, l, g):
                    q = l * NG + g
                    pe.wait_ge(s_gs, 64 * (2 * NG + q) + 64)
                    if l == LEVELS - 1 and not is_int(g, 0):
                        pe.wait_ge(s_in, q)
                    else:
                        pe.wait_ge(s_h0, 2 * NG)
                        pe.wait_ge(s_stg, 1 + 3 * NG + q)
                    sums(g, xs)

                def l_pe(self, l, g):
                    q = l * NG + g
                    pe.wait_ge(L[0]["h_ready"], 1 + GRU_L + q + 1)
                    if l < LEVELS - 1:
                        pe.wait_ge(s_in, q + 1)
                        back(pM[0], hB, P, m_t)
                    else:
                        pe.wait_ge(lns["fin1"][4], 1 + ND)
                        pe.wait_ge(s_fin, 1 + g)
                        back(pM[1], hB, P, m_t)

            schedule(pe, Tensor())

        @block.scalar
        def _(act):
            def normalise(tag, n, source, dest, p, drained=None):
                b, s = lnb[tag], lns[tag]
                act.wait_ge(s[3], n + 1)
                for j in range(J):
                    last = nc.scalar.activation(dest[:, j, :], source(j), ACT.Identity,
                                                scale=b["rs"][:, j:j + 1], bias=b["nm"][:, j:j + 1])
                last.then_inc(s[4], 1)

            def copy_m(lane, filled, count, dest, done):
                act.wait_ge(filled, count)
                nc.scalar.activation(dest, pM[lane][:, 0:W[lane]], ACT.Identity).then_inc(done, 1)

            class Scalar(Pieces):
                def act_r(self, s):
                    a = L[s.lane]
                    act.wait_ge(a["r_filled"], s.n + 1)
                    act.wait_ge(a["t_ready"], 1 + s.n)
                    nc.scalar.activation(rS[s.lane][:, :], pR[s.lane][:, 0:W[s.lane]], ACT.Sigmoid,
                                         bias=brz[:, 0:1]).then_inc(a["r_ready"], 1)

                def act_t(self, s):
                    a = L[s.lane]
                    if s.agg:
                        act.wait_ge(s_in, s.q + 1)
                    else:
                        act.wait_ge(a["t_ready"], 1 + s.n + 1)
                    act.wait_ge(a["h_ready"], 1 + s.n)
                    nc.scalar.activation(nS[s.lane][:, :], tS[s.lane][:, :], ACT.Tanh,
                                         bias=b3[:, 0, 2:3]).then_inc(a["tanh_ready"], 1)

                def act_z(self, s):
                    a = L[s.lane]
                    act.wait_ge(a["z_filled"], s.n + 1)
                    act.wait_ge(a["gated_ready"], 1 + s.n)
                    nc.scalar.activation(zS[s.lane][:, :], pZ[s.lane][:, 0:W[s.lane]], ACT.Sigmoid,
                                         bias=brz[:, 1:2]).then_inc(a["z_ready"], 1)

                def xt_act(self, d):
                    copy_m(1, m_xt, d + 1, xT1[:, :], s_xT1)

                def zsig(self, d):
                    act.wait_ge(s_z1, d + 1)
                    nc.scalar.activation(z1[:, :, :], z1[:, :, :], ACT.Sigmoid).then_inc(s_sig1, 1)

                def x1_norm(self, d):
                    act.wait_ge(s_x1T, d)
                    normalise("pre1", d, lambda j: z1[:, j, :], xn1, DP)

                def x1_act(self, d):
                    if not is_int(d, 0):
                        act.wait_ge(L[1]["h_ready"], 1 + 4 * d - 3)
                        act.wait_ge(s_x2, d)
                    copy_m(1, m_x1, d + 1, x1T[:, :], s_x1T)

                def x2(self, d):
                    act.wait_ge(s_x1T, d + 1)
                    act.wait_ge(s_uT, d)
                    nc.scalar.activation(x2T[:, :], x1T[:, :], ACT.Identity, scale=2.0).then_inc(s_x2, 1)

                def fin_norm(self, d):
                    act.wait_ge(s_store1, 1 + 16 * d)
                    normalise("fin1", d, lambda j: pM[1][0:DP, j * P:(j + 1) * P], o1, DP)

                def xs_act(self, e):
                    act.wait_ge(m_zd, e)
                    copy_m(0, m_xs, e + 1, xsT[:, :], s_xsT)

                def zs_act(self, e):
                    act.wait_ge(s_zb, e + 1)
                    nc.scalar.activation(z0[:, :, :], z0[:, :, :], ACT.Sigmoid).then_inc(s_sig0, 1)

                def xn_norm(self, e):
                    act.wait_ge(st_xn, 1 + 16 * e)
                    act.wait_ge(m_xn, e)
                    normalise("lane0", e, lambda j: z0[:, j, :], xn0, P)

                def xn_act(self, i):
                    act.wait_ge(L[0]["h_ready"], 1 + 3 * i)
                    copy_m(0, m_xn, i + 1, hA[:, :], s_h0)

                def t_act(self, i, k):
                    act.wait_ge(st_stg, 1 + 16 * (3 * i + k))
                    copy_m(0, m_t, 3 * i + k + 1, stg[:, :, :].rearrange("p j f -> p (j f)"), s_stg)

                def g1b(self, i):
                    act.wait_ge(s_zb, NG + i + 1)
                    nc.scalar.activation(z0[:, :, :], z0[:, :, :], ACT.Sigmoid).then_inc(s_sig0, 1)

                def g3_norm(self, i):
                    act.wait_ge(st_xn, 1 + 16 * (NG + i))
                    act.wait_ge(m_xn, NG + i)
                    normalise("lane0", LN_G + i, lambda j: z0[:, j, :], xn0, P)

                def g3_act(self, i):
                    act.wait_ge(L[0]["h_ready"], 1 + 3 * NG)
                    act.wait_ge(st_h, 1 + 16 * i)
                    copy_m(0, m_xn, NG + i + 1, hA[:, :], s_h0)

                def l_act(self, l, g):
                    q = l * NG + g
                    if l < LEVELS - 1:
                        act.wait_ge(st_stg, 1 + 16 * (3 * NG + q))
                        copy_m(0, m_t, 3 * NG + q + 1, stg[:, :, :].rearrange("p j f -> p (j f)"), s_stg)

                def fin0(self, l, g):
                    act.wait_ge(st_xn, 1 + 16 * 2 * NG)
                    act.wait_ge(s_scat, 16 * NT + 16 * J * g)
                    normalise("lane0", LN_L + g, lambda j: z0[:, j, :], xn0, P)

            schedule(act, Scalar())

        @block.vector
        def _(dve):
            V = nc.vector

            def ln_stats(tag, n, source):
                b, s = lnb[tag], lns[tag]
                for j in range(J):
                    last = V.bn_stats(b["st"][:, j, :], source(j))
                last.then_inc(s[0], 1)
                dve.wait_ge(s[0], n + 1)
                dve.wait_ge(s[4], 1 + n)
                settle(dve, "dve")
                for j in range(J):
                    last = V.bn_aggr(b["ag"][:, j, :], b["st"][:, j, :])
                last.then_inc(s[1], 1)

            def carries(i, n):
                dve.wait_ge(m_sums, n + 1)
                for j in range(J):
                    dve.wait_ge(s_carry, 1 + J * n + j)
                    if j == 0:
                        dve.wait_ge(s_carried, 1 + n)
                    a = aggS[:, j * P:(j + 1) * P]
                    before = carry[:, 0:1] if j == 0 else aggS[:, j * P - 1:j * P]
                    V.scalar_tensor_tensor(out=a, in0=FL[:, bass.ds((i * J + j) * P, P)], scalar=before,
                                           in1=pM[0][:, j * P:(j + 1) * P], op0=ALU.mult, op1=ALU.add).then_inc(s_carry, 1)
                dve.wait_ge(s_carry, 1 + J * n + J)
                V.tensor_copy(carry[:, 0:1], aggS[:, GS - 1:GS]).then_inc(s_carried, 1)

            carry = ctx.enter_context(nc.sbuf_tensor("carry", [P, 1], f32))
            steps = [0]

            def chain(ins):
                steps[0] += 1
                ins.then_inc(s_chain, 1)
                dve.wait_ge(s_chain, steps[0])

            class Vector(Pieces):
                def prep_weights(self):
                    V.memset(dstR[:, :], N)
                    V.memset(prevR[:, :], N)
                    V.memset(nextR[:, :], N)
                    V.memset(srcR[:, :], 0)
                    V.memset(one[:, :], 1.0)
                    V.memset(carF[:, :], 0.0)
                    V.memset(carry[:, :], 0.0)
                    V.memset(recfill[:, :, 0], -1.0)
                    chain(V.memset(recfill[:, :, 1], 1.0))
                    V.memset(prevR[0:1, 0:1], -1).then_inc(s_pads, 1)
                    dve.wait_ge(s_wload, 16 * 9)
                    chain(V.tensor_tensor(brz[:, 0:2], b3[:, 0, 0:2], b3[:, 1, 0:2], ALU.add))
                    V.tensor_copy(b1f[:, 0, :], b1c[:, 0:1].broadcast_to([P, P]))
                    V.tensor_copy(b1f[:, 1, :], b1c[:, 1:2].broadcast_to([P, P]))
                    dve.wait_ge(s_prep_pe, 1)
                    V.tensor_copy(W1T[:, :, :].rearrange("p c f -> p (c f)"), pR[0][:, 0:2 * P])
                    V.tensor_copy(wiT[:, :], pN[0][:, 0:3 * P])
                    V.tensor_copy(whT[:, :], pZ[0][:, 0:3 * P])
                    V.tensor_copy(gwT[:, :, :].rearrange("p c f -> p (c f)"), pM[0][:, 0:LEVELS * P]).then_inc(s_prep_cp, 1)
                    dve.wait_ge(s_prep_pe, 2)
                    V.tensor_copy(W12[:, :], pR[1][:, 0:P])
                    for l, b in enumerate((pZ[1], pM[1], pR[0], pN[0])):
                        V.tensor_copy(wlT[:, l, :], b[:, 0:3 * P])
                    chain(V.tensor_copy(c_bc[:, :], pN[1][:, 0:P]))
                    V.tensor_tensor(cb2_bc[:, :], c_bc[:, :], b2_bc[:, :], ALU.add).then_inc(s_wready, 1)
                    dve.wait_ge(s_wready, 1)

                def prep_edges(self):
                    dve.wait_ge(s_eload, 16 * 9)
                    dve.wait_ge(s_const, 2)
                    for a, b in ((dstF, dstR), (prevF, prevR), (nextF, nextR), (srcF, srcR), (eF, eR)):
                        V.tensor_copy(a[:, :], b[:, :])
                    V.tensor_copy(ecol[:, :], ecI[:, :])
                    chain(V.tensor_copy(t0col[:, :], t0I[:, :]))
                    chain(V.tensor_tensor(startF[:, :], dstF[:, :], prevF[:, :], ALU.not_equal))
                    chain(V.tensor_tensor(startF[:, :], startF[:, :], eF[:, :], ALU.mult))
                    V.tensor_tensor_scan(runF[:, :], startF[:, :], startF[:, :], 0.0, ALU.max, ALU.max).then_inc(s_car_pe, 1)
                    dve.wait_ge(s_car_pe, 2)
                    chain(V.tensor_copy(mv[0:1, 0:NT], pR[0][0:1, 0:NT]))
                    V.tensor_tensor_scan(carF[0:1, 1:NT + 1], mv[0:1, 0:NT], mv[0:1, 0:NT], 0.0, ALU.max, ALU.max).then_inc(s_car_pe, 1)
                    dve.wait_ge(s_car_pe, 4)
                    chain(V.tensor_copy(isd[0:NT, 0:1], pN[0][0:NT, 0:1]))
                    V.tensor_scalar(firstF[:, :], runF[:, :], isd[0:NT, 0:1], None, ALU.max).then_inc(s_first, 1)
                    dve.wait_ge(s_first, 1)
                    chain(V.tensor_tensor(dinvF[:, :], eF[:, :], firstF[:, :], ALU.subtract))
                    V.tensor_scalar(dinvF[:, :], dinvF[:, :], 2.0, None, ALU.add).then_inc(s_deg, 1)
                    chain(V.tensor_tensor(scatF[:, :], dstF[:, :], nextF[:, :], ALU.is_equal))
                    V.scalar_tensor_tensor(out=scatF[:, :], in0=scatF[:, :], scalar=float(2 * N), in1=dstF[:, :],
                                           op0=ALU.mult, op1=ALU.add).then_inc(s_col_pe, 1)
                    dve.wait_ge(s_col_pe, 2)
                    V.tensor_copy(dstC[:, :], pZ[0][:, 0:NT])
                    V.tensor_copy(srcI[:, :], pZ[0][:, NT:2 * NT])
                    V.tensor_copy(dinvD[:, :], pZ[0][:, 2 * NT:3 * NT])
                    V.tensor_copy(recrow[:, :, 1], pZ[0][:, 2 * NT:3 * NT])
                    V.tensor_copy(scatI[:, :], pZ[0][:, 3 * NT:4 * NT])
                    chain(V.tensor_copy(recrow[:, :, 0], ecol[:, :]))
                    V.tensor_scalar(dstI[:, :], dstC[:, :], float(N - 1), None, ALU.min).then_inc(s_cols, 1)

                def build_s(self, c):
                    dve.wait_ge(s_firstld, 16)
                    for t in range(RC):
                        cols = bass.ds((c * RC + t) * P, P)
                        V.tensor_scalar(FL[:, cols], S[:, cols], t0col[:, bass.ds(c * RC + t, 1)], None, ALU.is_lt)
                        V.scalar_tensor_tensor(out=S[:, cols], in0=S[:, cols], scalar=ecol[:, bass.ds(c * RC + t, 1)],
                                               in1=tri[:, :], op0=ALU.is_le, op1=ALU.mult).then_inc(s_S, 1)

                def prep_edges2(self):
                    dve.wait_ge(s_S, NT)
                    dve.wait_ge(s_recS, RL)
                    V.tensor_scalar(isd[:, :], recS[:, :, 0], 0.0, None, ALU.is_ge)
                    chain(V.tensor_tensor(mv[:, :], recS[:, :, 0], ecol[:, :], ALU.subtract))
                    chain(V.scalar_tensor_tensor(out=mv[:, :], in0=mv[:, :], scalar=float(NS), in1=isd[:, :],
                                                 op0=ALU.add, op1=ALU.mult))
                    V.tensor_tensor(idxI[:, :], mv[:, :], ecol[:, :], ALU.add).then_inc(s_idx, 1)
                    dve.wait_ge(s_idx, 1)

                def dve_t(self, s):
                    a, w, t = L[s.lane], W[s.lane], tS[s.lane][:, :]
                    dve.wait_ge(a["r_ready"], 1 + s.n + 1)
                    dve.wait_ge(a["n_filled"], s.n + 1)
                    V.scalar_tensor_tensor(out=t, in0=pN[s.lane][:, 0:w], scalar=b3[:, 1, 2:3], in1=rS[s.lane][:, :],
                                           op0=ALU.add, op1=ALU.mult).then_inc(a["t_ready"], 1)
                    if s.agg:
                        dve.wait_ge(a["t_ready"], 1 + s.n + 1)
                        dve.wait_ge(m_in, s.q + 1)
                        V.tensor_tensor(t, t, pM[0][:, :], ALU.add).then_inc(s_in, 1)

                def dve_diff(self, s):
                    a = L[s.lane]
                    dve.wait_ge(a["tanh_ready"], s.n + 1)
                    dve.wait_ge(a["h_ready"], 1 + s.n)
                    if s.kind == "src" and s.k == 0:
                        dve.wait_ge(s_h0, s.i + 1)
                    if s.kind == "edge":
                        dve.wait_ge(s_ldh, 16 * s.q + 16)
                    V.tensor_tensor(dS[s.lane][:, :], s.h, nS[s.lane][:, :], ALU.subtract).then_inc(a["diff_ready"], 1)

                def dve_gated(self, s):
                    a = L[s.lane]
                    dve.wait_ge(a["diff_ready"], s.n + 1)
                    dve.wait_ge(a["z_ready"], 1 + s.n + 1)
                    V.tensor_tensor(dS[s.lane][:, :], dS[s.lane][:, :], zS[s.lane][:, :], ALU.mult).then_inc(a["gated_ready"], 1)

                def dve_h(self, s):
                    a = L[s.lane]
                    dve.wait_ge(a["gated_ready"], 1 + s.n + 1)
                    if s.kind == "dense" and s.k == 0:
                        dve.wait_ge(s_uT, s.d)
                    if s.kind == "edge":
                        dve.wait_ge(m_t, 3 * NG + s.q)
                        dve.wait_ge(st_h, 1 + (16 * (NG + s.q) if s.l < LEVELS - 1 else 16 * NG * LEVELS))
                    V.tensor_tensor(s.hout, dS[s.lane][:, :], nS[s.lane][:, :], ALU.add).then_inc(a["h_ready"], 1)

                def zadd(self, d):
                    dve.wait_ge(m_z, d + 1)
                    dve.wait_ge(lns["pre1"][4], 1 + d)
                    V.tensor_tensor(z1[:, :, :], pM[1][0:DP, :].rearrange("p (j f) -> p j f", j=J),
                                    cb2_bc[0:DP, :].unsqueeze(1).broadcast_to([DP, J, P]), ALU.add).then_inc(s_z1, 1)

                def zstat(self, d):
                    dve.wait_ge(s_sig1, d + 1)
                    V.tensor_tensor(z1[:, :, :], z1[:, :, :], xr1[:, :, :], ALU.add).then_inc(s_u1, 1)
                    dve.wait_ge(s_u1, d + 1)
                    ln_stats("pre1", d, lambda j: z1[:, j, :])

                def u(self, d):
                    dve.wait_ge(m_fin, d)
                    dve.wait_ge(s_x2, d + 1)
                    dve.wait_ge(L[1]["h_ready"], 1 + 4 * d + 4)
                    V.tensor_tensor(uT[:, :], x2T[:, :], h1[:, :], ALU.add).then_inc(s_uT, 1)

                def fin_stat(self, d):
                    dve.wait_ge(m_fin, d + 1)
                    ln_stats("fin1", d, lambda j: pM[1][0:DP, j * P:(j + 1) * P])

                def scale(self, to, rows, by, e):
                    for j in range(J):
                        last = V.tensor_scalar(to[:, j, :], rows[:, j, :], by(e * J + j), None, ALU.mult)
                    last.then_inc(s_scaled, 1)

                def scale_msg(self, e):
                    dve.wait_ge(s_gs, 64 * e + 64)
                    dve.wait_ge(m_sums, e)
                    self.scale(msg, xs, lambda t: recS[:, bass.ds(t, 1), 1], e)

                def scale_xdd(self, e):
                    dve.wait_ge(s_gd, 64 * e + 64)
                    dve.wait_ge(m_xdd, e)
                    self.scale(xdd, xd, lambda t: dinvD[:, bass.ds(t, 1)], e)

                def carry_s(self, e):
                    dve.wait_ge(m_zd, e)
                    carries(e, e)

                def zs_dve(self, e):
                    dve.wait_ge(m_zs, e + 1)
                    dve.wait_ge(st_zs, 1 + 16 * e)
                    V.tensor_tensor(zrow[:, :, :], pM[0][:, :].rearrange("p (j f) -> p j f", j=J),
                                    c_bc[:, :].unsqueeze(1).broadcast_to([P, J, P]), ALU.add).then_inc(s_zs, 1)
                    dve.wait_ge(s_zs, e + 1)
                    dve.wait_ge(lns["lane0"][4], 1 + e)
                    V.tensor_tensor(z0[:, :, :], zrow[:, :, :], b2_bc[:, :].unsqueeze(1).broadcast_to([P, J, P]),
                                    ALU.add).then_inc(s_zb, 1)

                def self_dve(self, e):
                    dve.wait_ge(m_xdd, e + 1)
                    V.tensor_tensor(aggS[:, :], aggS[:, :], pM[0][:, :], ALU.add).then_inc(s_self, 1)

                def us(self, e):
                    dve.wait_ge(s_sig0, e + 1)
                    V.tensor_tensor(z0[:, :, :], z0[:, :, :], xs[:, :, :], ALU.add).then_inc(s_u0, 1)
                    dve.wait_ge(s_u0, 1 + e + 1)
                    ln_stats("lane0", e, lambda j: z0[:, j, :])

                def zd_dve(self, e):
                    dve.wait_ge(m_zd, e + 1)
                    dve.wait_ge(st_zd, 1 + 16 * e)
                    for j in range(J):
                        last = V.scalar_tensor_tensor(out=zD[:, j, :], in0=pM[0][:, j * P:(j + 1) * P],
                                                      scalar=dinvD[:, bass.ds(e * J + j, 1)], in1=c_bc[:, :],
                                                      op0=ALU.mult, op1=ALU.add)
                    last.then_inc(s_zd, 1)

                def g_scale(self, i):
                    dve.wait_ge(s_gs, 64 * (NG + i) + 64)
                    dve.wait_ge(m_sums, NG + i)
                    self.scale(msg, xs, lambda t: recS[:, bass.ds(t, 1), 1], i)

                def g_carry(self, i):
                    dve.wait_ge(m_zd, NG)
                    dve.wait_ge(m_agg, 1 + i)
                    carries(i, NG + i)

                def g1(self, i):
                    dve.wait_ge(m_agg, 1 + i + 1)
                    dve.wait_ge(s_ldz, 16 * i + 16)
                    dve.wait_ge(lns["lane0"][4], 1 + LN_G + i)
                    for j in range(J):
                        last = V.scalar_tensor_tensor(out=z0[:, j, :], in0=zDr[:, j, :], scalar=dinvD[:, bass.ds(i * J + j, 1)],
                                                      in1=pM[0][:, j * P:(j + 1) * P], op0=ALU.mult, op1=ALU.add)
                    last.then_inc(s_zpre, 1)

                def g1b(self, i):
                    dve.wait_ge(s_zpre, 1 + i + 1)
                    for j in range(J):
                        last = V.scalar_tensor_tensor(out=z0[:, j, :], in0=z0[:, j, :], scalar=dinvD[:, bass.ds(i * J + j, 1)],
                                                      in1=b2_bc[:, :], op0=ALU.mult, op1=ALU.add)
                    last.then_inc(s_zb, 1)

                def g2(self, i):
                    dve.wait_ge(s_sig0, NG + i + 1)
                    dve.wait_ge(s_ldx, 16 * i + 16)
                    V.tensor_tensor(z0[:, :, :], z0[:, :, :], xdr[:, :, :], ALU.add).then_inc(s_u0, 1)
                    dve.wait_ge(s_u0, 1 + NG + i + 1)
                    ln_stats("lane0", LN_G + i, lambda j: z0[:, j, :])

                def carry_l(self, l, g):
                    q = l * NG + g
                    dve.wait_ge(m_agg, 1 + NG)
                    dve.wait_ge(L[0]["z_filled"], GRU_L + q)
                    carries(g, 2 * NG + q)

                def fin0(self, l, g):
                    q = l * NG + g
                    dve.wait_ge(m_t, 3 * NG + q + 1)
                    dve.wait_ge(s_ldx, 16 * (NG + g) + 16)
                    dve.wait_ge(lns["lane0"][4], 1 + LN_L + g)
                    V.scalar_tensor_tensor(out=z0[:, :, :].rearrange("p j f -> p (j f)"),
                                           in0=xdr[:, :, :].rearrange("p j f -> p (j f)"), scalar=2.0,
                                           in1=pM[1][:, :], op0=ALU.mult, op1=ALU.add).then_inc(s_fin, 1)
                    dve.wait_ge(s_fin, 1 + g + 1)
                    ln_stats("lane0", LN_L + g, lambda j: z0[:, j, :])

            schedule(dve, Vector())


_INS = ['x', 'src', 'dst', 'L0_gnn_W1', 'L0_gnn_b1', 'L0_gnn_W2', 'L0_gnn_b2', 'L1_gnn_weight',
        'L1_gnn_w_ih', 'L1_gnn_w_hh', 'L1_gnn_b_ih', 'L1_gnn_b_hh']


def kernel(**inputs):
    import numpy as _np
    import concourse.bacc as _bacc
    from concourse import mybir as _mybir
    from concourse.bass_utils import run_bass_kernel_spmd as _run

    nc = _bacc.Bacc("TRN2", target_bir_lowering=False, num_devices=1)
    arrays, args = {}, []
    for name in _INS:
        a = _np.ascontiguousarray(inputs[name])
        arrays[f"in_{name}_dram"] = a
        args.append(nc.dram_tensor(f"in_{name}_dram", a.shape, _mybir.dt.from_np(a.dtype), kind="ExternalInput").ap())
    shape = inputs["x"].shape
    args.append(nc.dram_tensor("out_0_dram", shape, _mybir.dt.float32, kind="ExternalOutput").ap())
    gcn_resnorm_ggnn_resnorm(nc, *args)
    r = _run(nc, [arrays], core_ids=[0])
    return r.results[0]["out_0_dram"]
```
